# Optimizing a Trainium2 kernel written in Bass

```python
import numpy as np
import jax
import jax.numpy as jnp

def _softmax(x, axis=-1):
    return jax.nn.softmax(x, axis=axis)

def _gelu(x):
    return jax.nn.gelu(x, approximate=True)

def _silu(x):
    return jax.nn.silu(x)

def _sigmoid(x):
    return jax.nn.sigmoid(x)

def _layernorm(x, axis=-1, eps=1e-05):
    m = jnp.mean(x, axis=axis, keepdims=True)
    v = jnp.var(x, axis=axis, keepdims=True)
    return (x - m) / jnp.sqrt(v + eps)

def _scatter_add(tgt, idx, src, axis=0):
    return tgt.at[idx].add(src)

def _segment_sum(src, seg, n):
    return jax.ops.segment_sum(src, seg, n)
kernel_name = 'mk_adaln_d1_jaxref_r8_82b141'

def setup_inputs(seed: int=0):
    np.random.seed(seed)
    _w = jnp.asarray

    def _L0_attn_setup():
        import jax, jax.numpy as jnp
        import numpy as np
        HIDDEN = 512
        N_HEADS = 32
        N_KV_HEADS = 8
        HEAD_DIM = HIDDEN // N_HEADS
        N_REP = N_HEADS // N_KV_HEADS
        KV_DIM = N_KV_HEADS * HEAD_DIM

        def _kaiming_uniform(key, out_f, in_f):
            bound = 1.0 / np.sqrt(in_f)
            return jax.random.uniform(key, (out_f, in_f), jnp.float32, -bound, bound)

        def bitnet_linear(x, weight, scale_param):
            s = jnp.maximum(jnp.mean(jnp.abs(weight), axis=1), 1e-08)
            binary_w = jnp.sign(weight / s[:, None])
            y = jnp.einsum('bsi,oi->bso', x, binary_w)
            y = y * (s * scale_param)[None, None, :]
            return jnp.nan_to_num(y, nan=0.0, posinf=1000000.0, neginf=-1000000.0)
        key = jax.random.key(seed)
        ks = jax.random.split(key, 5)
        return {'hidden_states': jax.random.normal(ks[0], (1, 256, HIDDEN), jnp.float32), 'q_weight': _kaiming_uniform(ks[1], HIDDEN, HIDDEN), 'q_scale': jnp.ones((HIDDEN,), jnp.float32), 'k_weight': _kaiming_uniform(ks[2], KV_DIM, HIDDEN), 'k_scale': jnp.ones((KV_DIM,), jnp.float32), 'v_weight': _kaiming_uniform(ks[3], KV_DIM, HIDDEN), 'v_scale': jnp.ones((KV_DIM,), jnp.float32), 'o_weight': _kaiming_uniform(ks[4], HIDDEN, HIDDEN), 'o_scale': jnp.ones((HIDDEN,), jnp.float32)}
    _L0_attn_in = _L0_attn_setup()

    def _L0_ffn_setup():
        import jax, jax.numpy as jnp
        import numpy as np
        HIDDEN = 512
        MOE_INTER = 128
        SHARED_INTER = 512
        NUM_EXPERTS = 16
        TOP_K = 2

        def _moe_forward(x, gate_w, w_gate_up, w_down, shared_w_gate_up, shared_w_down):
            orig_shape = x.shape
            x2 = x.reshape(-1, orig_shape[-1])
            gu_s = x2 @ shared_w_gate_up.T
            g_s, u_s = jnp.split(gu_s, 2, axis=-1)
            shared_out = jax.nn.silu(g_s) * u_s @ shared_w_down.T
            logits = x2 @ gate_w.T
            probs = jax.nn.softmax(logits, axis=-1)
            topk_vals, topk_idx = jax.lax.top_k(probs, TOP_K)
            topk_vals = topk_vals / jnp.sum(topk_vals, axis=-1, keepdims=True)
            combine = jnp.sum(jax.nn.one_hot(topk_idx, NUM_EXPERTS, dtype=x2.dtype) * topk_vals[..., None], axis=1)
            gu = jnp.einsum('th,eih->eti', x2, w_gate_up)
            g, u = jnp.split(gu, 2, axis=-1)
            act = jax.nn.silu(g) * u
            out_e = jnp.einsum('eti,ehi->eth', act, w_down)
            moe_out = jnp.einsum('eth,te->th', out_e, combine)
            return (moe_out + shared_out).reshape(orig_shape)
        key = jax.random.key(seed)
        ks = jax.random.split(key, 6)
        s = 0.02
        hidden_states = jax.random.normal(ks[0], (2, 256, HIDDEN), dtype=jnp.float32)
        gate_w = jax.random.normal(ks[1], (NUM_EXPERTS, HIDDEN), dtype=jnp.float32) * s
        w_gate_up = jax.random.normal(ks[2], (NUM_EXPERTS, 2 * MOE_INTER, HIDDEN), dtype=jnp.float32) * s
        w_down = jax.random.normal(ks[3], (NUM_EXPERTS, HIDDEN, MOE_INTER), dtype=jnp.float32) * s
        shared_w_gate_up = jax.random.normal(ks[4], (2 * SHARED_INTER, HIDDEN), dtype=jnp.float32) * s
        shared_w_down = jax.random.normal(ks[5], (HIDDEN, SHARED_INTER), dtype=jnp.float32) * s
        return {'hidden_states': hidden_states, 'gate_w': gate_w, 'w_gate_up': w_gate_up, 'w_down': w_down, 'shared_w_gate_up': shared_w_gate_up, 'shared_w_down': shared_w_down}
    _L0_ffn_in = _L0_ffn_setup()
    _L0_c = _w((lambda *s: np.random.randn(*s).astype(np.float32) * 0.05)(1, 512))
    _L0_wmod = _w((lambda *s: np.random.randn(*s).astype(np.float32) * 0.05)(512, 6 * 512) * 512 ** (-0.5))
    _d = {'L0_attn_hidden_states': _L0_attn_in['hidden_states'], 'L0_attn_q_weight': _L0_attn_in['q_weight'], 'L0_attn_q_scale': _L0_attn_in['q_scale'], 'L0_attn_k_weight': _L0_attn_in['k_weight'], 'L0_attn_k_scale': _L0_attn_in['k_scale'], 'L0_attn_v_weight': _L0_attn_in['v_weight'], 'L0_attn_v_scale': _L0_attn_in['v_scale'], 'L0_attn_o_weight': _L0_attn_in['o_weight'], 'L0_attn_o_scale': _L0_attn_in['o_scale'], 'L0_ffn_gate_w': _L0_ffn_in['gate_w'], 'L0_ffn_w_gate_up': _L0_ffn_in['w_gate_up'], 'L0_ffn_w_down': _L0_ffn_in['w_down'], 'L0_ffn_shared_w_gate_up': _L0_ffn_in['shared_w_gate_up'], 'L0_ffn_shared_w_down': _L0_ffn_in['shared_w_down'], 'L0_c': _L0_c, 'L0_wmod': _L0_wmod}
    _x0 = _d['L0_attn_hidden_states']
    _d['L0_attn_hidden_states'] = jax.random.normal(jax.random.fold_in(jax.random.key(seed), 1), (1, 1024, 512), dtype=_x0.dtype)
    del _x0
    return _d

def reference(L0_attn_hidden_states, L0_attn_q_weight, L0_attn_q_scale, L0_attn_k_weight, L0_attn_k_scale, L0_attn_v_weight, L0_attn_v_scale, L0_attn_o_weight, L0_attn_o_scale, L0_ffn_gate_w, L0_ffn_w_gate_up, L0_ffn_w_down, L0_ffn_shared_w_gate_up, L0_ffn_shared_w_down, L0_c, L0_wmod):

    def _L0_attn_ref(hidden_states, q_weight, q_scale, k_weight, k_scale, v_weight, v_scale, o_weight, o_scale):
        import jax, jax.numpy as jnp
        import numpy as np
        HIDDEN = 512
        N_HEADS = 32
        N_KV_HEADS = 8
        HEAD_DIM = HIDDEN // N_HEADS
        N_REP = N_HEADS // N_KV_HEADS
        KV_DIM = N_KV_HEADS * HEAD_DIM

        def _kaiming_uniform(key, out_f, in_f):
            bound = 1.0 / np.sqrt(in_f)
            return jax.random.uniform(key, (out_f, in_f), jnp.float32, -bound, bound)

        def bitnet_linear(x, weight, scale_param):
            s = jnp.maximum(jnp.mean(jnp.abs(weight), axis=1), 1e-08)
            binary_w = jnp.sign(weight / s[:, None])
            y = jnp.einsum('bsi,oi->bso', x, binary_w)
            y = y * (s * scale_param)[None, None, :]
            return jnp.nan_to_num(y, nan=0.0, posinf=1000000.0, neginf=-1000000.0)
        b, s, _ = hidden_states.shape
        q = bitnet_linear(hidden_states, q_weight, q_scale)
        k = bitnet_linear(hidden_states, k_weight, k_scale)
        v = bitnet_linear(hidden_states, v_weight, v_scale)
        q = q.reshape(b, s, N_HEADS, HEAD_DIM).transpose(0, 2, 1, 3)
        k = k.reshape(b, s, N_KV_HEADS, HEAD_DIM).transpose(0, 2, 1, 3)
        v = v.reshape(b, s, N_KV_HEADS, HEAD_DIM).transpose(0, 2, 1, 3)
        k = jnp.repeat(k, N_REP, axis=1)
        v = jnp.repeat(v, N_REP, axis=1)
        scores = jnp.einsum('bhqd,bhkd->bhqk', q, k) / np.sqrt(HEAD_DIM)
        attn = jax.nn.softmax(scores, axis=-1)
        out = jnp.einsum('bhqk,bhkd->bhqd', attn, v)
        out = out.transpose(0, 2, 1, 3).reshape(b, s, HIDDEN)
        return bitnet_linear(out, o_weight, o_scale)

    def _L0_ffn_ref(hidden_states, gate_w, w_gate_up, w_down, shared_w_gate_up, shared_w_down):
        import jax, jax.numpy as jnp
        import numpy as np
        HIDDEN = 512
        MOE_INTER = 128
        SHARED_INTER = 512
        NUM_EXPERTS = 16
        TOP_K = 2

        def _moe_forward(x, gate_w, w_gate_up, w_down, shared_w_gate_up, shared_w_down):
            orig_shape = x.shape
            x2 = x.reshape(-1, orig_shape[-1])
            gu_s = x2 @ shared_w_gate_up.T
            g_s, u_s = jnp.split(gu_s, 2, axis=-1)
            shared_out = jax.nn.silu(g_s) * u_s @ shared_w_down.T
            logits = x2 @ gate_w.T
            probs = jax.nn.softmax(logits, axis=-1)
            topk_vals, topk_idx = jax.lax.top_k(probs, TOP_K)
            topk_vals = topk_vals / jnp.sum(topk_vals, axis=-1, keepdims=True)
            combine = jnp.sum(jax.nn.one_hot(topk_idx, NUM_EXPERTS, dtype=x2.dtype) * topk_vals[..., None], axis=1)
            gu = jnp.einsum('th,eih->eti', x2, w_gate_up)
            g, u = jnp.split(gu, 2, axis=-1)
            act = jax.nn.silu(g) * u
            out_e = jnp.einsum('eti,ehi->eth', act, w_down)
            moe_out = jnp.einsum('eth,te->th', out_e, combine)
            return (moe_out + shared_out).reshape(orig_shape)
        return _moe_forward(hidden_states, gate_w, w_gate_up, w_down, shared_w_gate_up, shared_w_down)
    x = L0_attn_hidden_states
    mod = (_silu(L0_c) @ L0_wmod).reshape(L0_c.shape[0], 6, 1, -1)
    sa, ca, ga, sb, cb, gb = (mod[:, 0], mod[:, 1], mod[:, 2], mod[:, 3], mod[:, 4], mod[:, 5])
    ga = (2 * (ga >= 0) - 1) * jnp.maximum(jnp.abs(ga), 0.25)
    gb = (2 * (gb >= 0) - 1) * jnp.maximum(jnp.abs(gb), 0.25)
    h = _layernorm(x, axis=-1) * (1 + ca) + sa
    x = x + ga * _L0_attn_ref(h, L0_attn_q_weight, L0_attn_q_scale, L0_attn_k_weight, L0_attn_k_scale, L0_attn_v_weight, L0_attn_v_scale, L0_attn_o_weight, L0_attn_o_scale)
    h = _layernorm(x, axis=-1) * (1 + cb) + sb
    x = x + gb * _L0_ffn_ref(h, L0_ffn_gate_w, L0_ffn_w_gate_up, L0_ffn_w_down, L0_ffn_shared_w_gate_up, L0_ffn_shared_w_down)
    return x

_drawn_inputs = setup_inputs


def setup_inputs(seed=0):
    import zlib

    import numpy as np

    out = dict(_drawn_inputs(seed))
    spreads = {'L0_attn_q_scale': (1.0, 0.6),
     'L0_attn_k_scale': (1.0, 0.6),
     'L0_attn_v_scale': (1.0, 0.6),
     'L0_attn_o_scale': (1.0, 0.6)}
    factors = {'L0_attn_q_weight': 8.0,
     'L0_attn_k_weight': 8.0,
     'L0_attn_v_weight': 8.0,
     'L0_attn_o_weight': 8.0,
     'L0_ffn_gate_w': 8.0,
     'L0_ffn_w_gate_up': 8.0,
     'L0_ffn_w_down': 8.0,
     'L0_ffn_shared_w_gate_up': 4.599,
     'L0_ffn_shared_w_down': 4.604,
     'L0_c': 4.252,
     'L0_wmod': 4.083}
    for name, (base, spread) in spreads.items():
        noise = np.random.default_rng([zlib.crc32(name.encode()), seed]).standard_normal(out[name].shape)
        drawn = base * np.exp(spread * noise) if base else spread * noise
        out[name] = jnp.asarray(drawn.astype(out[name].dtype))
    for name, factor in factors.items():
        out[name] = (out[name] * factor).astype(out[name].dtype)
    return out
```

```python
import concourse.bass as bass
from concourse import mybir
from contextlib import ExitStack

P = 128
S = 1024
D = 512
KC = D // P
TT = S // P
HALF = 512
NH, NKV, DH = 32, 8, 16
G = NH // NKV
KV = NKV * DH
QK_TILES = (D + KV) // P
PARTS = 3
PAIRS = ((0, 0), (0, 1), (1, 0), (0, 2), (2, 0), (1, 1))
KROWS = len(PAIRS) * DH
AROWS = KROWS + PARTS
E, I, TOPK = 16, 128, 2
SI = 512
TILES = (TOPK * S - E) // P + E
LN_EPS = 1e-5
MAX_BANKS = 3
BIG = 1e6


def build(nc, x, wqkv, wo, qk_scale, v_scale, o_scale, gate, wgu, wd, sgu, sd, c, wmod, out):
    f32, bf16, i32 = mybir.dt.float32, mybir.dt.bfloat16, mybir.dt.int32
    ALU, ACT, AX = mybir.AluOpType, mybir.ActivationFunctionType, mybir.AxisListType.X
    x_t = x.rearrange("(t p) n -> p t n", p=P)
    out_t = out.rearrange("(t p) n -> p t n", p=P)
    wmod_k = wmod.rearrange("(k p) n -> p k n", p=P)

    ctx = ExitStack()
    with ctx:
        def sb(name, shape, dt=f32):
            return ctx.enter_context(nc.sbuf_tensor(name, shape, dt))

        def sem(name):
            return ctx.enter_context(nc.semaphore(name))

        q_parts_d = nc.dram_tensor("q_parts_d", [PARTS, D + KV, S], bf16).ap()
        rows_d = nc.dram_tensor("rows_d", [TILES * P, D], f32).ap()
        moe_d = nc.dram_tensor("moe_d", [TILES * P, D], f32).ap()

        wgu_sb = sb("wgu_sb", [P, E, KC * 2 * I])
        r1 = sb("r1", [P, 12288])
        r2 = sb("r2", [P, TT * D])
        r3 = sb("r3", [P, TT * D])
        rx = sb("rx", [P, TT * D])
        sgu_sb = sb("sgu_sb", [P, KC, 2 * SI])
        r5 = sb("r5", [P, KC * D])
        tmp = sb("tmp", [P, 3, D])
        rows = sb("rows", [P, 5, D])
        c_bc = sb("c_bc", [P, KC, P])
        ident = sb("ident", [P, P])
        before = sb("before", [P, P])
        ones = sb("ones", [P, P])
        x_sb = rx[:].rearrange("p (t n) -> p t n", n=D)
        wmod_ring = r1[:, 0:4096].rearrange("p (b k n) -> p b k n", b=2, k=KC)
        absw = r1[:, 4096:7168].rearrange("p (k n) -> p k n", k=KC)
        absw_o = r1[:, 7168:9216].rearrange("p (k n) -> p k n", k=KC)
        signw = r1[:, 9216:12288].rearrange("p (k n) -> p k n", k=KC)
        parts_st = r1[:, 4096:5632].bitcast(bf16).rearrange("p (b a n) -> p b a n", b=2, a=PARTS)
        signw_o = r5[:].rearrange("p (k n) -> p k n", k=KC)
        xn = r2[:].rearrange("p (t n) -> p t n", n=D)
        hT = r3[:].rearrange("p (k n) -> p k n", k=KC)
        q_ring = r1[:, 0:4096].bitcast(bf16).rearrange("p (b h n) -> p b h n", b=2, h=G)
        k_ring = r1[:, 4096:5120].bitcast(bf16).rearrange("p (b n) -> p b n", b=2)
        ov = r1[:, 5120:6144].rearrange("p (b n) -> p b n", b=2)
        vg = r1[:, 6144:6656].rearrange("p (b t n) -> p b t n", b=2, t=TT)
        v_sb = r1[:, 6656:8704].rearrange("p (t h n) -> p t h n", t=TT, h=NKV)
        probs = rx[:].rearrange("p (b n) -> p b n", b=4)
        oT = r2[:].rearrange("p (m n) -> p m n", m=KC)
        den = r3[:].rearrange("p (m n) -> p m n", m=KC)
        wd_sb = r1[:, 0:8192].rearrange("p (e n) -> p e n", e=E)
        h2T = r1[:, 8192:12288].rearrange("p (k n) -> p k n", k=KC)
        h2 = r3[:].rearrange("p (t n) -> p t n", n=D)
        sd_sb = r5[:].rearrange("p (k n) -> p k n", k=KC)
        asT = r2[:].rearrange("p (k n) -> p k n", k=KC)
        xs = r3[:, 0:1024].rearrange("p (b n) -> p b n", b=2)
        xT = r3[:, 1024:2048].rearrange("p (b n) -> p b n", b=2)
        sg = r3[:, 2048:2304].rearrange("p (b n) -> p b n", b=2)
        act_sb = r3[:, 2304:2560].rearrange("p (b n) -> p b n", b=2)
        actT = r3[:, 2560:2816].rearrange("p (b n) -> p b n", b=2)
        y_sb = r3[:, 2816:3840].rearrange("p (b n) -> p b n", b=2)
        y_in = r2[:, 0:2048].rearrange("p (b k n) -> p b k n", b=2, k=TOPK)

        scol = sb("scol", [P, QK_TILES])
        qk_sc = sb("qk_sc", [P, QK_TILES])
        v_sc = sb("v_sc", [P, KV])
        c_sb = sb("c_sb", [P, KC])
        c_si = sb("c_si", [P, KC])
        mcol = sb("mcol", [P, 2, KC])
        stats = sb("stats", [P, TT, 6])
        mv = sb("mv", [P, TT, 2])
        rstd = sb("rstd", [P, TT])
        gate_sb = sb("gate_sb", [P, KC, E])
        mxh = sb("mxh", [P, 2 * G * TT])
        mxc = sb("mxc", [P, G * TT])
        rt = sb("rt", [P, 448])
        mneg = rt[0:G * TT, 0:2 * P].rearrange("p (a n) -> p a n", n=P)
        mparts = rt[0:G * TT, 2 * P:2 * P + 192].bitcast(bf16).rearrange("p (a n) -> p a n", n=P)
        c_flat = c_bc[:].rearrange("p k n -> p (k n)")
        lg = c_flat[:, 0:128].rearrange("p (t e) -> p t e", e=E)
        pr = c_flat[:, 128:256].rearrange("p (t e) -> p t e", e=E)
        both = c_flat[:, 256:400].rearrange("p (t e) -> p t e", e=E)
        cand = rt[:, 0:128].rearrange("p (t e) -> p t e", e=E)
        hot = rt[:, 128:416].rearrange("p (k t e) -> p k t e", k=TOPK, e=E)
        col = sb("col", [P, 6, TT])
        wcol = sb("wcol", [P, TOPK, TT])
        rev = sb("rev", [P, E])
        pos_f = sb("pos_f", [P, TOPK, TT])
        pos = sb("pos", [P, TOPK, TT], i32)
        cnt_i = c_flat[:, 400:432].bitcast(i32).rearrange("p (a e) -> p a e", e=E)
        cnt = sb("cnt", [P, 4, E])
        tile_no = sb("tile_no", [1, TILES])
        tile_cmp = tmp[0:1, 2, 0:TILES * E].rearrange("p (j e) -> p j e", e=E)
        tile_e = mxh[0:1, 0:2 * TILES].rearrange("p (a n) -> p a n", a=2)
        tile_ei = sb("tile_ei", [1, TILES], i32)

        ps = ctx.enter_context(nc.psum_tensor("ps", [P, 8, HALF], f32))

        x_in, w_in, wo_in, small_in, c_in = (sem(n) for n in ("x_in", "w_in", "wo_in", "small_in", "c_in"))
        wmod_in = [sem("wmod_in0"), sem("wmod_in1")]
        consts, abs_ready, sign_ready, c_ready = (sem(n) for n in ("consts", "abs_ready", "sign_ready", "c_ready"))
        w_sums, mod_mm, mod_read = sem("w_sums"), sem("mod_mm"), sem("mod_read")
        var_ready, std_ready, xn_ready = sem("var_ready"), sem("std_ready"), sem("xn_ready")
        h_t, hT_ready, qkv_mm, qkv_read = sem("h_t"), sem("hT_ready"), sem("qkv_mm"), sem("qkv_read")
        parts_ready, v_ready, v_ones = sem("parts_ready"), sem("v_ready"), sem("v_ones")
        parts_out = [sem("parts_out0"), sem("parts_out1")]
        qk_in = [sem("qk_in0"), sem("qk_in1")]
        max_row_in = [sem("max_row_in0"), sem("max_row_in1")]
        k_ones = sem("k_ones")
        max_scores, max_read, max_cols = sem("max_scores"), sem("max_read"), sem("max_cols")
        max_t, max_parts = sem("max_t"), sem("max_parts")
        scores, probs_ready, pv_done = sem("scores"), sem("probs_ready"), sem("pv_done")
        o_read, vg_ready = sem("o_read"), sem("vg_ready")
        o_out = [sem("o_out0"), sem("o_out1")]
        wgu_in, sgu_in, wd_in, sd_in = sem("wgu_in"), sem("sgu_in"), sem("wd_in"), sem("sd_in")
        gate_in, x2_in, zero_ready, zero_out = sem("gate_in"), sem("x2_in"), sem("zero_ready"), sem("zero_out")
        oT_ready, o_mm, o_mm_read = sem("oT_ready"), sem("o_mm"), sem("o_mm_read")
        h2_ready, h2_t, h2T_ready, logits = sem("h2_ready"), sem("h2_t"), sem("h2T_ready"), sem("logits")
        shift_ready, exp_ready, hot_ready, ranks = sem("shift_ready"), sem("exp_ready"), sem("hot_ready"), sem("ranks")
        pos_ready, rows_out, tile_ready = sem("pos_ready"), sem("rows_out"), sem("tile_ready")
        s_gu, s_silu, s_act, s_down, s_added = (sem(n) for n in ("s_gu", "s_silu", "s_act", "s_down", "s_added"))
        xs_in = [sem("xs_in0"), sem("xs_in1")]
        x_tr, xT_ready, gu_mm, sg_ready = sem("x_tr"), sem("xT_ready"), sem("gu_mm"), sem("sg_ready")
        act_ready, act_tr, actT_ready = sem("act_ready"), sem("act_tr"), sem("actT_ready")
        dn_mm, y_ready = sem("dn_mm"), sem("y_ready")
        y_out = [sem("y_out0"), sem("y_out1")]
        got_y = [sem("got_y0"), sem("got_y1")]
        out_ready, out_done = sem("out_ready"), sem("out_done")
        dve_chain, act_chain = sem("dve_chain"), sem("act_chain")

        block = ctx.enter_context(nc.Block())

        def parity(g):
            return g % 2

        @block.sync
        def _(sp):
            sp.dma_start(c_sb[:], c).then_inc(c_in, 16)
            for h in range(2):
                sp.dma_start(x_sb[:, 4 * h:4 * h + 4, :], x_t[:, 4 * h:4 * h + 4, :]).then_inc(x_in, 16)
                if h == 0:
                    sp.wait_ge(x_in, 16)
            sp.dma_start(signw, wqkv).then_inc(w_in, 16)
            sp.dma_start(qk_sc[:], qk_scale).then_inc(small_in, 16)
            sp.dma_start(v_sc[:], v_scale.partition_broadcast(P)).then_inc(small_in, 16)
            sp.dma_start(rows[:, 4, :], o_scale.partition_broadcast(P)).then_inc(small_in, 16)
            sp.dma_start(gate_sb[:], gate).then_inc(gate_in, 16)
            for j in range(4):
                if j >= 2:
                    sp.wait_ge(mod_mm, j - 1)
                sp.dma_start(wmod_ring[:, j % 2], wmod_k[:, :, j * D:(j + 1) * D]).then_inc(wmod_in[j % 2], 16)
                if j == 1:
                    sp.dma_start(signw_o, wo).then_inc(wo_in, 16)
            for n in range(2 * QK_TILES):
                half, m = divmod(n, QK_TILES)
                sp.wait_ge(parts_ready, n + 1)
                sp.dma_start(q_parts_d[:, m * P:(m + 1) * P, half * HALF:(half + 1) * HALF].rearrange("a p n -> p a n"),
                             parts_st[:, n % 2]).then_inc(parts_out[n % 2], 16)
            for b in range(2):
                sp.wait_ge(parts_out[b], 16 * QK_TILES)

            def load_group(g, par):
                for n, (a, b) in enumerate(PAIRS):
                    q = q_parts_d[a, bass.ds(g * (G * DH), G * DH), :].rearrange("(h d) n -> d h n", d=DH)
                    sp.dma_start(q_ring[DH * n:DH * n + DH, par], q).then_inc(qk_in[par], 16)
                    sp.dma_start(k_ring[DH * n:DH * n + DH, par], q_parts_d[b, bass.ds(g * DH + D, DH), :])\
                        .then_inc(qk_in[par], 16)

            def load_max(g, par):
                sp.wait_ge(max_parts, g + 1)
                for a in range(PARTS):
                    sp.dma_start(q_ring[KROWS + a:KROWS + a + 1, par], mparts[:, a, :]).then_inc(max_row_in[par], 16)

            def store_o(g, par, half):
                sp.wait_ge(o_read, g * 2 + half + 1)
                m = g // 2 if isinstance(g, int) else (g - par) // 2
                for hd in range(G):
                    row = par * G * DH + hd * DH
                    for src, dst in ((32 * hd, oT), (32 * hd + DH, den)):
                        sp.dma_start(dst[row:row + DH, bass.ds(m, 1), half * HALF:(half + 1) * HALF]
                                     .rearrange("p a n -> p (a n)"),
                                     ov[src:src + DH, half, :]).then_inc(o_out[half], 16)

            sp.wait_ge(mod_mm, 6)
            load_group(0, 0)
            load_group(1, 1)
            load_max(0, 0)

            def group(g, par, first=False, last=False, loads=True):
                if not first:
                    store_o(g - 1, 1 - par, 1)
                store_o(g, par, 0)
                if not last:
                    load_max(g + 1, 1 - par)
                if loads:
                    sp.wait_ge(scores, g * 32 + 32)
                    load_group(g + 2, par)

            group(0, 0, first=True)
            with sp.Fori(0, 2) as i:
                group(i * 2 + 1, 1)
                group(i * 2 + 2, 0)
            group(5, 1)
            group(6, 0, loads=False)
            group(7, 1, last=True, loads=False)
            store_o(7, 1, 1)

            sp.wait_ge(pv_done, NKV * 16)
            for h in range(2):
                sp.dma_start(x_sb[:, 4 * h:4 * h + 4, :], x_t[:, 4 * h:4 * h + 4, :]).then_inc(x2_in, 16)
            for half in range(2):
                sp.wait_ge(o_out[half], NKV * 2 * G * 16)
            sp.dma_start(wd_sb, wd).then_inc(wd_in, 16)
            sp.wait_ge(o_mm, TT)
            sp.dma_start(sd_sb, sd).then_inc(sd_in, 16)

            sp.wait_ge(rows_out, 16 * TOPK * TT)

            def load_rows(j, b):
                sp.dma_start(xs[:, b, :], rows_d[bass.ds(j * P, P), :]).then_inc(xs_in[b], 16)

            load_rows(0, 0)
            load_rows(1, 1)
            with sp.Fori(0, (TILES - 3) // 2) as i:
                for b in range(2):
                    sp.wait_ge(x_tr, i * 2 + b + 1)
                    load_rows(i * 2 + b + 2, b)
            j = TILES - 3
            sp.wait_ge(x_tr, j + 1)
            load_rows(j + 2, 0)
            for t in range(TT):
                sp.wait_ge(out_ready, t + 1)
                sp.dma_start(out_t[:, t, :], x_sb[:, t, :]).then_inc(out_done, 16)
            sp.wait_ge(out_done, 16 * TT)

        @block.gpsimd
        def _(pool):
            nc.gpsimd.memset(ident[:], 0.0).then_inc(consts, 1)
            nc.gpsimd.memset(before[:], 1.0).then_inc(consts, 1)
            nc.gpsimd.memset(ones[:], 1.0).then_inc(consts, 1)
            nc.gpsimd.memset(wgu_sb[:, 0, 0:D], 0.0).then_inc(zero_ready, 1)
            pool.wait_ge(consts, 3)
            nc.gpsimd.affine_select(out=ident[:], in_=ident[:], compare_op=ALU.not_equal, fill=1.0, base=0,
                                    pattern=[[-1, P]], channel_multiplier=1).then_inc(consts, 1)
            nc.gpsimd.affine_select(out=before[:], in_=before[:], compare_op=ALU.is_gt, fill=0.0, base=0,
                                    pattern=[[1, P]], channel_multiplier=-1).then_inc(consts, 1)
            nc.gpsimd.iota(rev[:], pattern=[[-1, E]], base=E, channel_multiplier=0,
                           allow_small_or_imprecise_dtypes=True).then_inc(consts, 1)
            nc.gpsimd.iota(tile_no[:], pattern=[[1, TILES]], base=0, channel_multiplier=0,
                           allow_small_or_imprecise_dtypes=True).then_inc(consts, 1)
            pool.wait_ge(zero_ready, 1)
            pool.dma_start(rows_d.rearrange("(t p) n -> p t n", p=P),
                           wgu_sb[:, 0:1, 0:D].to_broadcast([P, TILES, D])).then_inc(zero_out, 16)
            pool.dma_start(sgu_sb[:], sgu).then_inc(sgu_in, 16)
            pool.wait_ge(w_sums, 2)
            nc.gpsimd.memset(v_sb[:, :, :, DH:2 * DH], 1.0).then_inc(v_ones, 1)
            for b in range(2):
                pool.wait_ge(parts_out[b], 16 * QK_TILES)
            pool.wait_ge(v_ones, 1)
            nc.gpsimd.memset(k_ring[KROWS:AROWS, :, :], 1.0).then_inc(k_ones, 1)
            pool.wait_ge(v_ready, 2)
            pool.wait_ge(k_ones, 1)
            pool.wait_ge(zero_out, 16)

            def group_v(g, par):
                nc.gpsimd.tensor_copy(vg[:, par],
                                      v_sb[:, :, bass.ds(g, 1), :].rearrange("p t a n -> p t (a n)"))\
                    .then_inc(vg_ready, 1)
                pool.dma_start(wgu_sb[:, bass.ds(g * 2, 2), :], wgu[:, bass.ds(g * 2, 2), :]).then_inc(wgu_in, 16)

            group_v(0, 0)
            group_v(1, 1)
            with pool.Fori(0, 3) as i:
                for par in range(2):
                    pool.wait_ge(pv_done, i * 32 + (par + 1) * 16)
                    group_v(i * 2 + (par + 2), par)
            pool.wait_ge(pos_ready, 1)
            pool.wait_ge(h2_ready, TT)
            for t in range(TT):
                for k in range(TOPK):
                    nc.gpsimd.indirect_dma_start(
                        out=rows_d, out_offset=bass.IndirectOffsetOnAxis(ap=pos[:, k, t:t + 1], axis=0),
                        in_=h2[:, t, :], in_offset=None).then_inc(rows_out, 16)
            pool.wait_ge(y_out[0], 16 * ((TILES + 1) // 2))
            pool.wait_ge(y_out[1], 16 * (TILES // 2))
            pool.wait_ge(s_down, TT)
            for t in range(TT):
                if t >= 2:
                    pool.wait_ge(out_ready, t - 1)
                for k in range(TOPK):
                    nc.gpsimd.indirect_dma_start(
                        out=y_in[:, t % 2, k, :], out_offset=None, in_=moe_d,
                        in_offset=bass.IndirectOffsetOnAxis(ap=pos[:, k, t:t + 1], axis=0))\
                        .then_inc(got_y[t % 2], 16)

        @block.scalar
        def _(act):
            act.wait_ge(c_in, 16)
            nc.scalar.activation(c_si[:], c_sb[:], ACT.Silu).then_inc(c_ready, 1)
            act.wait_ge(c_ready, 1)
            nc.scalar.activation(c_bc[:], c_si[:].unsqueeze(2).to_broadcast([P, KC, P]), ACT.Copy)\
                .then_inc(c_ready, 1)
            for h in range(2):
                act.wait_ge(var_ready, h + 1)
                nc.scalar.activation(rstd[:, 4 * h:4 * h + 4], rstd[:, 4 * h:4 * h + 4], ACT.Sqrt)\
                    .then_inc(std_ready, 1)
                if h == 0:
                    act.wait_ge(w_in, 16)
                    nc.scalar.activation(absw, signw, ACT.Abs).then_inc(abs_ready, 1)
                    act.wait_ge(abs_ready, 1)
                    nc.scalar.activation(signw, signw, ACT.Sign).then_inc(sign_ready, 1)
            act.wait_ge(wo_in, 16)
            nc.scalar.activation(absw_o, signw_o, ACT.Abs).then_inc(abs_ready, 1)
            act.wait_ge(abs_ready, 2)
            nc.scalar.activation(signw_o, signw_o, ACT.Sign).then_inc(sign_ready, 1)

            for j in range(4, 6):
                act.wait_ge(mod_mm, j - 1)
                act.dma_start(wmod_ring[:, j % 2], wmod_k[:, :, j * D:(j + 1) * D]).then_inc(wmod_in[j % 2], 16)

            def read_o(g, half):
                act.wait_ge(pv_done, g * 16 + 8 * half + 8)
                if not (isinstance(g, int) and g == 0):
                    act.wait_ge(o_out[half], g * (2 * G * 16))
                nc.scalar.activation(ov[:, half, :], ps[:, 4, :], ACT.Copy).then_inc(o_read, 1)

            def group(g, first=False):
                for s in range(16):
                    for i in range(2):
                        act.wait_ge(scores, g * 32 + (2 * s + i + 1))
                        if i == 0 and not (first and s < 2):
                            act.wait_ge(pv_done, g * 16 + (s - 1))
                        nc.scalar.activation(probs[:, (2 * s + i) % 4, :],
                                             ps[:, 2 * i:2 * i + 2, :].rearrange("p b n -> p (b n)"),
                                             ACT.Exp, scale=DH ** -0.5).then_inc(probs_ready, 1)
                    if s == 0 and not first:
                        read_o(g - 1, 1)
                    if s == 8:
                        read_o(g, 0)

            group(0, first=True)
            with act.Fori(0, NKV - 1) as i:
                group(i + 1)
            read_o(NKV - 1, 1)

            for t in range(TT):
                act.wait_ge(var_ready, 3 + t)
                nc.scalar.activation(rstd[:, t:t + 1], rstd[:, t:t + 1], ACT.Sqrt).then_inc(std_ready, 1)
            for n in range(2 * KC):
                half, k = divmod(n, KC)
                act.wait_ge(h2_t, n + 1)
                nc.scalar.activation(h2T[:, k, half * HALF:(half + 1) * HALF], ps[:, 2 + n % 2, :], ACT.Copy)\
                    .then_inc(h2T_ready, 1)
            act.wait_ge(shift_ready, 1)
            nc.scalar.activation(pr, lg, ACT.Exp).then_inc(exp_ready, 1)
            for n in range(2 * KC):
                act.wait_ge(s_gu, n + 1)
                if n >= 2:
                    act.wait_ge(s_act, n - 1)
                nc.scalar.activation(tmp[:, n % 2, :], ps[:, 4 * (n % 2) + 2, :], ACT.Silu).then_inc(s_silu, 1)

            def silu(j, b, first=False):
                act.wait_ge(gu_mm, j + 1)
                if not first:
                    act.wait_ge(act_ready, j - 1)
                nc.scalar.activation(sg[:, b, :], ps[:, 2 + b, 0:I], ACT.Silu).then_inc(sg_ready, 1)

            def copy_act(j, b, first=False):
                act.wait_ge(act_tr, j + 1)
                if not first:
                    act.wait_ge(dn_mm, j - 1)
                nc.scalar.activation(actT[:, b, :], ps[:, 4 + b, 0:P], ACT.Copy).then_inc(actT_ready, 1)

            def copy_y(j, b, first=False):
                act.wait_ge(dn_mm, j + 1)
                if not first:
                    act.wait_ge(y_out[b], (j - b) * 8)
                nc.scalar.activation(y_sb[:, b, :], ps[:, 6 + b, :], ACT.Copy).then_inc(y_ready, 1)
                act.wait_ge(y_ready, j + 1)
                act.dma_start(moe_d[bass.ds(j * P, P), :], y_sb[:, b, :]).then_inc(y_out[b], 16)

            silu(0, 0, first=True)
            copy_act(0, 0, first=True)
            silu(1, 1, first=True)
            copy_y(0, 0, first=True)
            copy_act(1, 1, first=True)
            silu(2, 0)
            copy_y(1, 1, first=True)
            with act.Fori(0, (TILES - 3) // 2) as i:
                for b in range(2):
                    j = i * 2 + (b + 2)
                    copy_act(j, b)
                    silu(j + 1, 1 - b)
                    copy_y(j, b)
            j = TILES - 1
            copy_act(j, 0)
            copy_y(j, 0)

        @block.vector
        def _(dve):
            linked = [0]

            def link(ins):
                linked[0] += 1
                ins.then_inc(dve_chain, 1)
                dve.wait_ge(dve_chain, linked[0])

            V = nc.vector

            def nan_to_num(v, a, mask):
                link(V.tensor_scalar(mask, v, 0.0, 0.0, ALU.mult, ALU.not_equal))
                link(V.tensor_scalar(a, v, 0.0, BIG, ALU.max, ALU.min))
                link(V.scalar_tensor_tensor(out=a, in0=v, scalar=0.0, in1=a, op0=ALU.min, op1=ALU.add))
                link(V.tensor_scalar(a, a, -BIG, None, ALU.max))
                link(V.copy_predicated(v, mask, a))

            z, za, zm = tmp[:, 0, :], tmp[:, 1, :], tmp[:, 2, :].bitcast(i32)

            def norm_stats(t):
                link(V.bn_stats(stats[:, t, :], x_sb[:, t, :]))
                link(V.bn_aggr(mv[:, t, :], stats[:, t, :]))

            for h in range(2):
                dve.wait_ge(x_in, 16 * (h + 1))
                for t in range(4 * h, 4 * h + 4):
                    norm_stats(t)
                V.tensor_scalar(rstd[:, 4 * h:4 * h + 4], mv[:, 4 * h:4 * h + 4, 1], LN_EPS, None, ALU.add)\
                    .then_inc(var_ready, 1)
                dve.wait_ge(std_ready, h + 1)
                link(V.reciprocal(rstd[:, 4 * h:4 * h + 4], rstd[:, 4 * h:4 * h + 4]))
                for t in range(4 * h, 4 * h + 4):
                    V.tensor_scalar(xn[:, t, :], x_sb[:, t, :], mv[:, t, 0:1], rstd[:, t:t + 1],
                                    ALU.subtract, ALU.mult).then_inc(xn_ready, 1)
            dve.wait_ge(w_sums, 1)
            dve.wait_ge(small_in, 48)
            link(V.tensor_scalar(scol[:], ps[:, 0, 0:QK_TILES], 1.0 / D, 1e-8, ALU.mult, ALU.max))
            link(V.tensor_tensor(scol[:], scol[:], qk_sc[:], ALU.mult))
            link(V.tensor_scalar(za[:, 0:KV], ps[:, 1, 0:KV], 1.0 / D, 1e-8, ALU.mult, ALU.max))
            link(V.tensor_tensor(v_sc[:], za[:, 0:KV], v_sc[:], ALU.mult))
            dve.wait_ge(mod_mm, 2)
            for j in range(2):
                link(V.tensor_scalar(mcol[:, j, :], ps[:, 3, KC * j:KC * j + KC], float(j), None, ALU.add))
            for n in range(2 * KC):
                half, k = divmod(n, KC)
                dve.wait_ge(h_t, n + 1)
                V.tensor_scalar(hT[:, k, half * HALF:(half + 1) * HALF], ps[:, n % 2, :],
                                mcol[:, 1, k:k + 1], mcol[:, 0, k:k + 1], ALU.mult, ALU.add).then_inc(hT_ready, 1)
            n = 0
            for half in range(2):
                for m in range(QK_TILES):
                    u = half * (QK_TILES + 1) + m
                    dve.wait_ge(qkv_mm, u + 1)
                    link(V.tensor_scalar(z, ps[:, 2 + u % 2, :], scol[:, m:m + 1], None, ALU.mult))
                    V.engine_nop().then_inc(qkv_read, 1)
                    nan_to_num(z, za, zm)
                    if n >= 2:
                        dve.wait_ge(parts_out[n % 2], 16 * (n // 2))
                    st = parts_st[:, n % 2]
                    link(V.tensor_copy(st[:, 0, :], z))
                    link(V.tensor_tensor(z, z, st[:, 0, :], ALU.subtract))
                    link(V.tensor_copy(st[:, 1, :], z))
                    ins = V.tensor_tensor(st[:, 2, :], z, st[:, 1, :], ALU.subtract)
                    ins.then_inc(parts_ready, 1)
                    dve.wait_ge(parts_ready, n + 1)
                    n += 1
                u = half * (QK_TILES + 1) + QK_TILES
                dve.wait_ge(qkv_mm, u + 1)
                link(V.tensor_tensor(z.rearrange("p (t n) -> p t n", n=KV),
                                     ps[:, 2 + u % 2, :].rearrange("p (t n) -> p t n", n=KV),
                                     v_sc[:].unsqueeze(1).to_broadcast([P, 4, KV]), ALU.mult))
                V.engine_nop().then_inc(qkv_read, 1)
                nan_to_num(z, za, zm)
                V.tensor_copy(v_sb[:, 4 * half:4 * half + 4, :, 0:DH],
                              z.rearrange("p (t h n) -> p t h n", t=4, h=NKV)).then_inc(v_ready, 1)
                dve.wait_ge(v_ready, half + 1)
            dve.wait_ge(w_sums, 2)
            link(V.tensor_scalar(za, ps[:, 4, :], 1.0 / D, 1e-8, ALU.mult, ALU.max))
            link(V.tensor_tensor(rows[:, 4, :], za, rows[:, 4, :], ALU.mult))
            for j in range(4):
                dve.wait_ge(mod_mm, j + 3)
                src = ps[:, 5 + j % 2, :]
                if j in (0, 3):
                    link(V.tensor_scalar(z, src, 0.0, 2.0, ALU.is_ge, ALU.mult))
                    link(V.scalar_tensor_tensor(out=za, in0=z, scalar=1.0, in1=src, op0=ALU.subtract, op1=ALU.mult))
                    link(V.tensor_scalar(za, za, 0.25, None, ALU.max))
                    ins = V.scalar_tensor_tensor(out=rows[:, j, :], in0=z, scalar=1.0, in1=za,
                                                 op0=ALU.subtract, op1=ALU.mult)
                else:
                    ins = V.tensor_scalar(rows[:, j, :], src, 1.0 if j == 2 else 0.0, None, ALU.add)
                ins.then_inc(mod_read, 1)
                dve.wait_ge(mod_read, j + 1)

            def group_max(g, base):
                for n in range(2 * G * TT):
                    dve.wait_ge(max_scores, g * 64 + (n + 1))
                    V.reduce_max(mxh[:, n:n + 1], ps[:, 5 + n % MAX_BANKS, :], AX).then_inc(max_read, 1)
                dve.wait_ge(max_read, g * 64 + 64)
                pairs = mxh[:].rearrange("p (n k) -> p n k", k=2)
                V.tensor_tensor(mxc[:], pairs[:, :, 0], pairs[:, :, 1], ALU.max).then_inc(max_cols, 1)
                dve.wait_ge(max_cols, g + 1)
                dve.wait_ge(max_t, g + 1)
                k = [0]

                def step(ins):
                    k[0] += 1
                    ins.then_inc(dve_chain, 1)
                    dve.wait_ge(dve_chain, g * 4 + (base + k[0]))

                step(V.tensor_scalar(mneg[:, 0, :], ps[0:G * TT, 5, 0:P], -1.0, None, ALU.mult))
                return step

            def split_max(step, g):
                step(V.tensor_copy(mparts[:, 0, :], mneg[:, 0, :]))
                step(V.tensor_tensor(mneg[:, 1, :], mneg[:, 0, :], mparts[:, 0, :], ALU.subtract))
                step(V.tensor_copy(mparts[:, 1, :], mneg[:, 1, :]))
                V.tensor_tensor(mparts[:, 2, :], mneg[:, 1, :], mparts[:, 1, :], ALU.subtract)\
                    .then_inc(max_parts, 1)
                dve.wait_ge(max_parts, g + 1)

            base = linked[0]
            split_max(group_max(0, base), 0)
            with dve.Fori(0, 3) as i:
                for par in range(2):
                    g = i * 2 + (par + 1)
                    step = group_max(g, base)
                    dve.wait_ge(max_row_in[par], i * 48 + 48)
                    split_max(step, g)
            step = group_max(NKV - 1, base)
            dve.wait_ge(max_row_in[0], 4 * 48)
            split_max(step, NKV - 1)
            linked[0] = base + 4 * NKV

            for half in range(2):
                dve.wait_ge(o_out[half], NKV * 2 * G * 16)
            for m in range(KC):
                link(V.reciprocal(den[:, m, :], den[:, m, :]))
                V.tensor_tensor(oT[:, m, :], oT[:, m, :], den[:, m, :], ALU.mult).then_inc(oT_ready, 1)
            dve.wait_ge(oT_ready, KC)
            for t in range(TT):
                dve.wait_ge(o_mm, t + 1)
                link(V.tensor_tensor(z, ps[:, t % 2, :], rows[:, 4, :], ALU.mult))
                V.engine_nop().then_inc(o_mm_read, 1)
                nan_to_num(z, za, zm)
                link(V.tensor_tensor(z, z, rows[:, 0, :], ALU.mult))
                if t == 0:
                    dve.wait_ge(x2_in, 32)
                link(V.tensor_tensor(x_sb[:, t, :], x_sb[:, t, :], z, ALU.add))
                norm_stats(t)
                V.tensor_scalar(rstd[:, t:t + 1], mv[:, t, 1:2], LN_EPS, None, ALU.add).then_inc(var_ready, 1)
                dve.wait_ge(std_ready, 3 + t)
                link(V.reciprocal(rstd[:, t:t + 1], rstd[:, t:t + 1]))
                link(V.tensor_scalar(z, x_sb[:, t, :], mv[:, t, 0:1], rstd[:, t:t + 1], ALU.subtract, ALU.mult))
                link(V.tensor_tensor(z, z, rows[:, 2, :], ALU.mult))
                V.tensor_tensor(h2[:, t, :], z, rows[:, 1, :], ALU.add).then_inc(h2_ready, 1)
                dve.wait_ge(h2_ready, t + 1)

            dve.wait_ge(consts, 7)

            def bc(a):
                return a.unsqueeze(2).to_broadcast([P, TT, E])

            dve.wait_ge(logits, TT)
            lps = ps[:, 4, 0:TT * E].rearrange("p (t e) -> p t e", e=E)
            link(V.tensor_reduce(col[:, 0, :], lps, AX, ALU.max))
            V.tensor_tensor(lg, lps, bc(col[:, 0, :]), ALU.subtract).then_inc(shift_ready, 1)
            dve.wait_ge(exp_ready, 1)
            link(V.tensor_reduce(col[:, 1, :], pr, AX, ALU.add))
            link(V.reciprocal(col[:, 1, :], col[:, 1, :]))
            link(V.tensor_tensor(pr, pr, bc(col[:, 1, :]), ALU.mult))
            link(V.memset(hot, 0.0))
            for k in range(TOPK):
                link(V.tensor_reduce(col[:, 2 + k, :], pr, AX, ALU.max))
                link(V.tensor_tensor(cand, pr, bc(col[:, 2 + k, :]), ALU.is_equal))
                link(V.tensor_tensor(cand, cand, rev[:].unsqueeze(1).to_broadcast([P, TT, E]), ALU.mult))
                link(V.tensor_reduce(col[:, 4, :], cand, AX, ALU.max))
                link(V.tensor_tensor(hot[:, k, 0:TT, :], cand, bc(col[:, 4, :]), ALU.is_equal))
                if k == 0:
                    link(V.scalar_tensor_tensor(out=pr, in0=hot[:, 0, 0:TT, :], scalar=-2.0, in1=pr,
                                                op0=ALU.mult, op1=ALU.add))
            V.tensor_tensor(both, hot[:, 0], hot[:, 1], ALU.add).then_inc(hot_ready, 1)
            link(V.tensor_tensor(col[:, 4, :], col[:, 2, :], col[:, 3, :], ALU.add))
            link(V.reciprocal(col[:, 4, :], col[:, 4, :]))
            for k in range(TOPK):
                link(V.tensor_tensor(wcol[:, k, :], col[:, 2 + k, :], col[:, 4, :], ALU.mult))
            dve.wait_ge(ranks, 1)
            total = ps[:, 5, TT * E:(TT + 1) * E]
            link(V.memset(cnt[:], 0.0))
            link(V.tensor_scalar(cnt_i[:, 0, :], total, float(P - 1), None, ALU.add))
            link(V.tensor_scalar(cnt_i[:, 1, :], cnt_i[:, 0, :], 7, None, ALU.arith_shift_right))
            link(V.tensor_copy(cnt[:, 0, :], cnt_i[:, 1, :]))
            link(V.tensor_tensor_scan(cnt[:, 1, :], cnt[:, 0, :], cnt[:, 3, :], 0.0, ALU.add, ALU.add))
            link(V.tensor_tensor(cnt[:, 2, :], cnt[:, 1, :], cnt[:, 0, :], ALU.subtract))
            link(V.tensor_scalar(cnt[:, 2, :], cnt[:, 2, :], float(P), None, ALU.mult))
            link(V.tensor_tensor(lg, ps[:, 5, 0:TT * E].rearrange("p (t e) -> p t e", e=E),
                                 cnt[:, 2, :].unsqueeze(1).to_broadcast([P, TT, E]), ALU.add))
            for k in range(TOPK):
                link(V.tensor_tensor(cand, lg, hot[:, k, 0:TT, :], ALU.mult))
                link(V.tensor_reduce(pos_f[:, k, :], cand, AX, ALU.add))
            V.tensor_copy(pos[:], pos_f[:]).then_inc(pos_ready, 1)
            link(V.tensor_tensor(tile_cmp, tile_no[:].unsqueeze(2).to_broadcast([1, TILES, E]), cnt[0:1, 1, :].unsqueeze(1).to_broadcast([1, TILES, E]),
                                 ALU.is_ge))
            link(V.tensor_reduce(tile_e[:, 0, :], tile_cmp, AX, ALU.add))
            link(V.tensor_scalar(tile_e[:, 1, :], tile_e[:, 0, :], float(E - 1), None, ALU.min))
            V.tensor_copy(tile_ei[:], tile_e[:, 1, :]).then_inc(tile_ready, 1)

            for n in range(2 * KC):
                half, i = divmod(n, KC)
                dve.wait_ge(s_silu, n + 1)
                V.tensor_tensor(asT[:, i, half * HALF:(half + 1) * HALF], tmp[:, n % 2, :],
                                ps[:, 4 * (n % 2) + 3, :], ALU.mult).then_inc(s_act, 1)
            dve.wait_ge(s_act, 2 * KC)
            for t in range(TT):
                dve.wait_ge(s_down, t + 1)
                link(V.tensor_tensor(z, ps[:, t % 2, :], rows[:, 3, :], ALU.mult))
                V.tensor_tensor(x_sb[:, t, :], x_sb[:, t, :], z, ALU.add).then_inc(s_added, 1)
                dve.wait_ge(s_added, t + 1)

            def copy_x(j, b, first=False):
                dve.wait_ge(x_tr, j + 1)
                if not first:
                    dve.wait_ge(gu_mm, j - 1)
                V.tensor_copy(xT[:, b, :], ps[:, b, :]).then_inc(xT_ready, 1)

            def multiply(j, b, first=False):
                dve.wait_ge(sg_ready, j + 1)
                if not first:
                    dve.wait_ge(act_tr, j - 1)
                V.tensor_tensor(act_sb[:, b, :], sg[:, b, :], ps[:, 2 + b, I:2 * I], ALU.mult)\
                    .then_inc(act_ready, 1)

            dve.wait_ge(rows_out, 16 * TOPK * TT)
            copy_x(0, 0, first=True)
            copy_x(1, 1, first=True)
            multiply(0, 0, first=True)
            copy_x(2, 0)
            multiply(1, 1, first=True)
            with dve.Fori(0, (TILES - 3) // 2) as i:
                for b in range(2):
                    j = i * 2 + (b + 2)
                    copy_x(j + 1, 1 - b)
                    multiply(j, b)
            multiply(TILES - 1, 0)
            dve.wait_ge(s_added, TT)
            for t in range(TT):
                dve.wait_ge(got_y[t % 2], 32 * (t // 2 + 1))
                link(V.tensor_scalar(z, y_in[:, t % 2, 0, :], wcol[:, 0, t:t + 1], None, ALU.mult))
                link(V.scalar_tensor_tensor(out=z, in0=y_in[:, t % 2, 1, :], scalar=wcol[:, 1, t:t + 1], in1=z,
                                            op0=ALU.mult, op1=ALU.add))
                link(V.tensor_tensor(z, z, rows[:, 3, :], ALU.mult))
                V.tensor_tensor(x_sb[:, t, :], x_sb[:, t, :], z, ALU.add).then_inc(out_ready, 1)
                dve.wait_ge(out_ready, t + 1)

        @block.tensor
        def _(pe):
            T = nc.tensor

            def mm(o, lhsT, rhs, k, n):
                return T.matmul(o, lhsT, rhs, start=(k == 0), stop=(k == n - 1))

            pe.wait_ge(consts, 5)
            pe.wait_ge(abs_ready, 1)
            for m in range(QK_TILES):
                for k in range(KC):
                    mm(ps[:, 0, m:m + 1], absw[:, k, m * P:(m + 1) * P], ones[:, 0:1], k, KC)
            for k in range(KC):
                last = mm(ps[:, 1, 0:KV], ones[:], absw[:, k, D + KV:], k, KC)
            last.then_inc(w_sums, 1)
            pe.wait_ge(c_ready, 2)
            for j in range(2):
                pe.wait_ge(wmod_in[j], 16)
                for n in range(KC):
                    for k in range(KC):
                        last = mm(ps[:, 3, KC * j + n:KC * j + n + 1], wmod_ring[:, j, k, n * P:(n + 1) * P],
                                  c_si[:, k:k + 1], k, KC)
                last.then_inc(mod_mm, 1)
            pe.wait_ge(abs_ready, 2)
            for k in range(KC):
                last = mm(ps[:, 4, :], ones[:], absw_o[:, k, :], k, KC)
            last.then_inc(w_sums, 1)
            for n in range(2 * KC):
                half, k = divmod(n, KC)
                if k == 0:
                    pe.wait_ge(xn_ready, 4 * half + 4)
                if n == 0:
                    pe.wait_ge(dve_chain, 2 * TT + 2 + 4)
                if n >= 2:
                    pe.wait_ge(hT_ready, n - 1)
                for t in range(4):
                    last = T.transpose(ps[:, n % 2, t * P:(t + 1) * P], xn[:, 4 * half + t, k * P:(k + 1) * P], ident[:])
                last.then_inc(h_t, 1)
            pe.wait_ge(sign_ready, 1)
            for half in range(2):
                pe.wait_ge(hT_ready, KC * (half + 1))
                for m in range(QK_TILES + 1):
                    u = half * (QK_TILES + 1) + m
                    if u >= 2:
                        pe.wait_ge(qkv_read, u - 1)
                    o = ps[:, 2 + u % 2, :]
                    if m < QK_TILES:
                        for k in range(KC):
                            last = mm(o, signw[:, k, m * P:(m + 1) * P], hT[:, k, half * HALF:(half + 1) * HALF], k, KC)
                    else:
                        for t in range(4):
                            for k in range(KC):
                                a = half * HALF + t * P
                                last = mm(o[:, t * KV:(t + 1) * KV], hT[:, k, a:a + P], signw[:, k, D + KV:], k, KC)
                    last.then_inc(qkv_mm, 1)
            for j in range(2, 6):
                pe.wait_ge(wmod_in[j % 2], 16 * (j // 2 + 1))
                if j >= 4:
                    pe.wait_ge(mod_read, j - 3)
                for k in range(KC):
                    last = mm(ps[:, 5 + j % 2, :], c_bc[:, k, :], wmod_ring[:, j % 2, k, :], k, KC)
                last.then_inc(mod_mm, 1)
            pe.wait_ge(mod_read, 4)

            def max_scores_of(g, par, n, first=False):
                hd, t, kh = n // (2 * TT), (n // 2) % TT, n % 2
                if n == 0:
                    pe.wait_ge(qk_in[par], 16 * 2 * len(PAIRS) * (g // 2 + 1) if isinstance(g, int)
                               else (g - par) * 96 + 192)
                if n >= MAX_BANKS:
                    pe.wait_ge(max_read, g * 64 + (n - MAX_BANKS + 1))
                elif n == 0 and not first:
                    pe.wait_ge(max_parts, g)
                T.matmul(ps[:, 5 + n % MAX_BANKS, :], q_ring[0:KROWS, par, hd, t * P:(t + 1) * P],
                         k_ring[0:KROWS, par, kh * HALF:(kh + 1) * HALF], start=True, stop=True)\
                    .then_inc(max_scores, 1)

            def max_transpose(g):
                pe.wait_ge(max_cols, g + 1)
                T.transpose(ps[0:G * TT, 5, 0:P], mxc[:], ident[:]).then_inc(max_t, 1)

            def score(g, par, s, i, first=False):
                half, kt = divmod(s, TT)
                if s == 0 and i == 0:
                    pe.wait_ge(max_row_in[par], 48 * (g // 2 + 1) if isinstance(g, int) else (g - par) * 24 + 48)
                if not (first and s == 0):
                    pe.wait_ge(probs_ready, g * 32 + (2 * s + i - 1))
                for j in range(2):
                    last = T.matmul(ps[:, 2 * i + j, :], k_ring[0:AROWS, par, kt * P:(kt + 1) * P],
                                    q_ring[0:AROWS, par, 2 * i + j, half * HALF:(half + 1) * HALF],
                                    start=True, stop=True)
                last.then_inc(scores, 1)

            def pv(g, par, s, first=False):
                half, kt = divmod(s, TT)
                pe.wait_ge(probs_ready, g * 32 + (2 * s + 2))
                if s == 0:
                    pe.wait_ge(vg_ready, g + 1)
                if kt == 0 and not (first and half == 0):
                    pe.wait_ge(o_read, g * 2 + half)
                for hd in range(G):
                    last = T.matmul(ps[32 * hd:32 * hd + 32, 4, :], vg[:, par, kt, :],
                                    probs[:, (2 * s + hd // 2) % 4, (hd % 2) * HALF:(hd % 2 + 1) * HALF],
                                    start=(kt == 0), stop=(kt == TT - 1))
                last.then_inc(pv_done, 1)

            def group(g, par, first=False, last=False):
                n = 0

                def maxima(count):
                    nonlocal n
                    for _ in range(count):
                        if not last and n < 2 * G * TT:
                            max_scores_of(g + 1, 1 - par, n)
                            n += 1

                for s in range(16):
                    score(g, par, s, 0, first)
                    maxima(2)
                    score(g, par, s, 1, first)
                    maxima(2)
                    if s > 0:
                        pv(g, par, s - 1, first)
                    elif not first:
                        pv(g - 1, 1 - par, 15)
                    maxima(1)
                    if s == 13 and not last:
                        max_transpose(g + 1)

            pe.wait_ge(k_ones, 1)
            for n in range(2 * G * TT):
                max_scores_of(0, 0, n, first=True)
            max_transpose(0)
            group(0, 0, first=True)
            with pe.Fori(0, 3) as i:
                group(i * 2 + 1, 1)
                group(i * 2 + 2, 0)
            group(NKV - 1, 1, last=True)
            pv(NKV - 1, 1, 15)

            pe.wait_ge(sign_ready, 2)
            pe.wait_ge(oT_ready, KC)
            for t in range(TT):
                if t >= 2:
                    pe.wait_ge(o_mm_read, t - 1)
                for m in range(KC):
                    last = mm(ps[:, t % 2, :], oT[:, m, t * P:(t + 1) * P], signw_o[:, m, :], m, KC)
                last.then_inc(o_mm, 1)
            pe.wait_ge(gate_in, 16)
            for half in range(2):
                pe.wait_ge(h2_ready, 4 * half + 4)
                for k in range(KC):
                    n = half * KC + k
                    if n >= 2:
                        pe.wait_ge(h2T_ready, n - 1)
                    for t in range(4):
                        last = T.transpose(ps[:, 2 + n % 2, t * P:(t + 1) * P],
                                           h2[:, 4 * half + t, k * P:(k + 1) * P], ident[:])
                    last.then_inc(h2_t, 1)
                pe.wait_ge(h2T_ready, KC * (half + 1))
                for t in range(4 * half, 4 * half + 4):
                    for k in range(KC):
                        last = mm(ps[:, 4, t * E:(t + 1) * E], h2T[:, k, t * P:(t + 1) * P], gate_sb[:, k, :], k, KC)
                    last.then_inc(logits, 1)
            pe.wait_ge(sgu_in, 16)

            def shared_up(n):
                half, i = divmod(n, KC)
                if n >= 2:
                    pe.wait_ge(s_act, n - 1)
                for u in range(2):
                    for k in range(KC):
                        last = mm(ps[:, 4 * (n % 2) + 2 + u, :], sgu_sb[:, k, u * SI + i * P:u * SI + (i + 1) * P],
                                  h2T[:, k, half * HALF:(half + 1) * HALF], k, KC)
                last.then_inc(s_gu, 1)

            shared_up(0)
            shared_up(1)
            pe.wait_ge(hot_ready, 1)
            counts = ps[:, 5, 0:(TT + 1) * E]
            T.matmul(counts, before[:], both.rearrange("p t e -> p (t e)"), start=True, stop=False)
            for t in range(TT):
                n = TT - t
                last = T.matmul(ps[:, 5, (t + 1) * E:(TT + 1) * E], ones[:],
                                both[:, t:t + 1, :].to_broadcast([P, n, E]), start=False, stop=(t == TT - 1))
            last.then_inc(ranks, 1)
            pe.wait_ge(pos_ready, 1)
            for n in range(2, 2 * KC):
                shared_up(n)
            pe.wait_ge(sd_in, 16)
            pe.wait_ge(s_act, 2 * KC)
            for t in range(TT):
                if t >= 2:
                    pe.wait_ge(s_added, t - 1)
                for i in range(KC):
                    last = mm(ps[:, t % 2, :], asT[:, i, t * P:(t + 1) * P], sd_sb[:, i, :], i, KC)
                last.then_inc(s_down, 1)
            pe.wait_ge(s_added, TT)

            def transpose_x(j, b, first=False):
                pe.wait_ge(xs_in[b], (j - b) * 8 + 16)
                if not first:
                    pe.wait_ge(xT_ready, j - 1)
                for k in range(KC):
                    last = T.transpose(ps[:, b, k * P:(k + 1) * P], xs[:, b, k * P:(k + 1) * P], ident[:])
                last.then_inc(x_tr, 1)

            def expert_of(j):
                return pe.value_load(tile_ei[0:1, bass.ds(j, 1)], min_val=0, max_val=E - 1)

            def gate_up(j, b, e, first=False):
                pe.wait_ge(xT_ready, j + 1)
                if not first:
                    pe.wait_ge(act_ready, j - 1)
                w = wgu_sb[:, bass.ds(e, 1), :].rearrange("p a n -> p (a n)")
                for k in range(KC):
                    last = mm(ps[:, 2 + b, 0:2 * I], xT[:, b, k * P:(k + 1) * P], w[:, k * 2 * I:(k + 1) * 2 * I], k, KC)
                last.then_inc(gu_mm, 1)

            def transpose_act(j, b, first=False):
                pe.wait_ge(act_ready, j + 1)
                if not first:
                    pe.wait_ge(actT_ready, j - 1)
                T.transpose(ps[:, 4 + b, 0:P], act_sb[:, b, :], ident[:]).then_inc(act_tr, 1)

            def down(j, b, e, first=False):
                pe.wait_ge(actT_ready, j + 1)
                if not first:
                    pe.wait_ge(y_ready, j - 1)
                T.matmul(ps[:, 6 + b, :], actT[:, b, :], wd_sb[:, bass.ds(e, 1), :].rearrange("p a n -> p (a n)"),
                         start=True, stop=True).then_inc(dn_mm, 1)

            pe.wait_ge(tile_ready, 1)
            pe.wait_ge(wgu_in, 16 * E // 2)
            pe.wait_ge(wd_in, 16)
            transpose_x(0, 0, first=True)
            transpose_x(1, 1, first=True)
            gate_up(0, 0, expert_of(0), first=True)
            transpose_act(0, 0, first=True)
            transpose_x(2, 0)
            gate_up(1, 1, expert_of(1), first=True)
            down(0, 0, expert_of(0), first=True)
            transpose_act(1, 1, first=True)
            transpose_x(3, 1)
            gate_up(2, 0, expert_of(2))
            down(1, 1, expert_of(1), first=True)
            with pe.Fori(0, (TILES - 5) // 2) as i:
                for b in range(2):
                    j = i * 2 + (b + 2)
                    transpose_act(j, b)
                    transpose_x(j + 2, b)
                    gate_up(j + 1, 1 - b, expert_of(j + 1))
                    down(j, b, expert_of(j))
            j = TILES - 3
            transpose_act(j, 0)
            transpose_x(j + 2, 0)
            gate_up(j + 1, 1, expert_of(j + 1))
            down(j, 0, expert_of(j))
            transpose_act(j + 1, 1)
            gate_up(j + 2, 0, expert_of(j + 2))
            down(j + 1, 1, expert_of(j + 1))
            transpose_act(j + 2, 0)
            down(j + 2, 0, expert_of(j + 2))


def kernel(**inputs):
    import numpy as np
    import concourse.bacc as bacc
    from concourse.bass_utils import run_bass_kernel_spmd

    a = {k.removeprefix("L0_"): np.asarray(v) for k, v in inputs.items()}

    def chunks(w_t):
        return w_t.reshape(-1, P, w_t.shape[-1]).transpose(1, 0, 2)

    def columns(v):
        return v.reshape(-1, P).T

    arrays = {
        "x": a["attn_hidden_states"].reshape(S, D),
        "wqkv": chunks(np.concatenate([a["attn_q_weight"], a["attn_k_weight"], a["attn_v_weight"]]).T),
        "wo": chunks(a["attn_o_weight"].T),
        "qk_scale": columns(np.concatenate([a["attn_q_scale"], a["attn_k_scale"]])),
        "v_scale": a["attn_v_scale"],
        "o_scale": a["attn_o_scale"],
        "gate": chunks(a["ffn_gate_w"].T),
        "wgu": a["ffn_w_gate_up"].reshape(E, 2 * I, KC, P).transpose(3, 0, 2, 1).reshape(P, E, KC * 2 * I),
        "wd": a["ffn_w_down"].transpose(2, 0, 1),
        "sgu": chunks(a["ffn_shared_w_gate_up"].T),
        "sd": chunks(a["ffn_shared_w_down"].T),
        "c": columns(a["c"][0]),
        "wmod": a["wmod"],
    }
    arrays = {f"in_{k}": np.ascontiguousarray(v) for k, v in arrays.items()}
    nc = bacc.Bacc("TRN2", target_bir_lowering=False, num_devices=1)
    args = [nc.dram_tensor(k, v.shape, mybir.dt.from_np(v.dtype), kind="ExternalInput").ap() for k, v in arrays.items()]
    out = nc.dram_tensor("out", (S, D), mybir.dt.float32, kind="ExternalOutput").ap()
    build(nc, *args, out)
    r = run_bass_kernel_spmd(nc, [arrays], core_ids=[0])
    return r.results[0]["out"].reshape(1, S, D)
```

```python
import concourse.bass as bass
from concourse import mybir
from contextlib import ExitStack

P = 128
S = 1024
D = 512
KC = D // P
TT = S // P
HALF = 512
NH, NKV, DH = 32, 8, 16
G = NH // NKV
KV = NKV * DH
QK_TILES = (D + KV) // P
PARTS = 3
Q_PARTS_OF = (3, 2, 1)
KROWS = sum(Q_PARTS_OF) * DH
AROWS = KROWS + PARTS
E, I, TOPK = 16, 128, 2
SI = 512
TILES = (TOPK * S - E) // P + E
PARTS_OUT = 32 * QK_TILES
LN_EPS = 1e-5
MAX_BANKS = 3
HALF_UNITS = G * (TT // 2) * 2
PERIOD = ([("unit", n) for n in (0, 1)] + [("transpose", 1)] + [("unit", n) for n in range(2, HALF_UNITS + 2)]
          + [("transpose", 0)] + [("unit", n) for n in range(HALF_UNITS + 2, 2 * HALF_UNITS)])
LEAD = 46
assert len(PERIOD) % MAX_BANKS == 0
BIG = 1e6
MOD_COLS = {0: 0, 1: 1, 3: 2, 4: 3}
MOD_ROWS = {2: 0, 5: 1}
Y_RING = 4


def build(nc, x, wqkv, wo, qk_scale, v_scale, o_scale, gate, wgu, wd, sgu, sd, c, wmod, out):
    f32, bf16, i32 = mybir.dt.float32, mybir.dt.bfloat16, mybir.dt.int32
    ALU, ACT, AX = mybir.AluOpType, mybir.ActivationFunctionType, mybir.AxisListType.X
    x_t = x.rearrange("(t p) n -> p t n", p=P)
    out_t = out.rearrange("(t p) n -> p t n", p=P)
    wmod_k = wmod.rearrange("(k p) n -> p k n", p=P)

    ctx = ExitStack()
    with ctx:
        def sb(name, shape, dt=f32):
            return ctx.enter_context(nc.sbuf_tensor(name, shape, dt))

        def sem(name):
            return ctx.enter_context(nc.semaphore(name))

        q_parts_d = nc.dram_tensor("q_parts_d", [NKV, PARTS, DH, G, S], bf16).ap()
        k_parts_d = nc.dram_tensor("k_parts_d", [PARTS, KV, S], bf16).ap()
        o_d = nc.dram_tensor("o_d", [NKV, 2, G, 2 * DH, HALF], f32).ap()
        inv_d = nc.dram_tensor("inv_d", [NKV, 2, G, HALF], f32).ap()
        rows_d = nc.dram_tensor("rows_d", [TILES * P, D], f32).ap()
        moe_d = nc.dram_tensor("moe_d", [TILES * P, D], f32).ap()

        wgu_sb = sb("wgu_sb", [P, E, KC * 2 * I])
        r1 = sb("r1", [P, 12288])
        r2 = sb("r2", [P, TT * D])
        r3 = sb("r3", [P, TT * D])
        rx = sb("rx", [P, TT * D])
        sgu_sb = sb("sgu_sb", [P, KC, 2 * SI])
        r5 = sb("r5", [P, KC * D])
        tmp = sb("tmp", [P, 3, D])
        rows = sb("rows", [P, 3, D])
        c_bc = sb("c_bc", [P, KC, P])
        ident = sb("ident", [P, P])
        identb = sb("identb", [P, P], bf16)
        before = sb("before", [P, P])
        ones = sb("ones", [P, P])
        x_sb = rx[:].rearrange("p (t n) -> p t n", n=D)
        wmod_ring = r1[:, 0:4096].rearrange("p (b k n) -> p b k n", b=2, k=KC)
        signw = r1[:, 4096:7168].rearrange("p (k n) -> p k n", k=KC)
        absw = r1[:, 7168:10240].rearrange("p (k n) -> p k n", k=KC)
        absw_o = r1[:, 10240:12288].rearrange("p (k n) -> p k n", k=KC)
        v_sb = r1[:, 10240:12288].rearrange("p (t h n) -> p t h n", t=TT, h=NKV)
        zq = r1[:, 8704:9728].rearrange("p (b n) -> p b n", b=2)
        parts_st = r1[:, 7168:8704].bitcast(bf16).rearrange("p (b a n) -> p b a n", b=2, a=PARTS)
        signw_o = r5[:].rearrange("p (k n) -> p k n", k=KC)
        xn = r2[:].rearrange("p (t n) -> p t n", n=D)
        hT = r3[:].rearrange("p (k n) -> p k n", k=KC)
        q_ring = r1[:, 0:4096].bitcast(bf16).rearrange("p (b f h n) -> p b f h n", b=2, f=2, h=G)
        k_all = r1[:, 4096:8192].bitcast(bf16).rearrange("p (h n) -> p h n", h=NKV)
        ov = r1[:, 8192:9216].rearrange("p (b n) -> p b n", b=2)
        vg = r1[:, 9216:9728].rearrange("p (b t n) -> p b t n", b=2, t=TT)
        probs = rx[:].rearrange("p (b n) -> p b n", b=4)
        oT = r2[:].rearrange("p (m n) -> p m n", m=KC)
        inv = r3[:].rearrange("p (m n) -> p m n", m=KC)
        wd_sb = r1[:, 0:8192].rearrange("p (e n) -> p e n", e=E)
        h2T = r1[:, 8192:12288].rearrange("p (k n) -> p k n", k=KC)
        h2 = r3[:].rearrange("p (t n) -> p t n", n=D)
        sd_sb = r5[:].rearrange("p (k n) -> p k n", k=KC)
        asT = r2[:].rearrange("p (k n) -> p k n", k=KC)
        xs = r3[:, 0:1024].rearrange("p (b n) -> p b n", b=2)
        xT = r3[:, 1024:2048].rearrange("p (b n) -> p b n", b=2)
        sg = r3[:, 2048:2304].rearrange("p (b n) -> p b n", b=2)
        act_sb = r3[:, 2304:2560].rearrange("p (b n) -> p b n", b=2)
        actT = r3[:, 2560:2816].rearrange("p (b n) -> p b n", b=2)
        y_sb = r3[:, 2816:3840].rearrange("p (b n) -> p b n", b=2)
        y_in = r1[:, 8192:12288].rearrange("p (b k n) -> p b k n", b=Y_RING, k=TOPK)

        scol = sb("scol", [P, QK_TILES])
        qk_sc = sb("qk_sc", [P, QK_TILES])
        v_sc = sb("v_sc", [P, KV])
        c_sb = sb("c_sb", [P, KC])
        c_si = sb("c_si", [P, KC])
        mcol = sb("mcol", [P, 4, KC])
        stats = sb("stats", [P, TT, 6])
        mv = sb("mv", [P, TT, 2])
        rstd = sb("rstd", [P, TT])
        shift = sb("shift", [P, TT])
        gate_sb = sb("gate_sb", [P, KC, E])
        mxh = sb("mxh", [P, 2, HALF_UNITS])
        rt = sb("rt", [P, 448])
        mxc = rt[:, 0:16]
        mrest = rt[:, 16:48].rearrange("p (a n) -> p a n", a=2)
        mcols = rt[:, 48:72].bitcast(bf16).rearrange("p (a n) -> p a n", a=PARTS)
        mparts = rt[0:PARTS * 16, 72:200].bitcast(bf16).rearrange("p (b n) -> p b n", b=2)
        sums = rt[:, 200:232].rearrange("p (b n) -> p b n", b=2)
        c_flat = c_bc[:].rearrange("p k n -> p (k n)")
        lg = c_flat[:, 0:128].rearrange("p (t e) -> p t e", e=E)
        pr = c_flat[:, 128:256].rearrange("p (t e) -> p t e", e=E)
        both = c_flat[:, 256:400].rearrange("p (t e) -> p t e", e=E)
        cand = rt[:, 0:128].rearrange("p (t e) -> p t e", e=E)
        hot = rt[:, 128:416].rearrange("p (k t e) -> p k t e", k=TOPK, e=E)
        col = sb("col", [P, 6, TT])
        wcol = sb("wcol", [P, TOPK, TT])
        rev = sb("rev", [P, E])
        pos_f = sb("pos_f", [P, TOPK, TT])
        pos = sb("pos", [P, TOPK, TT], i32)
        cnt_i = c_flat[:, 400:432].bitcast(i32).rearrange("p (a e) -> p a e", e=E)
        cnt = sb("cnt", [P, 4, E])
        tile_no = rt[0:1, 416:416 + TILES]
        tile_cmp = tmp[0:1, 2, 0:TILES * E].rearrange("p (j e) -> p j e", e=E)
        tile_e = mxh[0:1, :, 0:TILES]
        tile_ei = sb("tile_ei", [1, TILES], i32)

        ps = ctx.enter_context(nc.psum_tensor("ps", [P, 8, HALF], f32))

        w_in, wo_in, small_in, c_in = (sem(n) for n in ("w_in", "wo_in", "small_in", "c_in"))
        x_in = [sem(f"x_in{n}") for n in range(TT // 2)]
        wmod_in = [sem("wmod_in0"), sem("wmod_in1")]
        consts, abs_ready, sign_ready, c_ready = (sem(n) for n in ("consts", "abs_ready", "sign_ready", "c_ready"))
        scales_ready, w_sums, mod_mm, mod_read = sem("scales_ready"), sem("w_sums"), sem("mod_mm"), sem("mod_read")
        var_ready, std_ready, xn_ready, norm_ready = (sem(n) for n in ("var_ready", "std_ready", "xn_ready", "norm_ready"))
        h_t, hT_ready, qkv_mm, qkv_read = sem("h_t"), sem("hT_ready"), sem("qkv_mm"), sem("qkv_read")
        parts_ready, v_ready, v_ones = sem("parts_ready"), sem("v_ready"), sem("v_ones")
        parts_out = [sem("parts_out0"), sem("parts_out1")]
        k_in = sem("k_in")
        q_in = [[sem(f"q_in{b}{h}") for h in range(2)] for b in range(2)]
        max_row_in = [sem("max_row_in0"), sem("max_row_in1")]
        k_ones, identb_ready = sem("k_ones"), sem("identb_ready")
        max_slot, max_read = sem("max_slot"), sem("max_read")
        max_cols, max_parts = sem("max_cols"), sem("max_parts")
        scores, probs_ready, pv_done = sem("scores"), sem("probs_ready"), sem("pv_done")
        o_read, vg_ready = sem("o_read"), sem("vg_ready")
        o_out = [sem("o_out0"), sem("o_out1")]
        o_in = [[sem(f"o_in{b}{h}") for h in range(2)] for b in range(2)]
        sums_in = [sem("sums_in0"), sem("sums_in1")]
        inv_out = [sem("inv_out0"), sem("inv_out1")]
        inv_ready = sem("inv_ready")
        wgu_in, sgu_in, wd_in, sd_in = sem("wgu_in"), sem("sgu_in"), sem("wd_in"), sem("sd_in")
        gate_in, x2_in, zero_ready, zero_out = sem("gate_in"), sem("x2_in"), sem("zero_ready"), sem("zero_out")
        oT_ready, o_mm, o_mm_read, z_ready = sem("oT_ready"), sem("o_mm"), sem("o_mm_read"), sem("z_ready")
        z_scaled, x_added = sem("z_scaled"), sem("x_added")
        h2_ready, h2_t, h2T_ready, logits = sem("h2_ready"), sem("h2_t"), sem("h2T_ready"), sem("logits")
        shift_ready, exp_ready, hot_ready, ranks = sem("shift_ready"), sem("exp_ready"), sem("hot_ready"), sem("ranks")
        pos_ready, rows_out, tile_ready = sem("pos_ready"), sem("rows_out"), sem("tile_ready")
        s_gu, s_silu, s_act, s_down = (sem(n) for n in ("s_gu", "s_silu", "s_act", "s_down"))
        xs_in = [sem("xs_in0"), sem("xs_in1")]
        x_tr, xT_ready, gu_mm, sg_ready = sem("x_tr"), sem("xT_ready"), sem("gu_mm"), sem("sg_ready")
        act_ready, act_tr, actT_ready = sem("act_ready"), sem("act_tr"), sem("actT_ready")
        dn_mm, y_ready = sem("dn_mm"), sem("y_ready")
        y_out = [sem("y_out0"), sem("y_out1")]
        got_y = [sem(f"got_y{n}") for n in range(Y_RING)]
        y0_ready = sem("y0_ready")
        out_ready, out_done = sem("out_ready"), sem("out_done")
        dve_chain, act_chain = sem("dve_chain"), sem("act_chain")

        block = ctx.enter_context(nc.Block())

        def slots_before(g, n):
            if isinstance(g, int) and g == 0:
                return n - (n > 2)
            return g * len(PERIOD) + (n - 1)

        @block.sync
        def _(sp):
            sp.dma_start(c_sb[:], c).then_inc(c_in, 16)
            for h in range(2):
                for t in range(4 * h, 4 * h + 4, 2):
                    sp.dma_start(x_sb[:, t:t + 2, :], x_t[:, t:t + 2, :]).then_inc(x_in[t // 2], 16)
                if h == 0:
                    sp.dma_start(signw, wqkv).then_inc(w_in, 16)
            for j in range(2):
                sp.dma_start(wmod_ring[:, j], wmod_k[:, :, j * D:(j + 1) * D]).then_inc(wmod_in[j], 16)
            sp.dma_start(qk_sc[:], qk_scale).then_inc(small_in, 16)
            sp.dma_start(v_sc[:], v_scale.partition_broadcast(P)).then_inc(small_in, 16)
            sp.dma_start(rows[:, 2, :], o_scale.partition_broadcast(P)).then_inc(small_in, 16)
            sp.dma_start(signw_o, wo).then_inc(wo_in, 16)
            sp.dma_start(gate_sb[:], gate).then_inc(gate_in, 16)
            for j in range(2, 4):
                sp.wait_ge(mod_mm, j - 1)
                sp.dma_start(wmod_ring[:, j % 2], wmod_k[:, :, j * D:(j + 1) * D]).then_inc(wmod_in[j % 2], 16)
            for n in range(2 * QK_TILES):
                m, half = divmod(n, 2)
                cols = slice(half * HALF, (half + 1) * HALF)
                sp.wait_ge(parts_ready, n + 1)
                for b in range(2):
                    r = slice(b * G * DH, (b + 1) * G * DH)
                    dst = (k_parts_d[:, r, cols].rearrange("a p n -> p a n") if m == 0 else
                           q_parts_d[2 * (m - 1) + b, :, :, :, cols].rearrange("a d h n -> (d h) a n"))
                    sp.dma_start(dst, parts_st[r, n % 2]).then_inc(parts_out[n % 2], 16)
            for b in range(2):
                sp.wait_ge(parts_out[b], PARTS_OUT)

            def load_q(g, par, half):
                cols = slice(half * HALF, (half + 1) * HALF)
                row = 0
                for n in Q_PARTS_OF:
                    sp.dma_start(q_ring[row:row + n * DH, par, half],
                                 q_parts_d[bass.ds(g, 1), 0:n, :, :, cols].rearrange("g a d h n -> (g a d) h n"))\
                        .then_inc(q_in[par][half], 16)
                    row += n * DH

            def load_max(g, par, half):
                sp.wait_ge(max_parts, g * 2 + half + 1)
                sp.dma_start(q_ring[KROWS:AROWS, par, half].rearrange("p h n -> p (h n)"), mparts[:, half, :])\
                    .then_inc(max_row_in[half], 16)

            def store_o(g, half):
                sp.wait_ge(o_read, g * 2 + half + 1)
                sp.dma_start(o_d[bass.ds(g, 1), half].rearrange("g h r n -> (g h r) n"), ov[:, half, :])\
                    .then_inc(o_out[half], 16)

            def chunk_of(g, par):
                return g // 2 if isinstance(g, int) else (g - par) // 2

            def load_o(g, par, half):
                sp.wait_ge(o_out[half], g * 16 + 16)
                rows64 = slice(par * G * DH, (par + 1) * G * DH)
                sp.dma_start(oT[rows64, bass.ds(chunk_of(g, par), 1), half * HALF:(half + 1) * HALF]
                             .rearrange("p a n -> p (a n)"),
                             o_d[bass.ds(g, 1), half, :, 0:DH, :].rearrange("g h d n -> (g h) d n"))\
                    .then_inc(o_in[par][half], 16)
                sp.dma_start(sums[:, half, :],
                             o_d[bass.ds(g, 1), half, :, DH, :].rearrange("g h (c n) -> (g h) c n", n=DH))\
                    .then_inc(sums_in[half], 16)

            def load_inv(g, par, half):
                sp.wait_ge(inv_ready, g * 2 + half + 1)
                sp.dma_start(inv_d[bass.ds(g, 1), half].rearrange("g h (c n) -> (g h c) n", n=DH), sums[:, half, :])\
                    .then_inc(inv_out[half], 16)
                sp.wait_ge(mod_mm, 6)
                sp.wait_ge(inv_out[half], g * 16 + 16)
                rows64 = slice(par * G * DH, (par + 1) * G * DH)
                sp.dma_start(inv[rows64, bass.ds(chunk_of(g, par), 1), half * HALF:(half + 1) * HALF]
                             .rearrange("p a n -> p (a n)"),
                             inv_d[bass.ds(g, 1), half].rearrange("g h n -> (g h) n").unsqueeze(1)
                             .to_broadcast([G, DH, HALF])).then_inc(o_in[par][half], 16)

            sp.wait_ge(mod_mm, 6)
            row = 0
            for part, n in enumerate(Q_PARTS_OF):
                for _ in range(n):
                    sp.dma_start(k_all[row:row + DH], k_parts_d[part].rearrange("(h d) n -> d h n", d=DH))\
                        .then_inc(k_in, 16)
                    row += DH
            for g in range(2):
                for half in range(2):
                    load_q(g, g, half)
            load_max(0, 0, 0)

            def group(g, par, first=False, last=False, loads=True):
                if not first:
                    store_o(g - 1, 1)
                    load_o(g - 1, 1 - par, 1)
                load_max(g, par, 1)
                if not first:
                    load_inv(g - 1, 1 - par, 1)
                if loads:
                    sp.wait_ge(scores, g * 32 + 16)
                    load_q(g + 2, par, 0)
                store_o(g, 0)
                load_o(g, par, 0)
                if not last:
                    load_max(g + 1, 1 - par, 0)
                load_inv(g, par, 0)
                if loads:
                    sp.wait_ge(scores, g * 32 + 32)
                    load_q(g + 2, par, 1)

            group(0, 0, first=True)
            with sp.Fori(0, 2) as i:
                group(i * 2 + 1, 1)
                group(i * 2 + 2, 0)
            group(5, 1)
            group(6, 0, loads=False)
            group(7, 1, last=True, loads=False)
            store_o(7, 1)
            load_o(7, 1, 1)
            load_inv(7, 1, 1)

            sp.wait_ge(pv_done, NKV * 16)
            for h in range(2):
                sp.dma_start(x_sb[:, 4 * h:4 * h + 4, :], x_t[:, 4 * h:4 * h + 4, :]).then_inc(x2_in, 16)
            sp.dma_start(wd_sb, wd).then_inc(wd_in, 16)
            sp.wait_ge(o_mm, TT)
            sp.dma_start(sd_sb, sd).then_inc(sd_in, 16)

            sp.wait_ge(rows_out, 16 * TOPK * TT)

            def load_rows(j, b):
                sp.dma_start(xs[:, b, :], rows_d[bass.ds(j * P, P), :]).then_inc(xs_in[b], 16)

            load_rows(0, 0)
            load_rows(1, 1)
            with sp.Fori(0, (TILES - 3) // 2) as i:
                for b in range(2):
                    sp.wait_ge(x_tr, i * 2 + b + 1)
                    load_rows(i * 2 + b + 2, b)
            j = TILES - 3
            sp.wait_ge(x_tr, j + 1)
            load_rows(j + 2, 0)
            for t in range(TT):
                sp.wait_ge(out_ready, t + 1)
                sp.dma_start(out_t[:, t, :], x_sb[:, t, :]).then_inc(out_done, 16)
            sp.wait_ge(out_done, 16 * TT)

        @block.gpsimd
        def _(pool):
            nc.gpsimd.memset(ident[:], 0.0).then_inc(consts, 1)
            nc.gpsimd.memset(before[:], 1.0).then_inc(consts, 1)
            nc.gpsimd.memset(ones[:], 1.0).then_inc(consts, 1)
            nc.gpsimd.memset(wgu_sb[:, 0, 0:D], 0.0).then_inc(zero_ready, 1)
            pool.wait_ge(consts, 3)
            nc.gpsimd.affine_select(out=ident[:], in_=ident[:], compare_op=ALU.not_equal, fill=1.0, base=0,
                                    pattern=[[-1, P]], channel_multiplier=1).then_inc(consts, 1)
            nc.gpsimd.affine_select(out=before[:], in_=before[:], compare_op=ALU.is_gt, fill=0.0, base=0,
                                    pattern=[[1, P]], channel_multiplier=-1).then_inc(consts, 1)
            nc.gpsimd.iota(rev[:], pattern=[[-1, E]], base=E, channel_multiplier=0,
                           allow_small_or_imprecise_dtypes=True).then_inc(consts, 1)
            nc.gpsimd.iota(tile_no, pattern=[[1, TILES]], base=0, channel_multiplier=0,
                           allow_small_or_imprecise_dtypes=True).then_inc(consts, 1)
            pool.wait_ge(zero_ready, 1)
            pool.wait_ge(consts, 6)
            nc.gpsimd.tensor_copy(identb[:], ident[:]).then_inc(identb_ready, 1)
            pool.wait_ge(w_sums, 2)
            pool.wait_ge(identb_ready, 1)
            nc.gpsimd.memset(v_sb[:, :, :, DH:2 * DH], 1.0).then_inc(v_ones, 1)
            pool.dma_start(rows_d.rearrange("(t p) n -> p t n", p=P),
                           wgu_sb[:, 0:1, 0:D].to_broadcast([P, TILES, D])).then_inc(zero_out, 16)
            for b in range(2):
                pool.wait_ge(parts_out[b], PARTS_OUT)
            pool.wait_ge(mod_mm, 6)
            pool.wait_ge(v_ones, 1)
            nc.gpsimd.memset(k_all[KROWS:AROWS, :, :], 1.0).then_inc(k_ones, 1)
            pool.dma_start(sgu_sb[:], sgu).then_inc(sgu_in, 16)
            pool.wait_ge(v_ready, 2)
            pool.wait_ge(k_ones, 1)
            pool.wait_ge(zero_out, 16)

            def group_v(g, par):
                nc.gpsimd.tensor_copy(vg[:, par], v_sb[:, :, bass.ds(g, 1), :].rearrange("p t a n -> p t (a n)"))\
                    .then_inc(vg_ready, 1)
                pool.dma_start(wgu_sb[:, bass.ds(g * 2, 2), :], wgu[:, bass.ds(g * 2, 2), :]).then_inc(wgu_in, 16)

            def divide(g, par):
                m = g // 2 if isinstance(g, int) else (g - par) // 2
                rows64 = slice(par * G * DH, (par + 1) * G * DH)
                for half in range(2):
                    if half == 0:
                        pool.wait_ge(vg_ready, min(g + 2, NKV) if isinstance(g, int) else g + 2)
                    else:
                        pool.wait_ge(oT_ready, g * 2 + 1)
                    pool.wait_ge(o_in[par][half], g // 2 * 32 + 32 if isinstance(g, int) else (g - par) * 16 + 32)
                    o = oT[rows64, bass.ds(m, 1), half * HALF:(half + 1) * HALF].rearrange("p a n -> p (a n)")
                    nc.gpsimd.tensor_tensor(o, o, inv[rows64, bass.ds(m, 1), half * HALF:(half + 1) * HALF]
                                            .rearrange("p a n -> p (a n)"), ALU.mult).then_inc(oT_ready, 1)

            group_v(0, 0)
            group_v(1, 1)
            with pool.Fori(0, KC - 1) as i:
                for par in range(2):
                    divide(i * 2 + par, par)
                    pool.wait_ge(pv_done, i * 32 + (par + 1) * 16)
                    pool.wait_ge(oT_ready, i * 4 + (2 * par + 2))
                    group_v(i * 2 + (par + 2), par)
            divide(NKV - 2, 0)
            pool.wait_ge(oT_ready, 2 * NKV - 2)
            divide(NKV - 1, 1)
            for t in range(TT):
                pool.wait_ge(z_ready, t + 1)
                if t == 0:
                    pool.wait_ge(oT_ready, 2 * NKV)
                    pool.wait_ge(x2_in, 32)
                else:
                    pool.wait_ge(x_added, t)
                nc.gpsimd.tensor_tensor(h2[:, t, :], h2[:, t, :], rows[:, 0, :], ALU.mult).then_inc(z_scaled, 1)
                pool.wait_ge(z_scaled, t + 1)
                nc.gpsimd.tensor_tensor(x_sb[:, t, :], x_sb[:, t, :], h2[:, t, :], ALU.add).then_inc(x_added, 1)
            pool.wait_ge(pos_ready, 1)
            pool.wait_ge(h2_ready, TT)
            for t in range(TT):
                for k in range(TOPK):
                    nc.gpsimd.indirect_dma_start(
                        out=rows_d, out_offset=bass.IndirectOffsetOnAxis(ap=pos[:, k, t:t + 1], axis=0),
                        in_=h2[:, t, :], in_offset=None).then_inc(rows_out, 16)
            pool.wait_ge(y_out[0], 16 * ((TILES + 1) // 2))
            pool.wait_ge(y_out[1], 16 * (TILES // 2))
            for t in range(TT):
                if t >= Y_RING:
                    pool.wait_ge(out_ready, t - Y_RING + 1)
                for k in range(TOPK):
                    nc.gpsimd.indirect_dma_start(
                        out=y_in[:, t % Y_RING, k, :], out_offset=None, in_=moe_d,
                        in_offset=bass.IndirectOffsetOnAxis(ap=pos[:, k, t:t + 1], axis=0))\
                        .then_inc(got_y[t % Y_RING], 16)

        @block.scalar
        def _(act):
            act.wait_ge(c_in, 16)
            nc.scalar.activation(c_si[:], c_sb[:], ACT.Silu).then_inc(c_ready, 1)
            act.wait_ge(c_ready, 1)
            nc.scalar.activation(c_bc[:], c_si[:].unsqueeze(2).to_broadcast([P, KC, P]), ACT.Copy)\
                .then_inc(c_ready, 1)
            for h in range(2):
                act.wait_ge(var_ready, h + 1)
                nc.scalar.activation(rstd[:, 4 * h:4 * h + 4], rstd[:, 4 * h:4 * h + 4], ACT.Sqrt)\
                    .then_inc(std_ready, 1)
                if h == 0:
                    act.wait_ge(w_in, 16)
                    nc.scalar.activation(absw, signw, ACT.Abs).then_inc(abs_ready, 1)
                    act.wait_ge(abs_ready, 1)
                    nc.scalar.activation(signw, signw, ACT.Sign).then_inc(sign_ready, 1)
            act.wait_ge(wo_in, 16)
            nc.scalar.activation(absw_o, signw_o, ACT.Abs).then_inc(abs_ready, 1)
            act.wait_ge(abs_ready, 2)
            nc.scalar.activation(signw_o, signw_o, ACT.Sign).then_inc(sign_ready, 1)

            for n in range(2 * QK_TILES):
                act.wait_ge(qkv_mm, n + 1)
                if n == 0:
                    act.wait_ge(scales_ready, 1)
                if n >= 2:
                    act.wait_ge(parts_ready, n - 1)
                nc.scalar.activation(zq[:, n % 2, :], ps[:, 2 + n % 2, :], ACT.Copy,
                                     scale=scol[:, n // 2:n // 2 + 1]).then_inc(qkv_read, 1)
            for j in range(4, 6):
                act.wait_ge(mod_mm, j - 1)
                act.dma_start(wmod_ring[:, j % 2], wmod_k[:, :, j * D:(j + 1) * D]).then_inc(wmod_in[j % 2], 16)

            def read_o(g, half):
                act.wait_ge(pv_done, g * 16 + 8 * half + 8)
                if not (isinstance(g, int) and g == 0):
                    act.wait_ge(o_out[half], g * 16)
                nc.scalar.activation(ov[:, half, :], ps[:, 4, :], ACT.Copy).then_inc(o_read, 1)

            def group(g, first=False):
                for s in range(16):
                    for i in range(2):
                        act.wait_ge(scores, g * 32 + (2 * s + i + 1))
                        if i == 0 and not (first and s < 2):
                            act.wait_ge(pv_done, g * 16 + (s - 1))
                        nc.scalar.activation(probs[:, (2 * s + i) % 4, :],
                                             ps[:, 2 * i:2 * i + 2, :].rearrange("p b n -> p (b n)"),
                                             ACT.Exp, scale=DH ** -0.5).then_inc(probs_ready, 1)
                    if s == 0 and not first:
                        read_o(g - 1, 1)
                    if s == 8:
                        read_o(g, 0)

            group(0, first=True)
            with act.Fori(0, NKV - 1) as i:
                group(i + 1)
            read_o(NKV - 1, 1)

            def deviation(t):
                act.wait_ge(var_ready, 3 + t)
                nc.scalar.activation(rstd[:, t:t + 1], rstd[:, t:t + 1], ACT.Sqrt).then_inc(std_ready, 1)

            def normalise(t):
                act.wait_ge(norm_ready, t + 1)
                nc.scalar.activation(h2[:, t, :], x_sb[:, t, :], ACT.Identity, bias=shift[:, t:t + 1],
                                     scale=rstd[:, t:t + 1]).then_inc(h2_ready, 1)

            def modulate(half):
                for k in range(KC):
                    n = half * KC + k
                    act.wait_ge(h2_t, n + 1)
                    nc.scalar.activation(h2T[:, k, half * HALF:(half + 1) * HALF], ps[:, n % 2, :], ACT.Identity,
                                         bias=mcol[:, 2, k:k + 1], scale=mcol[:, 3, k:k + 1]).then_inc(h2T_ready, 1)

            def shared_silu(n):
                act.wait_ge(s_gu, n + 1)
                if n >= 2:
                    act.wait_ge(s_act, n - 1)
                nc.scalar.activation(tmp[:, n % 2, :], ps[:, 4 * (n % 2) + 2, :], ACT.Silu).then_inc(s_silu, 1)

            for t in range(TT):
                deviation(t)
                normalise(t)
            modulate(0)
            shared_silu(0)
            modulate(1)
            act.wait_ge(shift_ready, 1)
            nc.scalar.activation(pr, lg, ACT.Exp).then_inc(exp_ready, 1)
            for n in range(1, 2 * KC):
                shared_silu(n)

            def silu(j, b, first=False):
                act.wait_ge(gu_mm, j + 1)
                if not first:
                    act.wait_ge(act_ready, j - 1)
                nc.scalar.activation(sg[:, b, :], ps[:, 2 + b, 0:I], ACT.Silu).then_inc(sg_ready, 1)

            def copy_act(j, b, first=False):
                act.wait_ge(act_tr, j + 1)
                if not first:
                    act.wait_ge(dn_mm, j - 1)
                nc.scalar.activation(actT[:, b, :], ps[:, 4 + b, 0:P], ACT.Copy).then_inc(actT_ready, 1)

            def copy_y(j, b, first=False):
                act.wait_ge(dn_mm, j + 1)
                if not first:
                    act.wait_ge(y_out[b], (j - b) * 8)
                nc.scalar.activation(y_sb[:, b, :], ps[:, 6 + b, :], ACT.Copy).then_inc(y_ready, 1)
                act.wait_ge(y_ready, j + 1)
                act.dma_start(moe_d[bass.ds(j * P, P), :], y_sb[:, b, :]).then_inc(y_out[b], 16)

            silu(0, 0, first=True)
            copy_act(0, 0, first=True)
            silu(1, 1, first=True)
            copy_y(0, 0, first=True)
            copy_act(1, 1, first=True)
            silu(2, 0)
            copy_y(1, 1, first=True)
            with act.Fori(0, (TILES - 3) // 2) as i:
                for b in range(2):
                    j = i * 2 + (b + 2)
                    copy_act(j, b)
                    silu(j + 1, 1 - b)
                    copy_y(j, b)
            j = TILES - 1
            copy_act(j, 0)
            copy_y(j, 0)
            for t in range(TT):
                act.wait_ge(got_y[t % Y_RING], 32 * (t // Y_RING + 1))
                y0 = y_in[:, t % Y_RING, 0, :]
                nc.scalar.activation(y0, y0, ACT.Copy, scale=wcol[:, 0, t:t + 1]).then_inc(y0_ready, 1)

        @block.vector
        def _(dve):
            linked = [0]

            def link(ins):
                linked[0] += 1
                ins.then_inc(dve_chain, 1)
                dve.wait_ge(dve_chain, linked[0])

            V = nc.vector

            def nan_to_num(v, a, mask):
                V.tensor_scalar(mask, v, 0.0, 0.0, ALU.mult, ALU.not_equal)
                link(V.tensor_scalar(a, v, BIG, -BIG, ALU.min, ALU.max))
                link(V.scalar_tensor_tensor(out=a, in0=v, scalar=0.0, in1=a, op0=ALU.max, op1=ALU.min))
                link(V.copy_predicated(v, mask, a))

            z, za, zm = tmp[:, 0, :], tmp[:, 1, :], tmp[:, 2, :].bitcast(i32)

            def norm_stats(t):
                link(V.bn_stats(stats[:, t, :], x_sb[:, t, :]))
                link(V.bn_aggr(mv[:, t, :], stats[:, t, :]))

            for h in range(2):
                for t in range(4 * h, 4 * h + 4):
                    dve.wait_ge(x_in[t // 2], 16)
                    norm_stats(t)
                V.tensor_scalar(rstd[:, 4 * h:4 * h + 4], mv[:, 4 * h:4 * h + 4, 1], LN_EPS, None, ALU.add)\
                    .then_inc(var_ready, 1)
                dve.wait_ge(std_ready, h + 1)
                link(V.reciprocal(rstd[:, 4 * h:4 * h + 4], rstd[:, 4 * h:4 * h + 4]))
                for t in range(4 * h, 4 * h + 4):
                    V.tensor_scalar(xn[:, t, :], x_sb[:, t, :], mv[:, t, 0:1], rstd[:, t:t + 1],
                                    ALU.subtract, ALU.mult).then_inc(xn_ready, 1)
            dve.wait_ge(w_sums, 1)
            dve.wait_ge(small_in, 48)
            link(V.tensor_scalar(scol[:], ps[:, 0, 0:QK_TILES], 1.0 / D, 1e-8, ALU.mult, ALU.max))
            link(V.tensor_scalar(za[:, 0:KV], ps[:, 1, 0:KV], 1.0 / D, 1e-8, ALU.mult, ALU.max))
            link(V.tensor_tensor(v_sc[:], za[:, 0:KV], v_sc[:], ALU.mult))
            V.tensor_tensor(scol[:], scol[:], qk_sc[:], ALU.mult).then_inc(scales_ready, 1)
            dve.wait_ge(mod_mm, 2)
            for j in range(2):
                link(V.tensor_scalar(mcol[:, j, :], ps[:, 3, KC * j:KC * j + KC], float(j), None, ALU.add))
            for n in range(2 * KC):
                half, k = divmod(n, KC)
                dve.wait_ge(h_t, n + 1)
                V.tensor_scalar(hT[:, k, half * HALF:(half + 1) * HALF], ps[:, n % 2, :],
                                mcol[:, 1, k:k + 1], mcol[:, 0, k:k + 1], ALU.mult, ALU.add).then_inc(hT_ready, 1)
            for n in range(2 * QK_TILES):
                v = zq[:, n % 2, :]
                dve.wait_ge(qkv_read, n + 1)
                nan_to_num(v, za, zm)
                if n >= 2:
                    dve.wait_ge(parts_out[n % 2], 32 * (n // 2))
                st = parts_st[:, n % 2]
                link(V.tensor_copy(st[:, 0, :], v))
                link(V.tensor_tensor(v, v, st[:, 0, :], ALU.subtract))
                link(V.tensor_copy(st[:, 1, :], v))
                V.tensor_tensor(st[:, 2, :], v, st[:, 1, :], ALU.subtract).then_inc(parts_ready, 1)
                dve.wait_ge(parts_ready, n + 1)
            dve.wait_ge(w_sums, 2)
            for half in range(2):
                u = 2 * QK_TILES + half
                dve.wait_ge(qkv_mm, u + 1)
                link(V.tensor_tensor(z.rearrange("p (t n) -> p t n", n=KV),
                                     ps[:, 2 + u % 2, :].rearrange("p (t n) -> p t n", n=KV),
                                     v_sc[:].unsqueeze(1).to_broadcast([P, 4, KV]), ALU.mult))
                nan_to_num(z, za, zm)
                V.tensor_copy(v_sb[:, 4 * half:4 * half + 4, :, 0:DH],
                              z.rearrange("p (t h n) -> p t h n", t=4, h=NKV)).then_inc(v_ready, 1)
                dve.wait_ge(v_ready, half + 1)
            dve.wait_ge(w_sums, 2)
            link(V.tensor_scalar(za, ps[:, 4, :], 1.0 / D, 1e-8, ALU.mult, ALU.max))
            link(V.tensor_tensor(rows[:, 2, :], za, rows[:, 2, :], ALU.mult))
            for j in range(2, 6):
                dve.wait_ge(mod_mm, j + 1)
                src = ps[:, 5 + j % 2, :]
                if j in MOD_ROWS:
                    link(V.tensor_scalar(z, src, 0.0, 2.0, ALU.is_ge, ALU.mult))
                    link(V.scalar_tensor_tensor(out=za, in0=z, scalar=1.0, in1=src, op0=ALU.subtract, op1=ALU.mult))
                    link(V.tensor_scalar(za, za, 0.25, None, ALU.max))
                    ins = V.scalar_tensor_tensor(out=rows[:, MOD_ROWS[j], :], in0=z, scalar=1.0, in1=za,
                                                 op0=ALU.subtract, op1=ALU.mult)
                else:
                    ins = V.tensor_scalar(mcol[:, MOD_COLS[j], :], src[:, 0:KC], float(j == 4), None, ALU.add)
                ins.then_inc(mod_read, 1)
                dve.wait_ge(mod_read, j - 1)

            def period(g, first=False, divisors=(1, 0), wait_sent=True, chain=None):
                for n, (kind, u) in enumerate(PERIOD):
                    if first and (kind, u) == ("transpose", 1):
                        continue
                    dve.wait_ge(max_slot, slots_before(g, n) + 1)
                    bank = ps[:, 5 + n % MAX_BANKS, :]
                    if kind == "unit":
                        half, u = divmod(u, HALF_UNITS)
                        V.reduce_max(mxh[:, half, u:u + 1], bank, AX).then_inc(max_read, 1)
                        if u == HALF_UNITS - 1:
                            dve.wait_ge(max_read, slots_before(g, n) + 1)
                            split_max(g, half, chain)
                    else:
                        read_parts(g - 1 if u else g, u, slots_before(g, n), bank, wait_sent)
                    if n == 4 and 1 in divisors:
                        reciprocals(g - 2, 1)
                    if n == 37 and 0 in divisors:
                        reciprocals(g - 1, 0)

            def split_max(g, half, chain):
                def step(k, ins):
                    ins.then_inc(dve_chain, 1)
                    dve.wait_ge(dve_chain, g * 8 + (chain + 4 * half + k))

                if half or not isinstance(g, int) or g > 0:
                    dve.wait_ge(max_parts, g * 2 + half)
                pairs = mxh[:, half, :].rearrange("p (n k) -> p n k", k=2)
                step(1, V.tensor_tensor(mxc, pairs[:, :, 0], pairs[:, :, 1], ALU.max))
                step(2, V.tensor_scalar(mcols[:, 0, :], mxc, -1.0, None, ALU.mult))
                step(3, V.scalar_tensor_tensor(out=mrest[:, 0, :], in0=mxc, scalar=-1.0, in1=mcols[:, 0, :],
                                               op0=ALU.mult, op1=ALU.subtract))
                step(4, V.tensor_copy(mcols[:, 1, :], mrest[:, 0, :]))
                V.tensor_tensor(mcols[:, 2, :], mrest[:, 0, :], mcols[:, 1, :], ALU.subtract).then_inc(max_cols, 1)

            def read_parts(g, half, before_it, bank, wait_sent):
                if wait_sent:
                    dve.wait_ge(max_row_in[half], g * 16)
                V.tensor_copy(mparts[:, half, :], bank[0:PARTS * 16, 0:P]).then_inc(max_parts, 1)
                dve.wait_ge(max_parts, g * 2 + half + 1)
                V.sem_inc(max_read, 1)

            def reciprocals(g, half):
                dve.wait_ge(sums_in[half], g * 16 + 16)
                V.reciprocal(sums[:, half, :], sums[:, half, :]).then_inc(inv_ready, 1)

            base = linked[0]
            period(0, first=True, divisors=(), wait_sent=False, chain=base)
            period(1, divisors=(0,), wait_sent=False, chain=base)
            with dve.Fori(2, NKV) as g:
                period(g, chain=base)
            dve.wait_ge(max_slot, slots_before(NKV, 0) + 1)
            read_parts(NKV - 1, 1, slots_before(NKV, 2), ps[:, 5 + 2, :], True)
            reciprocals(NKV - 2, 1)
            reciprocals(NKV - 1, 0)
            reciprocals(NKV - 1, 1)
            linked[0] = base + 8 * NKV

            def scale_o(t):
                if t == 0:
                    dve.wait_ge(oT_ready, 2 * NKV - 1)
                if t == TT // 2:
                    dve.wait_ge(oT_ready, 2 * NKV)
                z = h2[:, t, :]
                dve.wait_ge(o_mm, t + 1)
                V.tensor_tensor(z, ps[:, t % 4, :], rows[:, 2, :], ALU.mult).then_inc(o_mm_read, 1)
                dve.wait_ge(o_mm_read, t + 1)
                if t >= 2:
                    norm(t - 2)
                nan_to_num(z, za, zm)
                V.sem_inc(z_ready, 1)

            def variance(t):
                dve.wait_ge(x_added, t + 1)
                norm_stats(t)
                V.tensor_scalar(rstd[:, t:t + 1], mv[:, t, 1:2], LN_EPS, None, ALU.add).then_inc(var_ready, 1)

            def norm(t):
                dve.wait_ge(std_ready, 3 + t)
                link(V.reciprocal(rstd[:, t:t + 1], rstd[:, t:t + 1]))
                V.scalar_tensor_tensor(out=shift[:, t:t + 1], in0=mv[:, t, 0:1], scalar=-1.0, in1=rstd[:, t:t + 1],
                                       op0=ALU.mult, op1=ALU.mult).then_inc(norm_ready, 1)

            for t in range(TT):
                scale_o(t)
                if t > 0:
                    variance(t - 1)
            norm(TT - 2)
            variance(TT - 1)
            norm(TT - 1)

            def shared_mult(n):
                half, i = divmod(n, KC)
                dve.wait_ge(s_silu, n + 1)
                V.tensor_tensor(asT[:, i, half * HALF:(half + 1) * HALF], tmp[:, n % 2, :],
                                ps[:, 4 * (n % 2) + 3, :], ALU.mult).then_inc(s_act, 1)

            shared_mult(0)
            dve.wait_ge(consts, 7)

            def bc(a):
                return a.unsqueeze(2).to_broadcast([P, TT, E])

            dve.wait_ge(logits, TT)
            lps = ps[:, 4, 0:TT * E].rearrange("p (t e) -> p t e", e=E)
            link(V.tensor_reduce(col[:, 0, :], lps, AX, ALU.max))
            V.tensor_tensor(lg, lps, bc(col[:, 0, :]), ALU.subtract).then_inc(shift_ready, 1)
            dve.wait_ge(exp_ready, 1)
            link(V.tensor_reduce(col[:, 1, :], pr, AX, ALU.add))
            link(V.reciprocal(col[:, 1, :], col[:, 1, :]))
            link(V.tensor_tensor(pr, pr, bc(col[:, 1, :]), ALU.mult))
            link(V.memset(hot, 0.0))
            for k in range(TOPK):
                link(V.tensor_reduce(col[:, 2 + k, :], pr, AX, ALU.max))
                link(V.tensor_tensor(cand, pr, bc(col[:, 2 + k, :]), ALU.is_equal))
                link(V.tensor_tensor(cand, cand, rev[:].unsqueeze(1).to_broadcast([P, TT, E]), ALU.mult))
                link(V.tensor_reduce(col[:, 4, :], cand, AX, ALU.max))
                link(V.tensor_tensor(hot[:, k, 0:TT, :], cand, bc(col[:, 4, :]), ALU.is_equal))
                if k == 0:
                    link(V.scalar_tensor_tensor(out=pr, in0=hot[:, 0, 0:TT, :], scalar=-2.0, in1=pr,
                                                op0=ALU.mult, op1=ALU.add))
            V.tensor_tensor(both, hot[:, 0], hot[:, 1], ALU.add).then_inc(hot_ready, 1)
            link(V.tensor_tensor(col[:, 4, :], col[:, 2, :], col[:, 3, :], ALU.add))
            link(V.reciprocal(col[:, 4, :], col[:, 4, :]))
            for k in range(TOPK):
                link(V.tensor_tensor(wcol[:, k, :], col[:, 2 + k, :], col[:, 4, :], ALU.mult))
            dve.wait_ge(ranks, 1)
            total = ps[:, 5, TT * E:(TT + 1) * E]
            link(V.memset(cnt[:], 0.0))
            link(V.tensor_scalar(cnt_i[:, 0, :], total, float(P - 1), None, ALU.add))
            link(V.tensor_scalar(cnt_i[:, 1, :], cnt_i[:, 0, :], 7, None, ALU.arith_shift_right))
            link(V.tensor_copy(cnt[:, 0, :], cnt_i[:, 1, :]))
            link(V.tensor_tensor_scan(cnt[:, 1, :], cnt[:, 0, :], cnt[:, 3, :], 0.0, ALU.add, ALU.add))
            link(V.tensor_tensor(cnt[:, 2, :], cnt[:, 1, :], cnt[:, 0, :], ALU.subtract))
            link(V.tensor_scalar(cnt[:, 2, :], cnt[:, 2, :], float(P), None, ALU.mult))
            link(V.tensor_tensor(lg, ps[:, 5, 0:TT * E].rearrange("p (t e) -> p t e", e=E),
                                 cnt[:, 2, :].unsqueeze(1).to_broadcast([P, TT, E]), ALU.add))
            for k in range(TOPK):
                link(V.tensor_tensor(cand, lg, hot[:, k, 0:TT, :], ALU.mult))
                link(V.tensor_reduce(pos_f[:, k, :], cand, AX, ALU.add))
            V.tensor_copy(pos[:], pos_f[:]).then_inc(pos_ready, 1)
            link(V.tensor_tensor(tile_cmp, tile_no.unsqueeze(2).to_broadcast([1, TILES, E]), cnt[0:1, 1, :].unsqueeze(1).to_broadcast([1, TILES, E]),
                                 ALU.is_ge))
            link(V.tensor_reduce(tile_e[:, 0, :], tile_cmp, AX, ALU.add))
            link(V.tensor_scalar(tile_e[:, 1, :], tile_e[:, 0, :], float(E - 1), None, ALU.min))
            V.tensor_copy(tile_ei[:], tile_e[:, 1, :]).then_inc(tile_ready, 1)

            for n in range(1, 2 * KC):
                shared_mult(n)

            def copy_x(j, b, first=False):
                dve.wait_ge(x_tr, j + 1)
                if not first:
                    dve.wait_ge(gu_mm, j - 1)
                for k in range(KC):
                    chunk = slice(k * P, (k + 1) * P)
                    last = V.tensor_scalar(xT[:, b, chunk], ps[:, b, chunk], mcol[:, 3, k:k + 1], mcol[:, 2, k:k + 1],
                                           ALU.mult, ALU.add)
                last.then_inc(xT_ready, 1)

            def multiply(j, b, first=False):
                dve.wait_ge(sg_ready, j + 1)
                if not first:
                    dve.wait_ge(act_tr, j - 1)
                V.tensor_tensor(act_sb[:, b, :], sg[:, b, :], ps[:, 2 + b, I:2 * I], ALU.mult)\
                    .then_inc(act_ready, 1)

            dve.wait_ge(rows_out, 16 * TOPK * TT)
            copy_x(0, 0, first=True)
            copy_x(1, 1, first=True)
            multiply(0, 0, first=True)
            copy_x(2, 0)
            multiply(1, 1, first=True)
            with dve.Fori(0, (TILES - 3) // 2) as i:
                for b in range(2):
                    j = i * 2 + (b + 2)
                    copy_x(j + 1, 1 - b)
                    multiply(j, b)
            multiply(TILES - 1, 0)
            for t in range(TT):
                dve.wait_ge(y0_ready, t + 1)
                dve.wait_ge(s_down, t + 1)
                y = y_in[:, t % Y_RING]
                link(V.scalar_tensor_tensor(out=z, in0=y[:, 1, :], scalar=wcol[:, 1, t:t + 1], in1=ps[:, t, :],
                                            op0=ALU.mult, op1=ALU.add))
                link(V.tensor_tensor(z, z, y[:, 0, :], ALU.add))
                link(V.tensor_tensor(z, z, rows[:, 1, :], ALU.mult))
                V.tensor_tensor(x_sb[:, t, :], x_sb[:, t, :], z, ALU.add).then_inc(out_ready, 1)
                dve.wait_ge(out_ready, t + 1)

        @block.tensor
        def _(pe):
            T = nc.tensor

            def mm(o, lhsT, rhs, k, n):
                return T.matmul(o, lhsT, rhs, start=(k == 0), stop=(k == n - 1))

            pe.wait_ge(consts, 5)
            pe.wait_ge(abs_ready, 1)
            for m in range(QK_TILES):
                w = D if m == 0 else (m - 1) * P
                for k in range(KC):
                    mm(ps[:, 0, m:m + 1], absw[:, k, w:w + P], ones[:, 0:1], k, KC)
            for k in range(KC):
                last = mm(ps[:, 1, 0:KV], ones[:], absw[:, k, D + KV:], k, KC)
            last.then_inc(w_sums, 1)
            def mod_cols(j, o):
                for n in range(KC):
                    for k in range(KC):
                        last = mm(o[:, n:n + 1], wmod_ring[:, j % 2, k, n * P:(n + 1) * P], c_si[:, k:k + 1], k, KC)
                last.then_inc(mod_mm, 1)

            pe.wait_ge(c_ready, 2)
            for j in range(2):
                pe.wait_ge(wmod_in[j], 16)
                mod_cols(j, ps[:, 3, KC * j:KC * (j + 1)])
            pe.wait_ge(abs_ready, 2)
            for k in range(KC):
                last = mm(ps[:, 4, :], ones[:], absw_o[:, k, :], k, KC)
            last.then_inc(w_sums, 1)
            for n in range(2 * KC):
                half, k = divmod(n, KC)
                if k == 0:
                    pe.wait_ge(xn_ready, 4 * half + 4)
                if n == 0:
                    pe.wait_ge(scales_ready, 1)
                if n >= 2:
                    pe.wait_ge(hT_ready, n - 1)
                for t in range(4):
                    last = T.transpose(ps[:, n % 2, t * P:(t + 1) * P], xn[:, 4 * half + t, k * P:(k + 1) * P], ident[:])
                last.then_inc(h_t, 1)
            pe.wait_ge(sign_ready, 1)
            for u in range(2 * QK_TILES + 2):
                m, half = divmod(u, 2)
                if u < 2:
                    pe.wait_ge(hT_ready, KC * (half + 1))
                else:
                    pe.wait_ge(qkv_read, u - 1)
                o = ps[:, 2 + u % 2, :]
                if m < QK_TILES:
                    w = D if m == 0 else (m - 1) * P
                    for k in range(KC):
                        last = mm(o, signw[:, k, w:w + P], hT[:, k, half * HALF:(half + 1) * HALF], k, KC)
                else:
                    for t in range(4):
                        for k in range(KC):
                            a = half * HALF + t * P
                            last = mm(o[:, t * KV:(t + 1) * KV], hT[:, k, a:a + P], signw[:, k, D + KV:], k, KC)
                last.then_inc(qkv_mm, 1)
            for j in range(2, 6):
                pe.wait_ge(wmod_in[j % 2], 16 * (j // 2 + 1))
                if j >= 4:
                    pe.wait_ge(mod_read, j - 3)
                if j in MOD_COLS:
                    mod_cols(j, ps[:, 5 + j % 2, 0:KC])
                    continue
                for k in range(KC):
                    last = mm(ps[:, 5 + j % 2, :], c_bc[:, k, :], wmod_ring[:, j % 2, k, :], k, KC)
                last.then_inc(mod_mm, 1)
            pe.wait_ge(mod_read, 4)

            def max_slots(g, par, start, count, first=False):
                for n in range(start, min(start + count, len(PERIOD))):
                    kind, u = PERIOD[n]
                    if first and (kind, u) == ("transpose", 1):
                        continue
                    if not first:
                        pe.wait_ge(max_read, slots_before(g, n) + (1 - MAX_BANKS))
                    elif n >= MAX_BANKS:
                        pe.wait_ge(max_read, slots_before(g, n - MAX_BANKS) + (n != 5))
                    bank = ps[:, 5 + n % MAX_BANKS, :]
                    if kind == "unit":
                        half, v = divmod(u, HALF_UNITS)
                        hd, t, kh = v // TT, half * (TT // 2) + (v // 2) % (TT // 2), v % 2
                        if v == 0:
                            pe.wait_ge(q_in[par][half], q_loads(g, par))
                        T.matmul(bank, q_ring[0:KROWS, par, half, hd, (t % 4) * P:(t % 4 + 1) * P],
                                 keys(g, 0, KROWS, kh * HALF, HALF), start=True, stop=True).then_inc(max_slot, 1)
                    else:
                        pe.wait_ge(max_cols, (g * 2 if u else g * 2 + 1))
                        T.matmul(bank[0:PARTS * 16, 0:P], mcols.rearrange("p a n -> p (a n)"),
                                    identb[:], start=True, stop=True).then_inc(max_slot, 1)

            def keys(g, row, rows_, col, n):
                return k_all[row:rows_, bass.ds(g, 1), col:col + n].rearrange("p a n -> p (a n)")

            def q_loads(g, par):
                per = 16 * len(Q_PARTS_OF)
                return per * (g // 2 + 1) if isinstance(g, int) else (g - par) * (per // 2) + per

            def score(g, par, s, i, first=False):
                half, kt = divmod(s, TT)
                if kt == 0 and i == 0:
                    pe.wait_ge(max_row_in[half], g * 16 + 16)
                if not (first and s == 0):
                    pe.wait_ge(probs_ready, g * 32 + (2 * s + i - 1))
                for j in range(2):
                    last = T.matmul(ps[:, 2 * i + j, :], keys(g, 0, AROWS, kt * P, P),
                                    q_ring[0:AROWS, par, half, 2 * i + j, :],
                                    start=True, stop=True)
                last.then_inc(scores, 1)

            def pv(g, par, s, first=False):
                half, kt = divmod(s, TT)
                pe.wait_ge(probs_ready, g * 32 + (2 * s + 2))
                if s == 0:
                    pe.wait_ge(vg_ready, g + 1)
                if kt == 0 and not (first and half == 0):
                    pe.wait_ge(o_read, g * 2 + half)
                for hd in range(G):
                    last = T.matmul(ps[32 * hd:32 * hd + 32, 4, :], vg[:, par, kt, :],
                                    probs[:, (2 * s + hd // 2) % 4, (hd % 2) * HALF:(hd % 2 + 1) * HALF],
                                    start=(kt == 0), stop=(kt == TT - 1))
                last.then_inc(pv_done, 1)

            def group(g, par, first=False, last=False):
                done = 0

                def slots(count):
                    nonlocal done
                    for _ in range(count):
                        n = LEAD + done
                        done += 1
                        if n < len(PERIOD):
                            max_slots(g, par, n, 1, first=first)
                        elif n - len(PERIOD) < (3 if last else LEAD):
                            n -= len(PERIOD)
                            if not last:
                                max_slots(g + 1, 1 - par, n, 1)
                            elif n == 2:
                                max_slots(g + 1, 1 - par, n, 1)

                for s in range(16):
                    score(g, par, s, 0, first)
                    slots(2)
                    score(g, par, s, 1, first)
                    slots(2)
                    if s > 0:
                        pv(g, par, s - 1, first)
                    elif not first:
                        pv(g - 1, 1 - par, 15)
                    if s % 8 == 3:
                        slots(1)
                slots(len(PERIOD) - done)

            pe.wait_ge(k_ones, 1)
            pe.wait_ge(k_in, 16 * sum(Q_PARTS_OF))
            pe.wait_ge(identb_ready, 1)
            max_slots(0, 0, 0, LEAD, first=True)
            group(0, 0, first=True)
            with pe.Fori(0, 3) as i:
                group(i * 2 + 1, 1)
                group(i * 2 + 2, 0)
            group(NKV - 1, 1, last=True)
            pv(NKV - 1, 1, 15)

            pe.wait_ge(sign_ready, 2)
            for t in range(TT):
                if t % 4 == 0:
                    pe.wait_ge(oT_ready, 2 * NKV - 1 + t // 4)
                if t >= 4:
                    pe.wait_ge(o_mm_read, t - 3)
                for m in range(KC):
                    last = mm(ps[:, t % 4, :], oT[:, m, t * P:(t + 1) * P], signw_o[:, m, :], m, KC)
                last.then_inc(o_mm, 1)
            pe.wait_ge(gate_in, 16)
            pe.wait_ge(sgu_in, 16)

            def h2_transposes(half):
                pe.wait_ge(h2_ready, 4 * half + 4)
                for k in range(KC):
                    n = half * KC + k
                    if n >= 2:
                        pe.wait_ge(h2T_ready, n - 1)
                    for t in range(4):
                        last = T.transpose(ps[:, n % 2, t * P:(t + 1) * P],
                                           h2[:, 4 * half + t, k * P:(k + 1) * P], ident[:])
                    last.then_inc(h2_t, 1)

            def gate_logits(half):
                pe.wait_ge(h2T_ready, KC * (half + 1))
                for t in range(4 * half, 4 * half + 4):
                    for k in range(KC):
                        last = mm(ps[:, 4, t * E:(t + 1) * E], h2T[:, k, t * P:(t + 1) * P], gate_sb[:, k, :], k, KC)
                    last.then_inc(logits, 1)

            def shared_up(n):
                half, i = divmod(n, KC)
                if n >= 2:
                    pe.wait_ge(s_act, n - 1)
                for u in range(2):
                    for k in range(KC):
                        last = mm(ps[:, 4 * (n % 2) + 2 + u, :], sgu_sb[:, k, u * SI + i * P:u * SI + (i + 1) * P],
                                  h2T[:, k, half * HALF:(half + 1) * HALF], k, KC)
                last.then_inc(s_gu, 1)

            pe.wait_ge(o_mm_read, TT)
            h2_transposes(0)
            gate_logits(0)
            shared_up(0)
            h2_transposes(1)
            gate_logits(1)
            shared_up(1)
            pe.wait_ge(hot_ready, 1)
            counts = ps[:, 5, 0:(TT + 1) * E]
            T.matmul(counts, before[:], both.rearrange("p t e -> p (t e)"), start=True, stop=False)
            for t in range(TT):
                n = TT - t
                last = T.matmul(ps[:, 5, (t + 1) * E:(TT + 1) * E], ones[:],
                                both[:, t:t + 1, :].to_broadcast([P, n, E]), start=False, stop=(t == TT - 1))
            last.then_inc(ranks, 1)
            for n in range(2, 2 * KC):
                shared_up(n)
            pe.wait_ge(pos_ready, 1)

            def transpose_x(j, b, first=False):
                pe.wait_ge(xs_in[b], (j - b) * 8 + 16)
                if not first:
                    pe.wait_ge(xT_ready, j - 1)
                for k in range(KC):
                    last = T.transpose(ps[:, b, k * P:(k + 1) * P], xs[:, b, k * P:(k + 1) * P], ident[:])
                last.then_inc(x_tr, 1)

            def expert_of(j):
                return pe.value_load(tile_ei[0:1, bass.ds(j, 1)], min_val=0, max_val=E - 1)

            def gate_up(j, b, e, first=False):
                pe.wait_ge(xT_ready, j + 1)
                if not first:
                    pe.wait_ge(act_ready, j - 1)
                w = wgu_sb[:, bass.ds(e, 1), :].rearrange("p a n -> p (a n)")
                for k in range(KC):
                    last = mm(ps[:, 2 + b, 0:2 * I], xT[:, b, k * P:(k + 1) * P], w[:, k * 2 * I:(k + 1) * 2 * I], k, KC)
                last.then_inc(gu_mm, 1)

            def transpose_act(j, b, first=False):
                pe.wait_ge(act_ready, j + 1)
                if not first:
                    pe.wait_ge(actT_ready, j - 1)
                T.transpose(ps[:, 4 + b, 0:P], act_sb[:, b, :], ident[:]).then_inc(act_tr, 1)

            def down(j, b, e, first=False):
                pe.wait_ge(actT_ready, j + 1)
                if not first:
                    pe.wait_ge(y_ready, j - 1)
                T.matmul(ps[:, 6 + b, :], actT[:, b, :], wd_sb[:, bass.ds(e, 1), :].rearrange("p a n -> p (a n)"),
                         start=True, stop=True).then_inc(dn_mm, 1)

            pe.wait_ge(tile_ready, 1)
            pe.wait_ge(wgu_in, 16 * E // 2)
            pe.wait_ge(wd_in, 16)
            transpose_x(0, 0, first=True)
            transpose_x(1, 1, first=True)
            gate_up(0, 0, expert_of(0), first=True)
            transpose_act(0, 0, first=True)
            transpose_x(2, 0)
            gate_up(1, 1, expert_of(1), first=True)
            down(0, 0, expert_of(0), first=True)
            transpose_act(1, 1, first=True)
            transpose_x(3, 1)
            gate_up(2, 0, expert_of(2))
            down(1, 1, expert_of(1), first=True)
            with pe.Fori(0, (TILES - 5) // 2) as i:
                for b in range(2):
                    j = i * 2 + (b + 2)
                    e = expert_of(j)
                    e_next = expert_of(j + 1)
                    transpose_act(j, b)
                    transpose_x(j + 2, b)
                    gate_up(j + 1, 1 - b, e_next)
                    down(j, b, e)
            j = TILES - 3
            transpose_act(j, 0)
            transpose_x(j + 2, 0)
            gate_up(j + 1, 1, expert_of(j + 1))
            down(j, 0, expert_of(j))
            transpose_act(j + 1, 1)
            gate_up(j + 2, 0, expert_of(j + 2))
            down(j + 1, 1, expert_of(j + 1))
            transpose_act(j + 2, 0)
            down(j + 2, 0, expert_of(j + 2))
            pe.wait_ge(sd_in, 16)
            pe.wait_ge(s_act, 2 * KC)
            pe.wait_ge(xT_ready, TILES)
            pe.wait_ge(act_ready, TILES)
            pe.wait_ge(actT_ready, TILES)
            pe.wait_ge(y_ready, TILES)
            for t in range(TT):
                for i in range(KC):
                    last = mm(ps[:, t, :], asT[:, i, t * P:(t + 1) * P], sd_sb[:, i, :], i, KC)
                last.then_inc(s_down, 1)


def kernel(**inputs):
    import numpy as np
    import concourse.bacc as bacc
    from concourse.bass_utils import run_bass_kernel_spmd

    a = {k.removeprefix("L0_"): np.asarray(v) for k, v in inputs.items()}

    def chunks(w_t):
        return w_t.reshape(-1, P, w_t.shape[-1]).transpose(1, 0, 2)

    def columns(v):
        return v.reshape(-1, P).T

    def by_group(v):
        return v.reshape(NKV, G, DH, -1).transpose(0, 2, 1, 3).reshape(v.shape)

    arrays = {
        "x": a["attn_hidden_states"].reshape(S, D),
        "wqkv": chunks(np.concatenate([by_group(a["attn_q_weight"]), a["attn_k_weight"], a["attn_v_weight"]]).T),
        "wo": chunks(a["attn_o_weight"].T),
        "qk_scale": columns(np.concatenate([a["attn_k_scale"], by_group(a["attn_q_scale"])])),
        "v_scale": a["attn_v_scale"],
        "o_scale": a["attn_o_scale"],
        "gate": chunks(a["ffn_gate_w"].T),
        "wgu": a["ffn_w_gate_up"].reshape(E, 2 * I, KC, P).transpose(3, 0, 2, 1).reshape(P, E, KC * 2 * I),
        "wd": a["ffn_w_down"].transpose(2, 0, 1),
        "sgu": chunks(a["ffn_shared_w_gate_up"].T),
        "sd": chunks(a["ffn_shared_w_down"].T),
        "c": columns(a["c"][0]),
        "wmod": a["wmod"],
    }
    arrays = {f"in_{k}": np.ascontiguousarray(v) for k, v in arrays.items()}
    nc = bacc.Bacc("TRN2", target_bir_lowering=False, num_devices=1)
    args = [nc.dram_tensor(k, v.shape, mybir.dt.from_np(v.dtype), kind="ExternalInput").ap() for k, v in arrays.items()]
    out = nc.dram_tensor("out", (S, D), mybir.dt.float32, kind="ExternalOutput").ap()
    build(nc, *args, out)
    r = run_bass_kernel_spmd(nc, [arrays], core_ids=[0])
    return r.results[0]["out"].reshape(1, S, D)
```

```python
import concourse.bass as bass
from concourse import mybir
from contextlib import ExitStack

P = 128
S = 1024
D = 512
KC = D // P
TT = S // P
HALF = 512
NH, NKV, DH = 32, 8, 16
G = NH // NKV
KV = NKV * DH
QK_TILES = (D + KV) // P
PARTS = 3
Q_PARTS_OF = (3, 2, 1)
KROWS = sum(Q_PARTS_OF) * DH
AROWS = KROWS + PARTS
E, I, TOPK = 16, 128, 2
SI = 512
TILES = (TOPK * S - E) // P + E
PARTS_OUT = 32 * QK_TILES
LN_EPS = 1e-5
MAX_BANKS = 3
HALF_UNITS = G * (TT // 2) * 2
PERIOD = ([("unit", n) for n in (0, 1)] + [("transpose", 1)] + [("unit", n) for n in range(2, HALF_UNITS + 2)]
          + [("transpose", 0)] + [("unit", n) for n in range(HALF_UNITS + 2, 2 * HALF_UNITS)])
LEAD = 46
FIRST_UNITS = 7
SHARES = 7
assert len(PERIOD) % MAX_BANKS == 0
BIG = 1e6
MOD_COLS = {0: 0, 1: 1, 3: 2, 4: 3}
MOD_ROWS = {2: 0, 5: 1}
LATE = E - TT * D // (KC * 2 * I)
UNROLL = 6
SHARED_BANKS = (4, 5, 3, 1, 2, 0, 7, 6)
POOL_TILES = 4



def build(nc, x, wqkv, wo, qk_scale, v_scale, o_scale, gate, wgu, wd, sgu, sd, c, wmod, out):
    f32, bf16, i32 = mybir.dt.float32, mybir.dt.bfloat16, mybir.dt.int32
    ALU, ACT, AX = mybir.AluOpType, mybir.ActivationFunctionType, mybir.AxisListType.X
    x_t = x.rearrange("(t p) n -> p t n", p=P)
    out_t = out.rearrange("(t p) n -> p t n", p=P)
    wmod_k = wmod.rearrange("(k p) n -> p k n", p=P)

    ctx = ExitStack()
    with ctx:
        def sb(name, shape, dt=f32):
            return ctx.enter_context(nc.sbuf_tensor(name, shape, dt))

        def sem(name):
            return ctx.enter_context(nc.semaphore(name))

        q_parts_d = nc.dram_tensor("q_parts_d", [NKV, PARTS, DH, G, S], bf16).ap()
        k_parts_d = nc.dram_tensor("k_parts_d", [PARTS, KV, S], bf16).ap()
        o_d = nc.dram_tensor("o_d", [NKV, 2, G, 2 * DH, HALF], f32).ap()
        inv_d = nc.dram_tensor("inv_d", [NKV, 2, G, HALF], f32).ap()
        rows_d = nc.dram_tensor("rows_d", [TILES * P, D], f32).ap()
        moe_d = nc.dram_tensor("moe_d", [TILES * P, D], f32).ap()

        wgu_sb = sb("wgu_sb", [P, E, KC * 2 * I])
        r1 = sb("r1", [P, 12288])
        r2 = sb("r2", [P, TT * D])
        r3 = sb("r3", [P, TT * D])
        rx = sb("rx", [P, TT * D])
        sgu_sb = sb("sgu_sb", [P, KC, 2 * SI])
        r5 = sb("r5", [P, KC * D])
        tmp = sb("tmp", [P, 3, D])
        rows = sb("rows", [P, 3, D])
        c_bc = sb("c_bc", [P, KC, P])
        ident = sb("ident", [P, P])
        identb = sb("identb", [P, P], bf16)
        before = sb("before", [P, P])
        ones = sb("ones", [P, P])
        x_sb = rx[:].rearrange("p (t n) -> p t n", n=D)
        wgu_flat = wgu_sb[:].rearrange("p e n -> p (e n)")
        wmod_sb = wgu_flat[:, 4096:16384].rearrange("p (k n) -> p k n", k=KC)
        signw = sgu_sb[:].rearrange("p k n -> p (k n)")[:, 0:3072].rearrange("p (k n) -> p k n", k=KC)
        absw = r1[:, 0:3072].rearrange("p (k n) -> p k n", k=KC)
        absw_o = r1[:, 10240:12288].rearrange("p (k n) -> p k n", k=KC)
        v_sb = r1[:, 10240:12288].rearrange("p (t h n) -> p t h n", t=TT, h=NKV)
        zq = r1[:, 8704:9728].rearrange("p (b n) -> p b n", b=2)
        parts_st = wgu_flat[:, 1024:2560].bitcast(bf16).rearrange("p (b a n) -> p b a n", b=2, a=PARTS)
        mod_row = wgu_flat[0:1, 2560:3584].rearrange("p (b n) -> p b n", b=2)
        sum_row = r1[0:1, 8704:8704 + D + KV]
        o_mean = wgu_flat[:, 512:1024]
        sign_row = r1[:, 9728:10240]
        signw_o = r5[:].rearrange("p (k n) -> p k n", k=KC)
        xn = r2[:].rearrange("p (t n) -> p t n", n=D)
        hT = r3[:].rearrange("p (k n) -> p k n", k=KC)
        q_ring = r1[:, 0:4096].bitcast(bf16).rearrange("p (b f h n) -> p b f h n", b=2, f=2, h=G)
        k_all = r1[:, 4096:8192].bitcast(bf16).rearrange("p (h n) -> p h n", h=NKV)
        ov = r1[:, 8192:9216].rearrange("p (b n) -> p b n", b=2)
        vg = r1[:, 9216:9728].rearrange("p (b t n) -> p b t n", b=2, t=TT)
        probs = rx[:].rearrange("p (b n) -> p b n", b=4)
        oT = r2[:].rearrange("p (m n) -> p m n", m=KC)
        inv = r3[:].rearrange("p (m n) -> p m n", m=KC)
        x_res = wgu_flat[:, LATE * KC * 2 * I:].rearrange("p (t n) -> p t n", n=D)
        wd_sb = r1[:, 0:8192].rearrange("p (e n) -> p e n", e=E)
        h2T = r1[:, 8192:12288].rearrange("p (k n) -> p k n", k=KC)
        h2 = r3[:].rearrange("p (t n) -> p t n", n=D)
        sd_sb = r5[:].rearrange("p (k n) -> p k n", k=KC)
        asT = r2[:].rearrange("p (k n) -> p k n", k=KC)
        xs = r3[:, 0:1024].rearrange("p (b n) -> p b n", b=2)
        xT = r3[:, 1024:2048].rearrange("p (b n) -> p b n", b=2)
        sg = r3[:, 2048:2304].rearrange("p (b n) -> p b n", b=2)
        act_sb = r3[:, 2304:2560].rearrange("p (b n) -> p b n", b=2)
        actT = r3[:, 2560:2816].rearrange("p (b n) -> p b n", b=2)
        y_sb = r3[:, 2816:3840].rearrange("p (b n) -> p b n", b=2)
        y_in = wgu_flat[:, 0:TT * TOPK * D].rearrange("p (b k n) -> p b k n", b=TT, k=TOPK)

        scol = sb("scol", [P, QK_TILES])
        qk_sc = sb("qk_sc", [P, QK_TILES])
        v_sc = sb("v_sc", [P, KV])
        c_sb = sb("c_sb", [P, KC])
        c_si = sb("c_si", [P, KC])
        mcol = sb("mcol", [P, 4, KC])
        stats = sb("stats", [P, TT, 6])
        mv = sb("mv", [P, TT, 2])
        rstd = sb("rstd", [P, TT])
        shift = sb("shift", [P, TT])
        gate_sb = sb("gate_sb", [P, KC, E])
        mxh = sb("mxh", [P, 2, HALF_UNITS])
        rt = sb("rt", [P, 448])
        mxc = rt[:, 0:16]
        mrest = rt[:, 16:48].rearrange("p (a n) -> p a n", a=2)
        mcols = rt[:, 48:72].bitcast(bf16).rearrange("p (a n) -> p a n", a=PARTS)
        mparts = rt[0:PARTS * 16, 72:200].bitcast(bf16).rearrange("p (b n) -> p b n", b=2)
        sums = rt[:, 200:232].rearrange("p (b n) -> p b n", b=2)
        c_flat = c_bc[:].rearrange("p k n -> p (k n)")
        lg = c_flat[:, 0:128].rearrange("p (t e) -> p t e", e=E)
        pr = c_flat[:, 128:256].rearrange("p (t e) -> p t e", e=E)
        both = c_flat[:, 256:400].rearrange("p (t e) -> p t e", e=E)
        cand = rt[:, 0:128].rearrange("p (t e) -> p t e", e=E)
        hot = rt[:, 128:416].rearrange("p (k t e) -> p k t e", k=TOPK, e=E)
        col = sb("col", [P, 6, TT])
        wcol = sb("wcol", [P, TOPK, TT])
        rev = sb("rev", [P, E])
        pos_f = sb("pos_f", [P, TOPK, TT])
        pos = sb("pos", [P, TOPK, TT], i32)
        cnt_i = c_flat[:, 400:432].bitcast(i32).rearrange("p (a e) -> p a e", e=E)
        cnt = sb("cnt", [P, 4, E])
        tile_no = rt[0:1, 416:416 + TILES]
        tile_cmp = tmp[0:1, 2, 0:TILES * E].rearrange("p (j e) -> p j e", e=E)
        tile_e = mxh[0:1, :, 0:TILES]
        tile_ei = sb("tile_ei", [1, TILES], i32)

        ps = ctx.enter_context(nc.psum_tensor("ps", [P, 8, HALF], f32))

        w_in, wo_in, small_in, c_in = (sem(n) for n in ("w_in", "wo_in", "small_in", "c_in"))
        x_in = [sem(f"x_in{n}") for n in range(TT // 2)]
        wmod_in = [sem("wmod_in0"), sem("wmod_in1")]
        row_out, cols_mm, o_scaled = sem("row_out"), sem("cols_mm"), sem("o_scaled")
        mcol_ready, pool_chain = sem("mcol_ready"), sem("pool_chain")
        consts, abs_ready, sign_ready, c_ready = (sem(n) for n in ("consts", "abs_ready", "sign_ready", "c_ready"))
        scales_ready, w_sums, mod_mm, mod_read = sem("scales_ready"), sem("w_sums"), sem("mod_mm"), sem("mod_read")
        var_ready, std_ready, xn_ready, norm_ready = (
            sem(n) for n in ("var_ready", "std_ready", "xn_ready", "norm_ready"))
        h_t, hT_ready, qkv_mm, qkv_read = sem("h_t"), sem("hT_ready"), sem("qkv_mm"), sem("qkv_read")
        parts_ready, v_ready, v_ones = sem("parts_ready"), sem("v_ready"), sem("v_ones")
        parts_out = [sem("parts_out0"), sem("parts_out1")]
        k_in = sem("k_in")
        q_in = [[sem(f"q_in{b}{h}") for h in range(2)] for b in range(2)]
        max_row_in = [sem("max_row_in0"), sem("max_row_in1")]
        k_ones, identb_ready = sem("k_ones"), sem("identb_ready")
        max_slot, max_read = sem("max_slot"), sem("max_read")
        max_cols, max_parts = sem("max_cols"), sem("max_parts")
        scores, probs_ready, pv_done = sem("scores"), sem("probs_ready"), sem("pv_done")
        o_read, vg_ready = sem("o_read"), sem("vg_ready")
        o_out = [sem("o_out0"), sem("o_out1")]
        o_in = [[sem(f"o_in{b}{h}") for h in range(2)] for b in range(2)]
        sums_in = [sem("sums_in0"), sem("sums_in1")]
        inv_out = [sem("inv_out0"), sem("inv_out1")]
        inv_ready = sem("inv_ready")
        wgu_in, sgu_in, wd_in, sd_in = sem("wgu_in"), sem("sgu_in"), sem("wd_in"), sem("sd_in")
        gate_in, zero_ready, zero_out = sem("gate_in"), sem("zero_ready"), sem("zero_out")
        x2_in = sem("x2_in")
        oT_ready, o_mm, o_mm_read, z_ready = sem("oT_ready"), sem("o_mm"), sem("o_mm_read"), sem("z_ready")
        z_scaled, x_added = sem("z_scaled"), sem("x_added")
        h2_ready, h2_t, h2T_ready, logits = sem("h2_ready"), sem("h2_t"), sem("h2T_ready"), sem("logits")
        shift_ready, exp_ready, hot_ready, ranks = sem("shift_ready"), sem("exp_ready"), sem("hot_ready"), sem("ranks")
        pos_ready, rows_out, tile_ready = sem("pos_ready"), sem("rows_out"), sem("tile_ready")
        s_gu, s_silu, s_act, s_down = (sem(n) for n in ("s_gu", "s_silu", "s_act", "s_down"))
        xs_in = [sem("xs_in0"), sem("xs_in1")]
        x_tr, xT_ready, gu_mm, sg_ready = sem("x_tr"), sem("xT_ready"), sem("gu_mm"), sem("sg_ready")
        act_ready, act_tr, actT_ready = sem("act_ready"), sem("act_tr"), sem("actT_ready")
        dn_mm, y_ready = sem("dn_mm"), sem("y_ready")
        y_out = [sem("y_out0"), sem("y_out1")]
        got_y = [sem(f"got_y{n}") for n in range(TT)]
        y0_ready, moe_ready, pool_out_ready = sem("y0_ready"), sem("moe_ready"), sem("pool_out_ready")
        out_ready, out_done = sem("out_ready"), sem("out_done")
        dve_chain, max_chain = sem("dve_chain"), sem("max_chain")

        block = ctx.enter_context(nc.Block())

        def slots_before(g, n):
            if isinstance(g, int) and g == 0:
                return n - (n > 2)
            return g * len(PERIOD) + (n - 1)

        @block.sync
        def _(sp):
            sp.dma_start(c_sb[:], c).then_inc(c_in, 16)

            def load_x(h):
                for t in range(4 * h, 4 * h + 4, 2):
                    sp.dma_start(x_sb[:, t:t + 2, :], x_t[:, t:t + 2, :]).then_inc(x_in[t // 2], 16)

            load_x(0)
            sp.dma_start(wmod_sb[:, :, 0:2 * D], wmod_k[:, :, 0:2 * D]).then_inc(wmod_in[0], 16)
            load_x(1)
            sp.dma_start(signw, wqkv).then_inc(w_in, 16)
            sp.dma_start(qk_sc[:], qk_scale).then_inc(small_in, 16)
            sp.dma_start(v_sc[:], v_scale.partition_broadcast(P)).then_inc(small_in, 16)
            sp.dma_start(rows[:, 2, :], o_scale.partition_broadcast(P)).then_inc(small_in, 16)
            sp.dma_start(signw_o, wo).then_inc(wo_in, 16)
            sp.dma_start(wmod_sb[:, :, 2 * D:], wmod_k[:, :, 2 * D:]).then_inc(wmod_in[1], 16)
            sp.dma_start(gate_sb[:], gate).then_inc(gate_in, 16)

            def load_q(g, par, half):
                cols = slice(half * HALF, (half + 1) * HALF)
                row = 0
                for n in Q_PARTS_OF:
                    sp.dma_start(q_ring[row:row + n * DH, par, half],
                                 q_parts_d[bass.ds(g, 1), 0:n, :, :, cols].rearrange("g a d h n -> (g a d) h n"))\
                        .then_inc(q_in[par][half], 16)
                    row += n * DH

            def load_max(g, par, half):
                sp.wait_ge(max_parts, g * 2 + half + 1)
                sp.dma_start(q_ring[KROWS:AROWS, par, half].rearrange("p h n -> p (h n)"), mparts[:, half, :])\
                    .then_inc(max_row_in[half], 16)

            def store_o(g, half):
                sp.wait_ge(o_read, g * 2 + half + 1)
                sp.dma_start(o_d[bass.ds(g, 1), half].rearrange("g h r n -> (g h r) n"), ov[:, half, :])\
                    .then_inc(o_out[half], 16)

            def chunk_of(g, par):
                return g // 2 if isinstance(g, int) else (g - par) // 2

            def load_o(g, par, half):
                sp.wait_ge(o_out[half], g * 16 + 16)
                rows64 = slice(par * G * DH, (par + 1) * G * DH)
                sp.dma_start(oT[rows64, bass.ds(chunk_of(g, par), 1), half * HALF:(half + 1) * HALF]
                             .rearrange("p a n -> p (a n)"),
                             o_d[bass.ds(g, 1), half, :, 0:DH, :].rearrange("g h d n -> (g h) d n"))\
                    .then_inc(o_in[par][half], 16)
                sp.dma_start(sums[:, half, :],
                             o_d[bass.ds(g, 1), half, :, DH, :].rearrange("g h (c n) -> (g h) c n", n=DH))\
                    .then_inc(sums_in[half], 16)

            def load_inv(g, par, half):
                sp.wait_ge(inv_ready, g * 2 + half + 1)
                sp.dma_start(inv_d[bass.ds(g, 1), half].rearrange("g h (c n) -> (g h c) n", n=DH), sums[:, half, :])\
                    .then_inc(inv_out[half], 16)
                sp.wait_ge(mod_mm, 6)
                sp.wait_ge(inv_out[half], g * 16 + 16)
                rows64 = slice(par * G * DH, (par + 1) * G * DH)
                sp.dma_start(inv[rows64, bass.ds(chunk_of(g, par), 1), half * HALF:(half + 1) * HALF]
                             .rearrange("p a n -> p (a n)"),
                             inv_d[bass.ds(g, 1), half].rearrange("g h n -> (g h) n").unsqueeze(1)
                             .to_broadcast([G, DH, HALF])).then_inc(o_in[par][half], 16)

            for n in range(2 * QK_TILES):
                m, half = divmod(n, 2)
                cols = slice(half * HALF, (half + 1) * HALF)
                sp.wait_ge(parts_ready, n + 1)
                for b in range(2):
                    r = slice(b * G * DH, (b + 1) * G * DH)
                    dst = (k_parts_d[:, r, cols].rearrange("a p n -> p a n") if m == 0 else
                           q_parts_d[2 * (m - 1) + b, :, :, :, cols].rearrange("a d h n -> (d h) a n"))
                    sp.dma_start(dst, parts_st[r, n % 2]).then_inc(parts_out[n % 2], 16)
                if n == 1:
                    sp.wait_ge(parts_out[0], 32)
                    sp.wait_ge(parts_out[1], 32)
                    row = 0
                    for part, copies in enumerate(Q_PARTS_OF):
                        for _ in range(copies):
                            sp.dma_start(k_all[row:row + DH], k_parts_d[part].rearrange("(h d) n -> d h n", d=DH))\
                                .then_inc(k_in, 16)
                            row += DH
                if n == 3:
                    sp.wait_ge(w_sums, 1)
                    for b in range(2):
                        sp.wait_ge(parts_out[b], 64)
                        load_q(0, 0, b)
            for b in range(2):
                sp.wait_ge(parts_out[b], PARTS_OUT)
            load_max(0, 0, 0)
            for half in range(2):
                load_q(1, 1, half)

            def group(g, par, first=False, last=False, loads=True):
                if not first:
                    store_o(g - 1, 1)
                    load_o(g - 1, 1 - par, 1)
                load_max(g, par, 1)
                if not first:
                    load_inv(g - 1, 1 - par, 1)
                if loads:
                    sp.wait_ge(scores, g * 32 + 16)
                    load_q(g + 2, par, 0)
                store_o(g, 0)
                load_o(g, par, 0)
                if not last:
                    load_max(g + 1, 1 - par, 0)
                load_inv(g, par, 0)
                if loads:
                    sp.wait_ge(scores, g * 32 + 32)
                    load_q(g + 2, par, 1)

            group(0, 0, first=True)
            with sp.Fori(0, 2) as i:
                group(i * 2 + 1, 1)
                group(i * 2 + 2, 0)
            group(5, 1)
            sp.wait_ge(mod_mm, 6)
            sp.dma_start(x_res, x_t).then_inc(x2_in, 16)
            group(6, 0, loads=False)
            group(7, 1, last=True, loads=False)
            store_o(7, 1)
            load_o(7, 1, 1)
            load_inv(7, 1, 1)

            sp.wait_ge(pv_done, NKV * 16)
            sp.dma_start(wd_sb, wd).then_inc(wd_in, 16)
            sp.wait_ge(o_mm, TT)
            sp.dma_start(sd_sb, sd).then_inc(sd_in, 16)

            sp.wait_ge(rows_out, 16 * TOPK * TT)

            def load_rows(j, b):
                sp.dma_start(xs[:, b, :], rows_d[bass.ds(j * P, P), :]).then_inc(xs_in[b], 16)

            load_rows(0, 0)
            load_rows(1, 1)
            with sp.Fori(0, (TILES - 3) // 2) as i:
                for b in range(2):
                    sp.wait_ge(x_tr, i * 2 + b + 1)
                    load_rows(i * 2 + b + 2, b)
            j = TILES - 3
            sp.wait_ge(x_tr, j + 1)
            load_rows(j + 2, 0)
            for t in range(TT):
                if t < TT - POOL_TILES:
                    sp.wait_ge(out_ready, t + 1)
                else:
                    sp.wait_ge(pool_out_ready, t - (TT - POOL_TILES) + 1)
                sp.dma_start(out_t[:, t, :], x_sb[:, t, :]).then_inc(out_done, 16)
            sp.wait_ge(out_done, 16 * TT)

        @block.gpsimd
        def _(pool):
            nc.gpsimd.memset(ident[:], 0.0).then_inc(consts, 1)
            nc.gpsimd.memset(before[:], 1.0).then_inc(consts, 1)
            nc.gpsimd.memset(ones[:], 1.0).then_inc(consts, 1)
            pool.wait_ge(consts, 3)
            nc.gpsimd.memset(k_all[KROWS:AROWS, :, :], 1.0).then_inc(k_ones, 1)
            pool.wait_ge(k_ones, 1)
            nc.gpsimd.affine_select(out=ident[:], in_=ident[:], compare_op=ALU.not_equal, fill=1.0, base=0,
                                    pattern=[[-1, P]], channel_multiplier=1).then_inc(consts, 1)
            nc.gpsimd.affine_select(out=before[:], in_=before[:], compare_op=ALU.is_gt, fill=0.0, base=0,
                                    pattern=[[1, P]], channel_multiplier=-1).then_inc(consts, 1)
            nc.gpsimd.iota(rev[:], pattern=[[-1, E]], base=E, channel_multiplier=0,
                           allow_small_or_imprecise_dtypes=True).then_inc(consts, 1)
            nc.gpsimd.iota(tile_no, pattern=[[1, TILES]], base=0, channel_multiplier=0,
                           allow_small_or_imprecise_dtypes=True).then_inc(consts, 1)
            pool.wait_ge(consts, 7)
            nc.gpsimd.tensor_copy(identb[:], ident[:]).then_inc(identb_ready, 1)
            pool.wait_ge(w_sums, 2)
            pool.wait_ge(identb_ready, 1)
            nc.gpsimd.memset(v_sb[:, :, :, DH:2 * DH], 1.0).then_inc(v_ones, 1)
            linked = [0]

            def link(ins):
                linked[0] += 1
                ins.then_inc(pool_chain, 1)
                pool.wait_ge(pool_chain, linked[0])

            def keep_from_zero(row):
                link(nc.gpsimd.tensor_scalar(sign_row, row, 0.0, 2.0, ALU.is_ge, ALU.mult))
                link(nc.gpsimd.tensor_scalar(sign_row, sign_row, 1.0, None, ALU.subtract))
                link(nc.gpsimd.tensor_tensor(row, row, sign_row, ALU.mult))
                link(nc.gpsimd.tensor_scalar(row, row, 0.25, None, ALU.max))
                link(nc.gpsimd.tensor_tensor(row, row, sign_row, ALU.mult))

            pool.wait_ge(v_ones, 1)
            pool.wait_ge(o_scaled, 1)
            pool.wait_ge(small_in, 48)
            link(nc.gpsimd.tensor_scalar(o_mean, o_mean, 1e-8, None, ALU.max))
            link(nc.gpsimd.tensor_tensor(rows[:, 2, :], rows[:, 2, :], o_mean, ALU.mult))
            pool.wait_ge(mod_read, 1)
            keep_from_zero(rows[:, 0, :])
            pool.wait_ge(mod_mm, 6)
            nc.gpsimd.memset(c_bc[:], 0.0).then_inc(zero_ready, 1)
            pool.wait_ge(mod_read, 2)
            pool.wait_ge(zero_ready, 1)
            keep_from_zero(rows[:, 1, :])
            pool.wait_ge(qkv_mm, 2 * QK_TILES + 2)
            for b in range(2):
                pool.wait_ge(parts_out[b], PARTS_OUT)
            pool.wait_ge(mcol_ready, 1)
            pool.wait_ge(v_ready, 2)

            def group_v(g, par, expert, count):
                nc.gpsimd.tensor_copy(vg[:, par], v_sb[:, :, bass.ds(g, 1), :].rearrange("p t a n -> p t (a n)"))\
                    .then_inc(vg_ready, 1)
                pool.dma_start(wgu_sb[:, bass.ds(expert, count), :], wgu[:, bass.ds(expert, count), :])\
                    .then_inc(wgu_in, 16)

            def divide(g, par):
                m = g // 2 if isinstance(g, int) else (g - par) // 2
                rows64 = slice(par * G * DH, (par + 1) * G * DH)
                for half in range(2):
                    if half == 0:
                        pool.wait_ge(vg_ready, min(g + 2, NKV) if isinstance(g, int) else g + 2)
                    else:
                        pool.wait_ge(oT_ready, g * 2 + 1)
                    pool.wait_ge(o_in[par][half], g // 2 * 32 + 32 if isinstance(g, int) else (g - par) * 16 + 32)
                    o = oT[rows64, bass.ds(m, 1), half * HALF:(half + 1) * HALF].rearrange("p a n -> p (a n)")
                    nc.gpsimd.tensor_tensor(o, o, inv[rows64, bass.ds(m, 1), half * HALF:(half + 1) * HALF]
                                            .rearrange("p a n -> p (a n)"), ALU.mult).then_inc(oT_ready, 1)

            def zero_rows(first, count):
                pool.dma_start(rows_d[bass.ds(first * P, count * P), :].rearrange("(t p) n -> p t n", p=P),
                               c_bc[:].rearrange("p k n -> p (k n)").unsqueeze(1).to_broadcast([P, count, D]))\
                    .then_inc(zero_out, 16)

            group_v(0, 0, 0, 2)
            group_v(1, 1, 2, 2)
            per = TILES // (KC - 1)
            zero_rows(per * (KC - 1), TILES - per * (KC - 1))
            with pool.Fori(0, KC - 1) as i:
                zero_rows(i * per, per)
                for par in range(2):
                    divide(i * 2 + par, par)
                    pool.wait_ge(pv_done, i * 32 + (par + 1) * 16)
                    pool.wait_ge(oT_ready, i * 4 + (2 * par + 2))
                    group_v(i * 2 + (par + 2), par, i * 2 + (par + 4), 1)
            pool.dma_start(wgu_sb[:, NKV + 2:LATE, :], wgu[:, NKV + 2:LATE, :]).then_inc(wgu_in, 16)
            pool.dma_start(sgu_sb[:], sgu).then_inc(sgu_in, 16)
            divide(NKV - 2, 0)
            pool.wait_ge(oT_ready, 2 * NKV - 2)
            divide(NKV - 1, 1)
            for t in range(TT):
                pool.wait_ge(z_ready, t + 1)
                if t == 0:
                    pool.wait_ge(oT_ready, 2 * NKV)
                    pool.wait_ge(x2_in, 16)
                    pool.wait_ge(pv_done, NKV * 16)
                else:
                    pool.wait_ge(x_added, t)
                nc.gpsimd.tensor_tensor(h2[:, t, :], h2[:, t, :], rows[:, 0, :], ALU.mult).then_inc(z_scaled, 1)
                pool.wait_ge(z_scaled, t + 1)
                nc.gpsimd.tensor_tensor(x_sb[:, t, :], x_res[:, t, :], h2[:, t, :], ALU.add).then_inc(x_added, 1)
            pool.wait_ge(x_added, TT)
            pool.dma_start(wgu_sb[:, LATE:E, :], wgu[:, LATE:E, :]).then_inc(wgu_in, 16)
            pool.wait_ge(pos_ready, 1)
            pool.wait_ge(zero_out, 16 * KC)
            pool.wait_ge(h2_ready, TT)
            for t in range(TT):
                for k in range(TOPK):
                    nc.gpsimd.indirect_dma_start(
                        out=rows_d, out_offset=bass.IndirectOffsetOnAxis(ap=pos[:, k, t:t + 1], axis=0),
                        in_=h2[:, t, :], in_offset=None).then_inc(rows_out, 16)
            pool.wait_ge(y_out[0], 16 * ((TILES + 1) // 2))
            pool.wait_ge(y_out[1], 16 * (TILES // 2))
            pool.wait_ge(dn_mm, TILES)
            for t in range(TT):
                for k in range(TOPK):
                    nc.gpsimd.indirect_dma_start(
                        out=y_in[:, t, k, :], out_offset=None, in_=moe_d,
                        in_offset=bass.IndirectOffsetOnAxis(ap=pos[:, k, t:t + 1], axis=0)).then_inc(got_y[t], 16)
            for t in range(TT - POOL_TILES, TT):
                pool.wait_ge(moe_ready, t - (TT - POOL_TILES) + 1)
                if t > TT - POOL_TILES:
                    pool.wait_ge(pool_out_ready, t - (TT - POOL_TILES))
                nc.gpsimd.tensor_tensor(x_sb[:, t, :], x_sb[:, t, :], y_in[:, t, 1, :], ALU.add)\
                    .then_inc(pool_out_ready, 1)

        @block.scalar
        def _(act):
            act.wait_ge(c_in, 16)
            nc.scalar.activation(c_si[:], c_sb[:], ACT.Silu).then_inc(c_ready, 1)
            act.wait_ge(c_ready, 1)
            nc.scalar.activation(c_bc[:], c_si[:].unsqueeze(2).to_broadcast([P, KC, P]), ACT.Copy)\
                .then_inc(c_ready, 1)

            def copy_row(dst, src):
                nc.scalar.activation(dst, src, ACT.Copy).then_inc(row_out, 1)

            for h in range(2):
                act.wait_ge(var_ready, h + 1)
                nc.scalar.activation(rstd[:, 4 * h:4 * h + 4], rstd[:, 4 * h:4 * h + 4], ACT.Sqrt)\
                    .then_inc(std_ready, 1)
                if h == 0:
                    for j in range(2):
                        act.wait_ge(mod_mm, j + 1)
                        copy_row(mod_row[:, j, :], ps[0:1, 2 + j, :])
                    act.wait_ge(w_in, 16)
                    nc.scalar.activation(absw, signw, ACT.Abs).then_inc(abs_ready, 1)
                    act.wait_ge(abs_ready, 1)
                    nc.scalar.activation(signw, signw, ACT.Sign).then_inc(sign_ready, 1)
            act.wait_ge(w_sums, 1)
            copy_row(sum_row[:, 0:D], ps[0:1, 0, :])
            copy_row(sum_row[:, D:], ps[0:1, 3, 0:KV])
            act.wait_ge(wo_in, 16)
            nc.scalar.activation(absw_o, signw_o, ACT.Abs).then_inc(abs_ready, 1)
            act.wait_ge(abs_ready, 2)
            nc.scalar.activation(signw_o, signw_o, ACT.Sign).then_inc(sign_ready, 1)

            for n in range(2 * QK_TILES):
                act.wait_ge(qkv_mm, n + 1)
                if n == 0:
                    act.wait_ge(scales_ready, 1)
                if n >= 2:
                    act.wait_ge(parts_ready, n - 1)
                nc.scalar.activation(zq[:, n % 2, :], ps[:, 2 + n % 2, :], ACT.Copy,
                                     scale=scol[:, n // 2:n // 2 + 1]).then_inc(qkv_read, 1)
                if n == FIRST_UNITS:
                    act.wait_ge(w_sums, 2)
                    nc.scalar.activation(o_mean, ps[:, 4, :], ACT.Copy, scale=1.0 / D).then_inc(o_scaled, 1)
                    act.wait_ge(mod_mm, 3)
                    nc.scalar.activation(rows[:, 0, :], ps[:, 0, :], ACT.Copy).then_inc(mod_read, 1)
                if n in (FIRST_UNITS, FIRST_UNITS + 1):
                    j = n - FIRST_UNITS + 3
                    act.wait_ge(mod_mm, j + 1)
                    copy_row(mod_row[:, j % 2, :], ps[0:1, 1 if j == 3 else 4, :])

            act.wait_ge(mod_mm, 6)
            nc.scalar.activation(rows[:, 1, :], ps[:, 0, :], ACT.Copy).then_inc(mod_read, 1)

            def read_o(g, half):
                act.wait_ge(pv_done, g * 16 + 8 * half + 8)
                if not (isinstance(g, int) and g == 0):
                    act.wait_ge(o_out[half], g * 16)
                nc.scalar.activation(ov[:, half, :], ps[:, 4, :], ACT.Copy).then_inc(o_read, 1)

            def group(g, first=False):
                for s in range(16):
                    for i in range(2):
                        act.wait_ge(scores, g * 32 + (2 * s + i + 1))
                        if i == 0 and not (first and s < 2):
                            act.wait_ge(pv_done, g * 16 + (s - 1))
                        nc.scalar.activation(probs[:, (2 * s + i) % 4, :],
                                             ps[:, 2 * i:2 * i + 2, :].rearrange("p b n -> p (b n)"),
                                             ACT.Exp, scale=DH ** -0.5).then_inc(probs_ready, 1)
                    if s == 0 and not first:
                        read_o(g - 1, 1)
                    if s == 8:
                        read_o(g, 0)

            group(0, first=True)
            with act.Fori(0, NKV - 1) as i:
                group(i + 1)
            read_o(NKV - 1, 1)
            def deviation(t):
                act.wait_ge(var_ready, 3 + t)
                nc.scalar.activation(rstd[:, t:t + 1], rstd[:, t:t + 1], ACT.Sqrt).then_inc(std_ready, 1)

            def normalise(t):
                act.wait_ge(norm_ready, t + 1)
                nc.scalar.activation(h2[:, t, :], x_sb[:, t, :], ACT.Identity, bias=shift[:, t:t + 1],
                                     scale=rstd[:, t:t + 1]).then_inc(h2_ready, 1)

            def modulate(half, chunks):
                for k in chunks:
                    n = half * KC + k
                    act.wait_ge(h2_t, n + 1)
                    nc.scalar.activation(h2T[:, k, half * HALF:(half + 1) * HALF], ps[:, 4 + n % 2, :], ACT.Identity,
                                         bias=mcol[:, 2, k:k + 1], scale=mcol[:, 3, k:k + 1]).then_inc(h2T_ready, 1)

            def shared_silu(n):
                act.wait_ge(s_gu, n + 1)
                if n >= 2:
                    act.wait_ge(s_act, n - 1)
                nc.scalar.activation(tmp[:, n % 2, :], ps[:, 6 * (1 - n % 2), :], ACT.Silu).then_inc(s_silu, 1)

            for t in range(TT):
                deviation(t)
                normalise(t)
                if t in (TT // 2 - 1, TT // 2):
                    modulate(0, (0, 1) if t < TT // 2 else (2, 3))
            shared_silu(0)
            modulate(1, range(KC))
            act.wait_ge(shift_ready, 1)
            nc.scalar.activation(pr, lg, ACT.Exp).then_inc(exp_ready, 1)
            for n in range(1, 2 * KC):
                shared_silu(n)

            def silu(j, b, first=False):
                act.wait_ge(gu_mm, j + 1)
                if not first:
                    act.wait_ge(act_ready, j - 1)
                nc.scalar.activation(sg[:, b, :], ps[:, 2 + b, 0:I], ACT.Silu).then_inc(sg_ready, 1)

            def copy_act(j, b, first=False):
                act.wait_ge(act_tr, j + 1)
                if not first:
                    act.wait_ge(dn_mm, j - 1)
                nc.scalar.activation(actT[:, b, :], ps[:, b, 0:P], ACT.Copy).then_inc(actT_ready, 1)

            def copy_y(j, b, first=False):
                act.wait_ge(dn_mm, j + 1)
                if not first:
                    act.wait_ge(y_out[b], (j - b) * 8)
                nc.scalar.activation(y_sb[:, b, :], ps[:, 6 + b, :], ACT.Copy).then_inc(y_ready, 1)
                act.wait_ge(y_ready, j + 1)
                act.dma_start(moe_d[bass.ds(j * P, P), :], y_sb[:, b, :]).then_inc(y_out[b], 16)

            silu(0, 0, first=True)
            copy_act(0, 0, first=True)
            silu(1, 1, first=True)
            copy_y(0, 0, first=True)
            copy_act(1, 1, first=True)
            silu(2, 0)
            copy_y(1, 1, first=True)
            with act.Fori(0, (TILES - 3) // 2) as i:
                for b in range(2):
                    j = i * 2 + (b + 2)
                    copy_act(j, b)
                    silu(j + 1, 1 - b)
                    copy_y(j, b)
            j = TILES - 1
            copy_act(j, 0)
            copy_y(j, 0)
            for t in range(TT):
                act.wait_ge(got_y[t], 32)
                y0 = y_in[:, t, 0, :]
                nc.scalar.activation(y0, y0, ACT.Copy, scale=wcol[:, 0, t:t + 1]).then_inc(y0_ready, 1)

        @block.vector
        def _(dve):
            linked = [0]

            def link(ins):
                linked[0] += 1
                ins.then_inc(dve_chain, 1)
                dve.wait_ge(dve_chain, linked[0])

            V = nc.vector

            def nan_to_num(v, a, mask):
                V.tensor_scalar(mask, v, 0.0, 0.0, ALU.mult, ALU.not_equal)
                link(V.tensor_scalar(a, v, BIG, -BIG, ALU.min, ALU.max))
                link(V.scalar_tensor_tensor(out=a, in0=v, scalar=0.0, in1=a, op0=ALU.max, op1=ALU.min))
                link(V.copy_predicated(v, mask, a))

            z, za, zm = tmp[:, 0, :], tmp[:, 1, :], tmp[:, 2, :].bitcast(i32)

            def norm_stats(t):
                link(V.bn_stats(stats[:, t, :], x_sb[:, t, :]))
                link(V.bn_aggr(mv[:, t, :], stats[:, t, :]))

            for h in range(2):
                for t in range(4 * h, 4 * h + 4):
                    dve.wait_ge(x_in[t // 2], 16)
                    norm_stats(t)
                V.tensor_scalar(rstd[:, 4 * h:4 * h + 4], mv[:, 4 * h:4 * h + 4, 1], LN_EPS, None, ALU.add)\
                    .then_inc(var_ready, 1)
                dve.wait_ge(std_ready, h + 1)
                link(V.reciprocal(rstd[:, 4 * h:4 * h + 4], rstd[:, 4 * h:4 * h + 4]))
                for t in range(4 * h, 4 * h + 4):
                    V.tensor_scalar(xn[:, t, :], x_sb[:, t, :], mv[:, t, 0:1], rstd[:, t:t + 1],
                                    ALU.subtract, ALU.mult).then_inc(xn_ready, 1)
            dve.wait_ge(cols_mm, 2)
            link(V.tensor_copy(mcol[:, 0, :], ps[:, 1, 0:KC]))
            link(V.tensor_scalar(mcol[:, 1, :], ps[:, 1, KC:2 * KC], 1.0, None, ALU.add))
            for n in range(2 * KC):
                h, k = divmod(n, KC)
                dve.wait_ge(h_t, n + 1)
                V.tensor_scalar(hT[:, k, h * HALF:(h + 1) * HALF], ps[:, 4 + n % 4, :],
                                mcol[:, 1, k:k + 1], mcol[:, 0, k:k + 1], ALU.mult, ALU.add).then_inc(hT_ready, 1)
            dve.wait_ge(cols_mm, 3)
            dve.wait_ge(small_in, 48)
            link(V.tensor_scalar(scol[:], ps[:, 1, 0:QK_TILES], 1.0 / D, 1e-8, ALU.mult, ALU.max))
            link(V.tensor_scalar(za[:, 0:KV], ps[:, 3, KV:2 * KV], 1.0 / D, 1e-8, ALU.mult, ALU.max))
            link(V.tensor_tensor(v_sc[:], za[:, 0:KV], v_sc[:], ALU.mult))
            V.tensor_tensor(scol[:], scol[:], qk_sc[:], ALU.mult).then_inc(scales_ready, 1)

            def split_unit(n):
                v = zq[:, n % 2, :]
                dve.wait_ge(qkv_read, n + 1)
                nan_to_num(v, za, zm)
                if n >= 2:
                    dve.wait_ge(parts_out[n % 2], 32 * (n // 2))
                st = parts_st[:, n % 2]
                link(V.tensor_copy(st[:, 0, :], v))
                link(V.tensor_tensor(v, v, st[:, 0, :], ALU.subtract))
                link(V.tensor_copy(st[:, 1, :], v))
                V.tensor_tensor(st[:, 2, :], v, st[:, 1, :], ALU.subtract).then_inc(parts_ready, 1)
                dve.wait_ge(parts_ready, n + 1)

            def scale_v(half):
                u = 2 * QK_TILES + half
                dve.wait_ge(qkv_mm, u + 1)
                if half == 0:
                    dve.wait_ge(v_ones, 1)
                link(V.tensor_tensor(z.rearrange("p (t n) -> p t n", n=KV),
                                     ps[:, 2 + u % 2, :].rearrange("p (t n) -> p t n", n=KV),
                                     v_sc[:].unsqueeze(1).to_broadcast([P, 4, KV]), ALU.mult))
                nan_to_num(z, za, zm)
                V.tensor_copy(v_sb[:, 4 * half:4 * half + 4, :, 0:DH],
                              z.rearrange("p (t h n) -> p t h n", t=4, h=NKV)).then_inc(v_ready, 1)
                dve.wait_ge(v_ready, half + 1)

            def mod_columns():
                dve.wait_ge(cols_mm, 5)
                link(V.tensor_copy(mcol[:, 2, :], ps[:, 1, 0:KC]))
                V.tensor_scalar(mcol[:, 3, :], ps[:, 1, KC:2 * KC], 1.0, None, ALU.add).then_inc(mcol_ready, 1)
                dve.wait_ge(mcol_ready, 1)

            def period(g, first=False, divisors=(1, 0), wait_sent=True, start=0, stop=len(PERIOD)):
                for n in range(start, stop):
                    kind, u = PERIOD[n]
                    if first and (kind, u) == ("transpose", 1):
                        continue
                    dve.wait_ge(max_slot, slots_before(g, n) + 1)
                    bank = ps[:, 5 + n % MAX_BANKS, :]
                    if kind == "unit":
                        half, u = divmod(u, HALF_UNITS)
                        V.reduce_max(mxh[:, half, u:u + 1], bank, AX).then_inc(max_read, 1)
                        if u == HALF_UNITS - 1:
                            dve.wait_ge(max_read, slots_before(g, n) + 1)
                            split_max(g, half)
                    else:
                        read_parts(g - 1 if u else g, u, bank, wait_sent)
                    if n == 4 and 1 in divisors:
                        reciprocals(g - 2, 1)
                    if n == 37 and 0 in divisors:
                        reciprocals(g - 1, 0)

            def split_max(g, half):
                def step(k, ins):
                    ins.then_inc(max_chain, 1)
                    dve.wait_ge(max_chain, g * 8 + (4 * half + k))

                if half or not isinstance(g, int) or g > 0:
                    dve.wait_ge(max_parts, g * 2 + half)
                pairs = mxh[:, half, :].rearrange("p (n k) -> p n k", k=2)
                step(1, V.tensor_tensor(mxc, pairs[:, :, 0], pairs[:, :, 1], ALU.max))
                step(2, V.tensor_scalar(mcols[:, 0, :], mxc, -1.0, None, ALU.mult))
                step(3, V.scalar_tensor_tensor(out=mrest[:, 0, :], in0=mxc, scalar=-1.0, in1=mcols[:, 0, :],
                                               op0=ALU.mult, op1=ALU.subtract))
                step(4, V.tensor_copy(mcols[:, 1, :], mrest[:, 0, :]))
                V.tensor_tensor(mcols[:, 2, :], mrest[:, 0, :], mcols[:, 1, :], ALU.subtract).then_inc(max_cols, 1)

            def read_parts(g, half, bank, wait_sent):
                if wait_sent:
                    dve.wait_ge(max_row_in[half], g * 16)
                V.tensor_copy(mparts[:, half, :], bank[0:PARTS * 16, 0:P]).then_inc(max_parts, 1)
                dve.wait_ge(max_parts, g * 2 + half + 1)
                V.sem_inc(max_read, 1)

            def reciprocals(g, half):
                dve.wait_ge(sums_in[half], g * 16 + 16)
                V.reciprocal(sums[:, half, :], sums[:, half, :]).then_inc(inv_ready, 1)

            for n in range(FIRST_UNITS):
                split_unit(n)
            def share(n):
                period(0, first=True, divisors=(), wait_sent=False, start=LEAD * n // SHARES,
                       stop=LEAD * (n + 1) // SHARES)

            share(0)
            split_unit(FIRST_UNITS)
            share(1)
            share(2)
            split_unit(FIRST_UNITS + 1)
            share(3)
            split_unit(FIRST_UNITS + 2)
            share(4)
            scale_v(0)
            share(5)
            scale_v(1)
            share(6)
            mod_columns()
            period(0, first=True, divisors=(), wait_sent=False, start=LEAD)
            period(1, divisors=(0,), wait_sent=False)
            with dve.Fori(2, NKV) as g:
                period(g)
            dve.wait_ge(max_slot, slots_before(NKV, 0) + 1)
            read_parts(NKV - 1, 1, ps[:, 5 + 2, :], True)
            reciprocals(NKV - 2, 1)
            reciprocals(NKV - 1, 0)
            reciprocals(NKV - 1, 1)

            def later(ins):
                linked[0] += 1
                ins.then_inc(dve_chain, 1)
                return linked[0]

            def norm_and_scale(t, u):
                if t == 0:
                    dve.wait_ge(oT_ready, 2 * NKV - 1)
                if t == TT // 2:
                    dve.wait_ge(oT_ready, 2 * NKV)
                if t is not None:
                    v = h2[:, t, :]
                    dve.wait_ge(o_mm, t + 1)
                    V.tensor_tensor(v, ps[:, t % 3, :], rows[:, 2, :], ALU.mult).then_inc(o_mm_read, 1)
                if u is not None:
                    dve.wait_ge(x_added, u + 1)
                    stats_done = later(V.bn_stats(stats[:, u, :], x_sb[:, u, :]))
                if t is not None:
                    dve.wait_ge(o_mm_read, t + 1)
                    if t > 0:
                        dve.wait_ge(z_ready, t)
                    V.tensor_scalar(zm, v, 0.0, 0.0, ALU.mult, ALU.not_equal)
                    clamped = later(V.tensor_scalar(za, v, BIG, -BIG, ALU.min, ALU.max))
                if u is not None:
                    dve.wait_ge(dve_chain, stats_done)
                    mean_done = later(V.bn_aggr(mv[:, u, :], stats[:, u, :]))
                if t is not None:
                    dve.wait_ge(dve_chain, clamped)
                    replaced = later(V.scalar_tensor_tensor(out=za, in0=v, scalar=0.0, in1=za, op0=ALU.max,
                                                            op1=ALU.min))
                if u is not None:
                    dve.wait_ge(dve_chain, mean_done)
                    V.tensor_scalar(rstd[:, u:u + 1], mv[:, u, 1:2], LN_EPS, None, ALU.add).then_inc(var_ready, 1)
                if t is not None:
                    dve.wait_ge(dve_chain, replaced)
                    V.copy_predicated(v, zm, za).then_inc(z_ready, 1)
                if u is not None:
                    dve.wait_ge(std_ready, 3 + u)
                    link(V.reciprocal(rstd[:, u:u + 1], rstd[:, u:u + 1]))
                    V.scalar_tensor_tensor(out=shift[:, u:u + 1], in0=mv[:, u, 0:1], scalar=-1.0,
                                           in1=rstd[:, u:u + 1], op0=ALU.mult, op1=ALU.mult).then_inc(norm_ready, 1)

            for t in range(TT):
                norm_and_scale(t, t - 2 if t >= 2 else None)
            for u in (TT - 2, TT - 1):
                norm_and_scale(None, u)

            def shared_mult(n):
                half, i = divmod(n, KC)
                dve.wait_ge(s_silu, n + 1)
                V.tensor_tensor(asT[:, i, half * HALF:(half + 1) * HALF], tmp[:, n % 2, :],
                                ps[:, 6 * (1 - n % 2) + 1, :], ALU.mult).then_inc(s_act, 1)

            shared_mult(0)
            dve.wait_ge(consts, 7)

            def bc(a):
                return a.unsqueeze(2).to_broadcast([P, TT, E])

            dve.wait_ge(logits, TT)
            dve.wait_ge(zero_out, 16 * KC)
            lps = ps[:, 3, 0:TT * E].rearrange("p (t e) -> p t e", e=E)
            link(V.tensor_reduce(col[:, 0, :], lps, AX, ALU.max))
            V.tensor_tensor(lg, lps, bc(col[:, 0, :]), ALU.subtract).then_inc(shift_ready, 1)
            dve.wait_ge(exp_ready, 1)
            link(V.tensor_reduce(col[:, 1, :], pr, AX, ALU.add))
            link(V.reciprocal(col[:, 1, :], col[:, 1, :]))
            link(V.tensor_tensor(pr, pr, bc(col[:, 1, :]), ALU.mult))
            link(V.memset(hot, 0.0))
            for k in range(TOPK):
                link(V.tensor_reduce(col[:, 2 + k, :], pr, AX, ALU.max))
                link(V.tensor_tensor(cand, pr, bc(col[:, 2 + k, :]), ALU.is_equal))
                link(V.tensor_tensor(cand, cand, rev[:].unsqueeze(1).to_broadcast([P, TT, E]), ALU.mult))
                link(V.tensor_reduce(col[:, 4, :], cand, AX, ALU.max))
                link(V.tensor_tensor(hot[:, k, 0:TT, :], cand, bc(col[:, 4, :]), ALU.is_equal))
                if k == 0:
                    link(V.scalar_tensor_tensor(out=pr, in0=hot[:, 0, 0:TT, :], scalar=-2.0, in1=pr,
                                                op0=ALU.mult, op1=ALU.add))
            V.tensor_tensor(both, hot[:, 0], hot[:, 1], ALU.add).then_inc(hot_ready, 1)
            link(V.tensor_tensor(col[:, 4, :], col[:, 2, :], col[:, 3, :], ALU.add))
            link(V.reciprocal(col[:, 4, :], col[:, 4, :]))
            for k in range(TOPK):
                link(V.tensor_tensor(wcol[:, k, :], col[:, 2 + k, :], col[:, 4, :], ALU.mult))
            dve.wait_ge(ranks, 1)
            total = ps[:, 2, TT * E:(TT + 1) * E]
            link(V.memset(cnt[:], 0.0))
            link(V.tensor_scalar(cnt_i[:, 0, :], total, float(P - 1), None, ALU.add))
            link(V.tensor_scalar(cnt_i[:, 1, :], cnt_i[:, 0, :], 7, None, ALU.arith_shift_right))
            link(V.tensor_copy(cnt[:, 0, :], cnt_i[:, 1, :]))
            link(V.tensor_tensor_scan(cnt[:, 1, :], cnt[:, 0, :], cnt[:, 3, :], 0.0, ALU.add, ALU.add))
            link(V.tensor_tensor(cnt[:, 2, :], cnt[:, 1, :], cnt[:, 0, :], ALU.subtract))
            link(V.tensor_scalar(cnt[:, 2, :], cnt[:, 2, :], float(P), None, ALU.mult))
            link(V.tensor_tensor(lg, ps[:, 2, 0:TT * E].rearrange("p (t e) -> p t e", e=E),
                                 cnt[:, 2, :].unsqueeze(1).to_broadcast([P, TT, E]), ALU.add))
            for k in range(TOPK):
                link(V.tensor_tensor(cand, lg, hot[:, k, 0:TT, :], ALU.mult))
                link(V.tensor_reduce(pos_f[:, k, :], cand, AX, ALU.add))
            V.tensor_copy(pos[:], pos_f[:]).then_inc(pos_ready, 1)
            link(V.tensor_tensor(tile_cmp, tile_no.unsqueeze(2).to_broadcast([1, TILES, E]),
                                 cnt[0:1, 1, :].unsqueeze(1).to_broadcast([1, TILES, E]),
                                 ALU.is_ge))
            link(V.tensor_reduce(tile_e[:, 0, :], tile_cmp, AX, ALU.add))
            link(V.tensor_scalar(tile_e[:, 1, :], tile_e[:, 0, :], float(E - 1), None, ALU.min))
            V.tensor_copy(tile_ei[:], tile_e[:, 1, :]).then_inc(tile_ready, 1)

            for n in range(1, 2 * KC - 1):
                shared_mult(n)

            def copy_x(j, b, first=False):
                dve.wait_ge(x_tr, j + 1)
                if not first:
                    dve.wait_ge(gu_mm, j - 1)
                for k in range(KC):
                    chunk = slice(k * P, (k + 1) * P)
                    last = V.tensor_scalar(xT[:, b, chunk], ps[:, 4 + b, chunk],
                                           mcol[:, 3, k:k + 1], mcol[:, 2, k:k + 1], ALU.mult, ALU.add)
                last.then_inc(xT_ready, 1)

            def multiply(j, b, first=False):
                dve.wait_ge(sg_ready, j + 1)
                if not first:
                    dve.wait_ge(act_tr, j - 1)
                V.tensor_tensor(act_sb[:, b, :], sg[:, b, :], ps[:, 2 + b, I:2 * I], ALU.mult)\
                    .then_inc(act_ready, 1)

            dve.wait_ge(rows_out, 16 * TOPK * TT)
            copy_x(0, 0, first=True)
            copy_x(1, 1, first=True)
            shared_mult(2 * KC - 1)
            multiply(0, 0, first=True)
            copy_x(2, 0)
            multiply(1, 1, first=True)
            with dve.Fori(0, (TILES - 3) // 2) as i:
                for b in range(2):
                    j = i * 2 + (b + 2)
                    copy_x(j + 1, 1 - b)
                    multiply(j, b)
            multiply(TILES - 1, 0)
            for a in range(0, TT, 2):
                done = [0, 0]
                for n, t in enumerate((a, a + 1)):
                    dve.wait_ge(y0_ready, t + 1)
                    dve.wait_ge(s_down, t + 1)
                    y = y_in[:, t]
                    done[n] = later(V.scalar_tensor_tensor(out=y[:, 1, :], in0=y[:, 1, :],
                                                           scalar=wcol[:, 1, t:t + 1], in1=ps[:, SHARED_BANKS[t], :],
                                                           op0=ALU.mult, op1=ALU.add))
                for n, t in enumerate((a, a + 1)):
                    dve.wait_ge(dve_chain, done[n])
                    done[n] = later(V.tensor_tensor(y_in[:, t, 1, :], y_in[:, t, 1, :], y_in[:, t, 0, :], ALU.add))
                for n, t in enumerate((a, a + 1)):
                    dve.wait_ge(dve_chain, done[n])
                    ins = V.tensor_tensor(y_in[:, t, 1, :], y_in[:, t, 1, :], rows[:, 1, :], ALU.mult)
                    if t >= TT - POOL_TILES:
                        ins.then_inc(moe_ready, 1)
                    else:
                        done[n] = later(ins)
                for n, t in enumerate((a, a + 1)):
                    if t < TT - POOL_TILES:
                        dve.wait_ge(dve_chain, done[n])
                        V.tensor_tensor(x_sb[:, t, :], x_sb[:, t, :], y_in[:, t, 1, :], ALU.add)\
                            .then_inc(out_ready, 1)

        @block.tensor
        def _(pe):
            T = nc.tensor

            def mm(o, lhsT, rhs, k, n):
                return T.matmul(o, lhsT, rhs, start=(k == 0), stop=(k == n - 1))

            def mod_as_row(j, o, lhsT):
                for k in range(KC):
                    last = mm(o, lhsT(k), wmod_sb[:, k, j * D:(j + 1) * D], k, KC)
                last.then_inc(mod_mm, 1)

            def column_of_c(k):
                return c_si[:, k:k + 1]

            def to_columns(o, row, first, count):
                for n in range(count):
                    last = T.transpose(o[:, n:n + 1], row[:, first + n * P:first + (n + 1) * P], ident[0:1, 0:1])
                return last

            pe.wait_ge(consts, 7)

            def transpose_xn(half):
                pe.wait_ge(xn_ready, 4 * half + 4)
                for k in range(KC):
                    n = half * KC + k
                    if n >= 4:
                        pe.wait_ge(hT_ready, n - 3)
                    for t in range(4):
                        last = T.transpose(ps[:, 4 + n % 4, t * P:(t + 1) * P],
                                           xn[:, 4 * half + t, k * P:(k + 1) * P], ident[:])
                    last.then_inc(h_t, 1)

            transpose_xn(0)
            pe.wait_ge(c_ready, 1)
            pe.wait_ge(wmod_in[0], 16)
            for j in range(2):
                mod_as_row(j, ps[0:1, 2 + j, :], column_of_c)
            for j in range(2):
                pe.wait_ge(row_out, j + 1)
                to_columns(ps[:, 1, KC * j:KC * (j + 1)], mod_row[:, j, :], 0, KC).then_inc(cols_mm, 1)
            pe.wait_ge(abs_ready, 1)
            for k in range(KC):
                mm(ps[:, 0, :], ones[:], absw[:, k, 0:D], k, KC)
            for k in range(KC):
                last = mm(ps[:, 3, 0:2 * KV], ones[:], absw[:, k, D:], k, KC)
            last.then_inc(w_sums, 1)
            transpose_xn(1)
            pe.wait_ge(row_out, 4)
            to_columns(ps[:, 1, 0:1], sum_row, D, 1)
            to_columns(ps[:, 1, 1:QK_TILES], sum_row, 0, KC).then_inc(cols_mm, 1)

            def unit(u):
                m, half = divmod(u, 2)
                if u < 2:
                    pe.wait_ge(hT_ready, KC * (half + 1))
                else:
                    pe.wait_ge(qkv_read, u - 1)
                if u == 1:
                    pe.wait_ge(scales_ready, 1)
                o = ps[:, 2 + u % 2, :]
                if m < QK_TILES:
                    w = D if m == 0 else (m - 1) * P
                    for k in range(KC):
                        last = mm(o, signw[:, k, w:w + P], hT[:, k, half * HALF:(half + 1) * HALF], k, KC)
                else:
                    for t in range(4):
                        for k in range(KC):
                            a = half * HALF + t * P
                            last = mm(o[:, t * KV:(t + 1) * KV], hT[:, k, a:a + P], signw[:, k, D + KV:], k, KC)
                last.then_inc(qkv_mm, 1)

            def sums_of_o():
                pe.wait_ge(abs_ready, 2)
                pe.wait_ge(scales_ready, 1)
                for k in range(KC):
                    last = mm(ps[:, 4, :], ones[:], absw_o[:, k, :], k, KC)
                last.then_inc(w_sums, 1)

            def gate_row(j):
                pe.wait_ge(c_ready, 2)
                pe.wait_ge(wmod_in[1], 16)
                if j == 5:
                    pe.wait_ge(mod_read, 1)
                mod_as_row(j, ps[:, 0, :], lambda k: c_bc[:, k, :])

            def mod_row_of(j):
                if j == 4:
                    pe.wait_ge(o_scaled, 1)
                mod_as_row(j, ps[0:1, 1 if j == 3 else 4, :], column_of_c)

            def mod_columns(j):
                pe.wait_ge(row_out, j + 2)
                to_columns(ps[:, 1, KC * (j - 3):KC * (j - 2)], mod_row[:, j % 2, :], 0, KC).then_inc(cols_mm, 1)

            pe.wait_ge(sign_ready, 1)
            for u in range(FIRST_UNITS + 1):
                unit(u)
            sums_of_o()
            gate_row(2)
            mod_row_of(3)

            def max_slots(g, par, start, count, first=False):
                for n in range(start, min(start + count, len(PERIOD))):
                    kind, u = PERIOD[n]
                    if first and (kind, u) == ("transpose", 1):
                        continue
                    if not first:
                        pe.wait_ge(max_read, slots_before(g, n) + (1 - MAX_BANKS))
                    elif n >= MAX_BANKS:
                        pe.wait_ge(max_read, slots_before(g, n - MAX_BANKS) + (n != 5))
                    bank = ps[:, 5 + n % MAX_BANKS, :]
                    if kind == "unit":
                        half, v = divmod(u, HALF_UNITS)
                        hd, t, kh = v // TT, half * (TT // 2) + (v // 2) % (TT // 2), v % 2
                        if v == 0:
                            pe.wait_ge(q_in[par][half], q_loads(g, par))
                        T.matmul(bank, q_ring[0:KROWS, par, half, hd, (t % 4) * P:(t % 4 + 1) * P],
                                 keys(g, 0, KROWS, kh * HALF, HALF), start=True, stop=True).then_inc(max_slot, 1)
                    else:
                        pe.wait_ge(max_cols, (g * 2 if u else g * 2 + 1))
                        T.matmul(bank[0:PARTS * 16, 0:P], mcols.rearrange("p a n -> p (a n)"),
                                    identb[:], start=True, stop=True).then_inc(max_slot, 1)

            def keys(g, row, rows_, col, n):
                return k_all[row:rows_, bass.ds(g, 1), col:col + n].rearrange("p a n -> p (a n)")

            def q_loads(g, par):
                per = 16 * len(Q_PARTS_OF)
                return per * (g // 2 + 1) if isinstance(g, int) else (g - par) * (per // 2) + per

            def score(g, par, s, i, first=False):
                half, kt = divmod(s, TT)
                if kt == 0 and i == 0:
                    pe.wait_ge(max_row_in[half], g * 16 + 16)
                if not (first and s == 0):
                    pe.wait_ge(probs_ready, g * 32 + (2 * s + i - 1))
                for j in range(2):
                    last = T.matmul(ps[:, 2 * i + j, :], keys(g, 0, AROWS, kt * P, P),
                                    q_ring[0:AROWS, par, half, 2 * i + j, :],
                                    start=True, stop=True)
                last.then_inc(scores, 1)

            def pv(g, par, s, first=False):
                half, kt = divmod(s, TT)
                pe.wait_ge(probs_ready, g * 32 + (2 * s + 2))
                if s == 0:
                    pe.wait_ge(vg_ready, g + 1)
                if kt == 0 and not (first and half == 0):
                    pe.wait_ge(o_read, g * 2 + half)
                for hd in range(G):
                    last = T.matmul(ps[32 * hd:32 * hd + 32, 4, :], vg[:, par, kt, :],
                                    probs[:, (2 * s + hd // 2) % 4, (hd % 2) * HALF:(hd % 2 + 1) * HALF],
                                    start=(kt == 0), stop=(kt == TT - 1))
                last.then_inc(pv_done, 1)

            def group(g, par, first=False, last=False):
                done = 0

                def slots(count):
                    nonlocal done
                    for _ in range(count):
                        n = LEAD + done
                        done += 1
                        if n < len(PERIOD):
                            max_slots(g, par, n, 1, first=first)
                        elif not last or PERIOD[n - len(PERIOD)] == ("transpose", 1):
                            max_slots(g + 1, 1 - par, n - len(PERIOD), 1)

                for s in range(16):
                    score(g, par, s, 0, first)
                    slots(2)
                    score(g, par, s, 1, first)
                    slots(2)
                    if s > 0:
                        pv(g, par, s - 1, first)
                    elif not first:
                        pv(g - 1, 1 - par, 15)
                    if s % 8 == 3:
                        slots(1)
                slots(len(PERIOD) - done)

            pe.wait_ge(k_ones, 1)
            pe.wait_ge(k_in, 16 * sum(Q_PARTS_OF))
            pe.wait_ge(identb_ready, 1)
            def share(n):
                start = LEAD * n // SHARES
                max_slots(0, 0, start, LEAD * (n + 1) // SHARES - start, first=True)

            share(0)
            unit(FIRST_UNITS + 1)
            share(1)
            mod_row_of(4)
            share(2)
            mod_columns(3)
            mod_columns(4)
            unit(FIRST_UNITS + 2)
            share(3)
            unit(FIRST_UNITS + 3)
            share(4)
            unit(FIRST_UNITS + 4)
            share(5)
            gate_row(5)
            share(6)
            pe.wait_ge(mod_read, 2)
            pe.wait_ge(mcol_ready, 1)
            group(0, 0, first=True)
            with pe.Fori(0, 3) as i:
                group(i * 2 + 1, 1)
                group(i * 2 + 2, 0)
            group(NKV - 1, 1, last=True)
            pv(NKV - 1, 1, 15)

            pe.wait_ge(sign_ready, 2)
            for t in range(TT):
                if t % 4 == 0:
                    pe.wait_ge(oT_ready, 2 * NKV - 1 + t // 4)
                if t >= 3:
                    pe.wait_ge(o_mm_read, t - 2)
                for m in range(KC):
                    last = mm(ps[:, t % 3, :], oT[:, m, t * P:(t + 1) * P], signw_o[:, m, :], m, KC)
                last.then_inc(o_mm, 1)
            pe.wait_ge(gate_in, 16)
            pe.wait_ge(sgu_in, 16)

            def h2_transposes(half):
                pe.wait_ge(h2_ready, 4 * half + 4)
                for k in range(KC):
                    n = half * KC + k
                    if n >= 2:
                        pe.wait_ge(h2T_ready, n - 1)
                    for t in range(4):
                        last = T.transpose(ps[:, 4 + n % 2, t * P:(t + 1) * P],
                                           h2[:, 4 * half + t, k * P:(k + 1) * P], ident[:])
                    last.then_inc(h2_t, 1)

            def gate_logits(half):
                pe.wait_ge(h2T_ready, KC * (half + 1))
                for t in range(4 * half, 4 * half + 4):
                    for k in range(KC):
                        last = mm(ps[:, 3, t * E:(t + 1) * E], h2T[:, k, t * P:(t + 1) * P], gate_sb[:, k, :], k, KC)
                    last.then_inc(logits, 1)

            def shared_up(n):
                half, i = divmod(n, KC)
                pe.wait_ge(h2T_ready, KC * (half + 1))
                if n >= 2:
                    pe.wait_ge(s_act, n - 1)
                for u in range(2):
                    for k in range(KC):
                        last = mm(ps[:, 6 * (1 - n % 2) + u, :], sgu_sb[:, k, u * SI + i * P:u * SI + (i + 1) * P],
                                  h2T[:, k, half * HALF:(half + 1) * HALF], k, KC)
                last.then_inc(s_gu, 1)

            h2_transposes(0)
            shared_up(0)
            gate_logits(0)
            h2_transposes(1)
            gate_logits(1)
            pe.wait_ge(o_mm_read, TT)
            shared_up(1)
            pe.wait_ge(hot_ready, 1)
            counts = ps[:, 2, 0:(TT + 1) * E]
            T.matmul(counts, before[:], both.rearrange("p t e -> p (t e)"), start=True, stop=False)
            for t in range(TT):
                n = TT - t
                last = T.matmul(ps[:, 2, (t + 1) * E:(TT + 1) * E], ones[:],
                                both[:, t:t + 1, :].to_broadcast([P, n, E]), start=False, stop=(t == TT - 1))
            last.then_inc(ranks, 1)
            for n in range(2, 2 * KC - 1):
                shared_up(n)
            pe.wait_ge(pos_ready, 1)

            def transpose_x(j, b, first=False):
                pe.wait_ge(xs_in[b], (j - b) * 8 + 16)
                if not first:
                    pe.wait_ge(xT_ready, j - 1)
                for k in range(KC):
                    last = T.transpose(ps[:, 4 + b, k * P:(k + 1) * P], xs[:, b, k * P:(k + 1) * P], ident[:])
                last.then_inc(x_tr, 1)

            def expert_of(j):
                return pe.value_load(tile_ei[0:1, bass.ds(j, 1)], min_val=0, max_val=E - 1)

            def gate_up(j, b, e, first=False):
                pe.wait_ge(xT_ready, j + 1)
                if not first:
                    pe.wait_ge(act_ready, j - 1)
                w = wgu_sb[:, bass.ds(e, 1), :].rearrange("p a n -> p (a n)")
                for k in range(KC):
                    last = mm(ps[:, 2 + b, 0:2 * I], xT[:, b, k * P:(k + 1) * P],
                              w[:, k * 2 * I:(k + 1) * 2 * I], k, KC)
                last.then_inc(gu_mm, 1)

            def transpose_act(j, b, first=False):
                pe.wait_ge(act_ready, j + 1)
                if not first:
                    pe.wait_ge(actT_ready, j - 1)
                T.transpose(ps[:, b, 0:P], act_sb[:, b, :], ident[:]).then_inc(act_tr, 1)

            def down(j, b, e, first=False):
                pe.wait_ge(actT_ready, j + 1)
                if not first:
                    pe.wait_ge(y_ready, j - 1)
                T.matmul(ps[:, 6 + b, :], actT[:, b, :], wd_sb[:, bass.ds(e, 1), :].rearrange("p a n -> p (a n)"),
                         start=True, stop=True).then_inc(dn_mm, 1)

            pe.wait_ge(tile_ready, 1)
            pe.wait_ge(wgu_in, 16 * (NKV + 2))
            pe.wait_ge(wd_in, 16)
            transpose_x(0, 0, first=True)
            transpose_x(1, 1, first=True)
            shared_up(2 * KC - 1)
            gate_up(0, 0, expert_of(0), first=True)
            transpose_x(2, 0)
            pe.wait_ge(s_act, 2 * KC)
            transpose_act(0, 0, first=True)
            gate_up(1, 1, expert_of(1), first=True)
            down(0, 0, expert_of(0), first=True)
            transpose_act(1, 1, first=True)
            transpose_x(3, 1)
            gate_up(2, 0, expert_of(2))
            down(1, 1, expert_of(1), first=True)

            def expert_step(j, b, e):
                e_next = expert_of(j + 1)
                transpose_act(j, b)
                transpose_x(j + 2, b)
                gate_up(j + 1, 1 - b, e_next)
                down(j, b, e)
                return e_next

            with pe.Fori(0, (TILES - 5) // UNROLL) as i:
                e = expert_of(i * UNROLL + 2)
                for n in range(UNROLL):
                    e = expert_step(i * UNROLL + (n + 2), n % 2, e)
            j = 2 + (TILES - 5) // UNROLL * UNROLL
            e = expert_of(j)
            for j in range(j, TILES - 3):
                e = expert_step(j, j % 2, e)
            j = TILES - 3
            transpose_act(j, 0)
            transpose_x(j + 2, 0)
            gate_up(j + 1, 1, expert_of(j + 1))
            down(j, 0, expert_of(j))
            transpose_act(j + 1, 1)
            gate_up(j + 2, 0, expert_of(j + 2))
            down(j + 1, 1, expert_of(j + 1))

            bank_free = ((xT_ready, TILES), (xT_ready, TILES - 1), (act_ready, TILES - 1), (actT_ready, TILES - 1),
                         (act_ready, TILES), (actT_ready, TILES), (y_ready, TILES - 1), (y_ready, TILES))

            def shared_down(t, chunks=range(KC)):
                if 0 in chunks:
                    pe.wait_ge(*bank_free[t])
                for i in chunks:
                    last = mm(ps[:, SHARED_BANKS[t], :], asT[:, i, t * P:(t + 1) * P], sd_sb[:, i, :], i, KC)
                if KC - 1 in chunks:
                    last.then_inc(s_down, 1)

            pe.wait_ge(sd_in, 16)
            e = expert_of(j + 2)
            shared_down(0, range(0, 2))
            transpose_act(j + 2, 0)
            shared_down(0, range(2, 3))
            down(j + 2, 0, e)
            shared_down(0, range(3, KC))
            for t in range(1, TT):
                shared_down(t)



def kernel(**inputs):
    import numpy as np
    import concourse.bacc as bacc
    from concourse.bass_utils import run_bass_kernel_spmd

    a = {k.removeprefix("L0_"): np.asarray(v) for k, v in inputs.items()}

    def chunks(w_t):
        return w_t.reshape(-1, P, w_t.shape[-1]).transpose(1, 0, 2)

    def columns(v):
        return v.reshape(-1, P).T

    def by_group(v):
        return v.reshape(NKV, G, DH, -1).transpose(0, 2, 1, 3).reshape(v.shape)

    arrays = {
        "x": a["attn_hidden_states"].reshape(S, D),
        "wqkv": chunks(np.concatenate([by_group(a["attn_q_weight"]), a["attn_k_weight"], a["attn_v_weight"]]).T),
        "wo": chunks(a["attn_o_weight"].T),
        "qk_scale": columns(np.concatenate([a["attn_k_scale"], by_group(a["attn_q_scale"])])),
        "v_scale": a["attn_v_scale"],
        "o_scale": a["attn_o_scale"],
        "gate": chunks(a["ffn_gate_w"].T),
        "wgu": a["ffn_w_gate_up"].reshape(E, 2 * I, KC, P).transpose(3, 0, 2, 1).reshape(P, E, KC * 2 * I),
        "wd": a["ffn_w_down"].transpose(2, 0, 1),
        "sgu": chunks(a["ffn_shared_w_gate_up"].T),
        "sd": chunks(a["ffn_shared_w_down"].T),
        "c": columns(a["c"][0]),
        "wmod": a["wmod"],
    }
    arrays = {f"in_{k}": np.ascontiguousarray(v) for k, v in arrays.items()}
    nc = bacc.Bacc("TRN2", target_bir_lowering=False, num_devices=1)
    args = [nc.dram_tensor(k, v.shape, mybir.dt.from_np(v.dtype), kind="ExternalInput").ap() for k, v in arrays.items()]
    out = nc.dram_tensor("out", (S, D), mybir.dt.float32, kind="ExternalOutput").ap()
    build(nc, *args, out)
    r = run_bass_kernel_spmd(nc, [arrays], core_ids=[0])
    return r.results[0]["out"].reshape(1, S, D)
```
